# Optimizing a Trainium2 kernel written in Bass

```python
import numpy as np
import jax
import jax.numpy as jnp

def _softmax(x, axis=-1):
    return jax.nn.softmax(x, axis=axis)

def _gelu(x):
    return jax.nn.gelu(x, approximate=True)

def _silu(x):
    return jax.nn.silu(x)

def _sigmoid(x):
    return jax.nn.sigmoid(x)

def _layernorm(x, axis=-1, eps=1e-05):
    m = jnp.mean(x, axis=axis, keepdims=True)
    v = jnp.var(x, axis=axis, keepdims=True)
    return (x - m) / jnp.sqrt(v + eps)

def _scatter_add(tgt, idx, src, axis=0):
    return tgt.at[idx].add(src)

def _segment_sum(src, seg, n):
    return jax.ops.segment_sum(src, seg, n)
kernel_name = 'mk_seq_postln_d1_jaxref_r4_64ff01'

def setup_inputs(seed: int=0):
    np.random.seed(seed)
    _w = jnp.asarray

    def _L0_attn_setup():
        import jax, jax.numpy as jnp
        from jax import lax
        import numpy as np
        HEAD_SIZE = 64
        D_MIX = 32
        D_DECAY = 64
        D_GATE = 64

        def _wkv6(r, k, v, w, u):
            B, T, C = r.shape
            N = HEAD_SIZE
            H = C // N
            to_h = lambda a: a.reshape(B, T, H, N).transpose(1, 0, 2, 3)
            rT, kT, vT, wT = map(to_h, (r, k, v, w))

            def step(S, inp):
                rt, kt, vt, wt = inp
                kv = kt[..., :, None] * vt[..., None, :]
                y = jnp.einsum('bhi,bhij->bhj', rt, S + u[None, :, :, None] * kv)
                S = wt[..., None] * S + kv
                return (S, y)
            S0 = jnp.zeros((B, H, N, N), r.dtype)
            _, y = lax.scan(step, S0, (rT, kT, vT, wT))
            return y.transpose(1, 0, 2, 3).reshape(B, T, C)
        key = jax.random.key(seed)
        B, T, C = (4, 512, 256)
        H = C // HEAD_SIZE
        ks = jax.random.split(key, 24)
        n = lambda i, shape, s=1.0: jax.random.normal(ks[i], shape, dtype=jnp.float32) * s
        return {'x': n(0, (B, T, C)), 'maa_x': n(1, (C,), 0.1), 'maa_w': n(2, (C,), 0.1), 'maa_k': n(3, (C,), 0.1), 'maa_v': n(4, (C,), 0.1), 'maa_r': n(5, (C,), 0.1), 'maa_g': n(6, (C,), 0.1), 'maa_w1': n(7, (C, 5 * D_MIX), 0.01), 'maa_w2': n(8, (5, D_MIX, C), 0.01), 'Wr': n(9, (C, C), C ** (-0.5)), 'Wk': n(10, (C, C), C ** (-0.5)), 'Wv': n(11, (C, C), C ** (-0.5)), 'Wo': n(12, (C, C), C ** (-0.5)), 'gate_w1': n(13, (C, D_GATE), 0.01), 'gate_w2': n(14, (D_GATE, C), 0.01), 'time_decay': n(15, (C,), 1.0) - 4.0, 'decay_w1': n(16, (C, D_DECAY), 0.01), 'decay_w2': n(17, (D_DECAY, C), 0.01), 'u': n(18, (H, HEAD_SIZE), 0.1), 'ln_g': jnp.ones((C,), jnp.float32), 'ln_b': jnp.zeros((C,), jnp.float32)}
    _L0_attn_in = _L0_attn_setup()

    def _L0_ffn_setup():
        import jax, jax.numpy as jnp
        import numpy as np
        import math
        B, L, D = (4, 1024, 256)
        F = 1024
        E = 16
        CAP_FACTOR = 1.0
        EPS = 1e-05
        key = jax.random.key(seed)
        ks = jax.random.split(key, 8)
        std = 0.02
        return {'x': jax.random.normal(ks[0], (B, L, D), dtype=jnp.float32), 'norm_weight': jnp.ones((D,), dtype=jnp.float32), 'router_weight': jax.random.normal(ks[1], (E, D), dtype=jnp.float32) * std, 'router_bias': jnp.zeros((E,), dtype=jnp.float32), 'fc1_weight': jax.random.normal(ks[2], (E, F, D), dtype=jnp.float32) * std, 'fc1_bias': jnp.zeros((E, F), dtype=jnp.float32), 'fc2_weight': jax.random.normal(ks[3], (E, D, F), dtype=jnp.float32) * std, 'fc2_bias': jnp.zeros((E, D), dtype=jnp.float32)}
    _L0_ffn_in = _L0_ffn_setup()
    _d = {'L0_attn_x': _L0_attn_in['x'], 'L0_attn_maa_x': _L0_attn_in['maa_x'], 'L0_attn_maa_w': _L0_attn_in['maa_w'], 'L0_attn_maa_k': _L0_attn_in['maa_k'], 'L0_attn_maa_v': _L0_attn_in['maa_v'], 'L0_attn_maa_r': _L0_attn_in['maa_r'], 'L0_attn_maa_g': _L0_attn_in['maa_g'], 'L0_attn_maa_w1': _L0_attn_in['maa_w1'], 'L0_attn_maa_w2': _L0_attn_in['maa_w2'], 'L0_attn_Wr': _L0_attn_in['Wr'], 'L0_attn_Wk': _L0_attn_in['Wk'], 'L0_attn_Wv': _L0_attn_in['Wv'], 'L0_attn_Wo': _L0_attn_in['Wo'], 'L0_attn_gate_w1': _L0_attn_in['gate_w1'], 'L0_attn_gate_w2': _L0_attn_in['gate_w2'], 'L0_attn_time_decay': _L0_attn_in['time_decay'], 'L0_attn_decay_w1': _L0_attn_in['decay_w1'], 'L0_attn_decay_w2': _L0_attn_in['decay_w2'], 'L0_attn_u': _L0_attn_in['u'], 'L0_attn_ln_g': _L0_attn_in['ln_g'], 'L0_attn_ln_b': _L0_attn_in['ln_b'], 'L0_ffn_norm_weight': _L0_ffn_in['norm_weight'], 'L0_ffn_router_weight': _L0_ffn_in['router_weight'], 'L0_ffn_router_bias': _L0_ffn_in['router_bias'], 'L0_ffn_fc1_weight': _L0_ffn_in['fc1_weight'], 'L0_ffn_fc1_bias': _L0_ffn_in['fc1_bias'], 'L0_ffn_fc2_weight': _L0_ffn_in['fc2_weight'], 'L0_ffn_fc2_bias': _L0_ffn_in['fc2_bias']}
    _x0 = _d['L0_attn_x']
    _d['L0_attn_x'] = jax.random.normal(jax.random.fold_in(jax.random.key(seed), 1), (16, 512, 256), dtype=_x0.dtype)
    del _x0
    return _d

def reference(L0_attn_x, L0_attn_maa_x, L0_attn_maa_w, L0_attn_maa_k, L0_attn_maa_v, L0_attn_maa_r, L0_attn_maa_g, L0_attn_maa_w1, L0_attn_maa_w2, L0_attn_Wr, L0_attn_Wk, L0_attn_Wv, L0_attn_Wo, L0_attn_gate_w1, L0_attn_gate_w2, L0_attn_time_decay, L0_attn_decay_w1, L0_attn_decay_w2, L0_attn_u, L0_attn_ln_g, L0_attn_ln_b, L0_ffn_norm_weight, L0_ffn_router_weight, L0_ffn_router_bias, L0_ffn_fc1_weight, L0_ffn_fc1_bias, L0_ffn_fc2_weight, L0_ffn_fc2_bias):

    def _L0_attn_ref(x, maa_x, maa_w, maa_k, maa_v, maa_r, maa_g, maa_w1, maa_w2, Wr, Wk, Wv, Wo, gate_w1, gate_w2, time_decay, decay_w1, decay_w2, u, ln_g, ln_b):
        import jax, jax.numpy as jnp
        from jax import lax
        import numpy as np
        HEAD_SIZE = 64
        D_MIX = 32
        D_DECAY = 64
        D_GATE = 64

        def _wkv6(r, k, v, w, u):
            B, T, C = r.shape
            N = HEAD_SIZE
            H = C // N
            to_h = lambda a: a.reshape(B, T, H, N).transpose(1, 0, 2, 3)
            rT, kT, vT, wT = map(to_h, (r, k, v, w))

            def step(S, inp):
                rt, kt, vt, wt = inp
                kv = kt[..., :, None] * vt[..., None, :]
                y = jnp.einsum('bhi,bhij->bhj', rt, S + u[None, :, :, None] * kv)
                S = wt[..., None] * S + kv
                return (S, y)
            S0 = jnp.zeros((B, H, N, N), r.dtype)
            _, y = lax.scan(step, S0, (rT, kT, vT, wT))
            return y.transpose(1, 0, 2, 3).reshape(B, T, C)
        B, T, C = x.shape
        H, N = (C // HEAD_SIZE, HEAD_SIZE)
        xx = jnp.concatenate([jnp.zeros_like(x[:, :1]), x[:, :-1]], axis=1) - x
        xxx = x + xx * maa_x
        lora = jnp.tanh(xxx @ maa_w1).reshape(B, T, 5, D_MIX)
        m = jnp.einsum('btfd,fdc->fbtc', lora, maa_w2)
        mw, mk, mv, mr, mg = (m[0], m[1], m[2], m[3], m[4])
        xw = x + xx * (maa_w + mw)
        xk = x + xx * (maa_k + mk)
        xv = x + xx * (maa_v + mv)
        xr = x + xx * (maa_r + mr)
        xg = x + xx * (maa_g + mg)
        r = xr @ Wr
        k = xk @ Wk
        v = xv @ Wv
        g = jnp.tanh(xg @ gate_w1) @ gate_w2
        w = time_decay + jnp.tanh(xw @ decay_w1) @ decay_w2
        wdec = jnp.exp(-jnp.exp(w))
        y = _wkv6(r, k, v, wdec, u)
        yh = y.reshape(B, T, H, N)
        mu = yh.mean(-1, keepdims=True)
        var = yh.var(-1, keepdims=True)
        yn = ((yh - mu) / jnp.sqrt(var + 0.00064)).reshape(B, T, C) * ln_g + ln_b
        return yn * g @ Wo

    def _L0_ffn_ref(x, norm_weight, router_weight, router_bias, fc1_weight, fc1_bias, fc2_weight, fc2_bias):
        import jax, jax.numpy as jnp
        import numpy as np
        import math
        B, L, D = (4, 1024, 256)
        F = 1024
        E = 16
        CAP_FACTOR = 1.0
        EPS = 1e-05
        b, l, d = x.shape
        n_tokens = b * l
        n_experts = router_weight.shape[0]
        capacity = max(1, math.ceil(CAP_FACTOR * n_tokens / n_experts))
        top_k = min(capacity, n_tokens)
        xf = x.reshape(n_tokens, d)
        rms = jnp.sqrt(jnp.mean(xf * xf, axis=-1, keepdims=True) + EPS)
        xn = xf / rms * norm_weight
        logits = xn @ router_weight.T + router_bias
        probs = jax.nn.softmax(logits, axis=-1)
        _, idx = jax.lax.top_k(logits.T, top_k)
        xe = xn[idx]
        h = jnp.einsum('ecd,efd->ecf', xe, fc1_weight) + fc1_bias[:, None, :]
        h = jax.nn.gelu(h, approximate=False)
        y = jnp.einsum('ecf,edf->ecd', h, fc2_weight) + fc2_bias[:, None, :]
        gates = jnp.take_along_axis(probs.T, idx, axis=1)
        flat_idx = idx.reshape(-1)
        contrib = (y * gates[:, :, None]).reshape(-1, d)
        output = jnp.zeros((n_tokens, d), dtype=x.dtype).at[flat_idx].add(contrib)
        gate_sums = jnp.zeros((n_tokens, 1), dtype=x.dtype).at[flat_idx].add(gates.reshape(-1, 1))
        assigned = gate_sums > 0
        output = jnp.where(assigned, output / jnp.where(assigned, gate_sums, 1.0), output)
        return output.reshape(b, l, d)
    x = L0_attn_x
    x = _layernorm(x + _L0_attn_ref(x, L0_attn_maa_x, L0_attn_maa_w, L0_attn_maa_k, L0_attn_maa_v, L0_attn_maa_r, L0_attn_maa_g, L0_attn_maa_w1, L0_attn_maa_w2, L0_attn_Wr, L0_attn_Wk, L0_attn_Wv, L0_attn_Wo, L0_attn_gate_w1, L0_attn_gate_w2, L0_attn_time_decay, L0_attn_decay_w1, L0_attn_decay_w2, L0_attn_u, L0_attn_ln_g, L0_attn_ln_b), axis=-1)
    x = _layernorm(x + _L0_ffn_ref(x, L0_ffn_norm_weight, L0_ffn_router_weight, L0_ffn_router_bias, L0_ffn_fc1_weight, L0_ffn_fc1_bias, L0_ffn_fc2_weight, L0_ffn_fc2_bias), axis=-1)
    return x

_drawn_inputs = setup_inputs


def setup_inputs(seed=0):
    import zlib

    import numpy as np

    out = dict(_drawn_inputs(seed))
    spreads = {'L0_attn_ln_g': (1.0, 0.6),
     'L0_attn_ln_b': (0.0, 0.8),
     'L0_ffn_norm_weight': (1.0, 0.2),
     'L0_ffn_router_bias': (0.0, 2.0),
     'L0_ffn_fc1_bias': (0.0, 0.323),
     'L0_ffn_fc2_bias': (0.0, 0.1)}
    factors = {'L0_attn_maa_x': 8.0,
     'L0_attn_maa_w': 64.0,
     'L0_attn_maa_k': 8.0,
     'L0_attn_maa_v': 8.0,
     'L0_attn_maa_r': 8.0,
     'L0_attn_maa_g': 8.0,
     'L0_attn_maa_w1': 8.0,
     'L0_attn_maa_w2': 8.0,
     'L0_attn_Wr': 2.903,
     'L0_attn_Wk': 2.9,
     'L0_attn_Wv': 2.846,
     'L0_attn_Wo': 2.9,
     'L0_attn_gate_w1': 2.916,
     'L0_attn_gate_w2': 2.862,
     'L0_attn_time_decay': 4.754,
     'L0_attn_decay_w1': 64.0,
     'L0_attn_decay_w2': 64.0,
     'L0_attn_u': 8.0}
    for name, (base, spread) in spreads.items():
        noise = np.random.default_rng([zlib.crc32(name.encode()), seed]).standard_normal(out[name].shape)
        drawn = base * np.exp(spread * noise) if base else spread * noise
        out[name] = jnp.asarray(drawn.astype(out[name].dtype))
    for name, factor in factors.items():
        out[name] = (out[name] * factor).astype(out[name].dtype)
    return out
```

```python
import concourse.bass as bass
from concourse import mybir
from contextlib import ExitStack

F32 = mybir.dt.float32
I32 = mybir.dt.int32
U32 = mybir.dt.uint32
ALU = mybir.AluOpType
ACT = mybir.ActivationFunctionType
AX = mybir.AxisListType

P = 128
NB, T, C = 16, 512, 256
H, N = 4, 64
HP = C // P
CH = T // P
NT = NB * T
E = 16
TILES = NT // P
ROW = C + E
ARow = C + 4
CAP = NT // E
SEG = P // E
ST = NT // SEG
FF = 1024
FT = FF // P
G = CAP // P
MIXES = ("w", "k", "v", "r", "g")
LEVELS = (1, 2, 4, 8, 16, 32, 64)
LN_EPS = 1e-5
GN_EPS = 0.00064
RMS_EPS = 1e-5

PE_FRONT = (["lora_a", "lora_b", "m_w0", "m_w1", "m_k0", "m_k1", "dec1", "m_v0", "m_v1", "k0", "k1",
             "m_r0", "m_r1", "dec0", "dec2", "m_g0", "m_g1", "v0", "v1", "r0", "r1", "gate1", "g0", "g1"])
ACT_FRONT = ["lora_a", "lora_b", "dec1", "k0", "k1", "dec0e", "dec0", "dec2e", "dec2", "v0", "v1", "r0", "r1",
             "gate1", "g0", "g1"]
DVE_FRONT = ["xx", "xxx0", "xxx1"] + [f"m_{f}{h}" for f in MIXES for h in range(HP)]
POOL_FRONT = [f"x{f}" for f in MIXES]
FRONT_READER = {j: ("dve" if j.startswith("m_") else "act") for j in PE_FRONT}

PE_BACK = (["d"] + [f"l{b}" for b in LEVELS] + ["kt0", "u0", "kt1", "u1", "kt2", "u2"]
           + ["y0", "y1", "y2", "y3", "zt0", "o0", "zt1", "o1", "zt2", "o2", "zt3", "o3"]
           + ["xt0", "xt1", "xt2", "xt3", "lg", "lt"])
BACK_JOBS = [j for j in PE_BACK if not j.startswith("l") or j in ("lg", "lt")]
BACK_READER = {j: ("dve" if j[0] in "duyo" or j == "lg" else "act") for j in BACK_JOBS}
ACT_BACK = (["r2", "k2", "at32a", "at32b", "at64"] + [f"at{q}" for q in range(4)]
            + ["kt0", "kt1", "kt2"] + [f"zt{c}" for c in range(CH)]
            + [f"xt{c}" for c in range(CH)] + ["exp", "lt"])
DVE_BACK = (["ruk0", "ruk1", "r2", "w2", "d", "a1"]
            + [s for b in LEVELS[1:5] for s in (f"r{2*b}", f"w{2*b}", f"a{b}")]
            + [s for b in LEVELS[5:] for s in (f"r{2*b}", f"w{2*b}")]
            + ["u0", "u0b", "u1", "u1b", "u2", "u2b"]
            + [s for c in range(CH) for s in (f"ysum{c}", f"y{c}", f"sq{c}", f"ssq{c}", f"yv{c}")]
            + [s for c in range(CH) for s in (f"z{c}",)]
            + [s for c in range(CH) for s in (f"o{c}", f"st{c}", f"mv{c}")]
            + ["ve", "q1", "q2", "q3"]
            + [s for c in range(CH) for s in (f"x2_{c}", f"xn{c}")]
            + ["lg", "lmax", "lsub", "lsum", "lrec", "probs"])
POOL_BACK = ([f"k{2*b}" for b in LEVELS] + [f"yr{c}" for c in range(CH)]
             + [s for c in range(CH) for s in (f"zg{c}", f"zb{c}", f"z{c}")]
             + ["rstd", "rn", "x2all"])


class Counts:

    def __init__(self, done, order, turns):
        self.done, self.order, self.turns = done, order, turns
        self.at = {key: 0 for key in order}


class EngineSteps:

    def __init__(self, eng, name, counts):
        self.eng, self.name, self.c = eng, name, counts

    def did(self, ins, part, step):
        key = (self.name, part)
        steps = self.c.order[key]
        assert steps[self.c.at[key] % len(steps)] == step, (key, step, steps[self.c.at[key] % len(steps)])
        self.c.at[key] += 1
        ins.then_inc(self.c.done[key], 1)

    def need(self, who, part, step, n):
        steps = self.c.order[(who, part)]
        self.eng.wait_ge(self.c.done[(who, part)], (n + 1) * len(steps) + steps.index(step) + 1)\
            .then_inc(self.c.turns[self.name], 1)

    def arrived(self, dma_sem, value):
        self.eng.wait_ge(dma_sem, value).then_inc(self.c.turns[self.name], 1)

    def credit(self, *parts):
        for part in parts:
            self.eng.sem_inc(self.c.done[(self.name, part)], len(self.c.order[(self.name, part)]))


def stage_a(nc, io, keep):
    with ExitStack() as ctx:
        def sb(name, shape, dt=F32):
            return ctx.enter_context(nc.sbuf_tensor(name, shape, dt))

        def sem(name):
            return ctx.enter_context(nc.semaphore(name))

        cols = sb("cols", [P, 16])
        rows = sb("rows", [P, 3 * C + E])
        w1 = sb("w1", [P, HP, 160])
        w2 = sb("w2", [P, C])
        w2g = sb("w2g", [32, C])
        Wp = {n: sb(f"W{n}", [P, HP, C]) for n in "rkvo"}
        W1 = {n: sb(f"W1{n}", [P, HP, 64]) for n in "wg"}
        W2 = {n: sb(f"W2{n}", [64, C]) for n in "wg"}
        rwT = sb("rwT", [P, HP, E])
        ident = sb("ident", [P, P])
        pairones = sb("pairones", [P, 2])
        masks = sb("masks", [P, 6, 32], I32)
        maskf = sb("maskf", [P, 6, 32])
        neghalf = sb("neghalf", [P, 4])

        def col(n, hp):
            return cols[:, 2 * n + hp:2 * n + hp + 1]

        MAA = {"x": 0, "w": 1, "k": 2, "v": 3, "r": 4, "g": 5}
        lng, lnb, nwb = rows[:, 0:C], rows[:, C:2 * C], rows[:, 2 * C:3 * C]
        rb = rows[:, 3 * C:3 * C + E]

        xT = sb("xT", [P, HP, T + 1])
        xx = sb("xx", [P, HP, T])
        xxx = sb("xxx", [P, HP, T])
        mix = {f: sb(f"mix{f}", [P, HP, T]) for f in MIXES}
        lora = sb("lora", [P, T])
        lorag = sb("lorag", [32, T])
        dec1 = sb("dec1", [64, T])
        dece = sb("dece", [P, T])
        gate1 = sb("gate1", [64, T])
        rn_ = sb("r_next", [P, HP, T])
        kn_ = sb("k_next", [P, HP, T])
        wn_ = sb("w_next", [P, HP, T])
        vn_ = sb("v_tok", [P, CH, C])
        gn_ = sb("g_tok", [P, CH, C])
        ruk = sb("ruk", [P, HP, T])
        R = sb("R", [P, HP, T])
        K = sb("K", [P, HP, T])
        W = {1: wn_}
        for b in LEVELS:
            W[2 * b] = sb(f"Wl{2*b}", [P, HP, T // (2 * b)])
        Ad = sb("Ad", [P, 2, CH * HP, 32])
        At = sb("At", [P, 2, CH * HP, P])
        KT = sb("KT", [P, CH - 1, C])
        S = sb("S", [P, CH - 1, HP, P])
        yc = sb("yc", [P, CH, C])
        ysq = sb("ysq", [P, C])
        ysum = sb("ysum", [P, CH, H])
        yssq = sb("yssq", [P, CH, H])
        yvar = sb("yvar", [P, CH, H])
        yrs = sb("yrs", [P, CH, H])
        z = yc
        zT = sb("zT", [P, CH, HP, P])
        xtok = sb("xtok", [P, CH, C])
        x1 = sb("x1", [P, CH, C])
        x2 = x1
        st = sb("st", [P, CH, 6])
        mv = sb("mv", [P, CH, 2])
        ve = sb("ve", [P, CH])
        rstd = sb("rstd", [P, CH])
        q1 = sb("q1", [P, CH])
        q2 = sb("q2", [P, CH])
        q3 = sb("q3", [P, CH])
        rn = sb("rn", [P, CH])
        table = sb("table", [P, CH, ROW])
        xnT = sb("xnT", [P, CH, HP, P])
        lg = sb("lg", [P, CH, E])
        lsub = sb("lsub", [P, CH, E])
        lexp = sb("lexp", [P, CH, E])
        lmax = sb("lmax", [P, CH])
        lsum = sb("lsum", [P, CH])
        lrec = sb("lrec", [P, CH])
        lt = sb("lt", [CH * E, P])

        LV = ctx.enter_context(nc.psum_tensor("LV", [P, 2, 512], F32))
        FB = [ctx.enter_context(nc.psum_tensor(f"FB{i}", [P, 512], F32)) for i in range(3)]
        BB = [ctx.enter_context(nc.psum_tensor(f"BB{i}", [P, 512], F32)) for i in range(3)]

        consts_in = sem("consts_in")
        setup_pool, setup_pool2 = sem("setup_pool"), sem("setup_pool2")
        masks_ready = sem("masks_ready")
        zeros_ready = sem("zeros_ready")
        xT_in, xtok_in = sem("xT_in"), sem("xtok_in")
        table_out, logits_out = sem("table_out"), sem("logits_out")
        done = {(e, part): sem(f"{e}_{part}") for e in ("pe", "act", "dve", "pool", "sp") for part in ("front", "back")}
        order = {("pe", "front"): PE_FRONT, ("act", "front"): ACT_FRONT, ("dve", "front"): DVE_FRONT,
                 ("pool", "front"): POOL_FRONT, ("pe", "back"): PE_BACK, ("act", "back"): ACT_BACK,
                 ("dve", "back"): DVE_BACK, ("pool", "back"): POOL_BACK, ("sp", "back"): ["table", "logits"]}
        turns = {e: sem(f"{e}_turns") for e in ("pe", "act", "dve", "pool", "sp")}
        counts = Counts(done, order, turns)

        def Steps(eng, name):
            return EngineSteps(eng, name, counts)

        block = ctx.enter_context(nc.Block())

        @block.sync
        def _(sp):
            me = Steps(sp, "sp")
            sp.dma_start(cols[:, :], io["cols"]).then_inc(consts_in, 16)
            sp.dma_start(rows[:, :], io["rows"].broadcast_to([P, 3 * C + E])).then_inc(consts_in, 16)
            sp.dma_start(w1[:, :, :], io["maa_w1"].rearrange("(a p) n -> p a n", p=P)).then_inc(consts_in, 16)
            sp.dma_start(w2[:, :], io["maa_w2"][0:P, :]).then_inc(consts_in, 16)
            sp.dma_start(w2g[:, :], io["maa_w2"][P:P + 32, :]).then_inc(consts_in, 16)
            for n in "rkvo":
                sp.dma_start(Wp[n][:, :, :], io[f"W{n}"].rearrange("(a p) n -> p a n", p=P)).then_inc(consts_in, 16)
            for n, name in (("w", "decay"), ("g", "gate")):
                sp.dma_start(W1[n][:, :, :], io[f"{name}_w1"].rearrange("(a p) n -> p a n", p=P)).then_inc(consts_in, 16)
                sp.dma_start(W2[n][:, :], io[f"{name}_w2"]).then_inc(consts_in, 16)
            sp.dma_start(rwT[:, :, :], io["rwT"].rearrange("(a p) n -> p a n", p=P)).then_inc(consts_in, 16)
            xT_dram = io["xT"].rearrange("(a p) n -> p a n", p=P)
            me.credit("back")

            def load(n):
                me.need("pool", "front", "xg", n - 1)
                sp.dma_start(xT[:, :, 1:T + 1], xT_dram[:, :, bass.ds(n * T, T)]).then_inc(xT_in, 16)
                me.need("dve", "back", "o3", n - 1)
                sp.dma_start(xtok[:, :, :], io["x"][bass.ds(n * T, T), :].rearrange("(c p) d -> p c d", p=P))\
                    .then_inc(xtok_in, 16)

            def store(n):
                me.need("dve", "back", "probs", n)
                sp.dma_start(io["table"][bass.ds(n * T, T), :].rearrange("(c p) d -> p c d", p=P), table[:, :, :])\
                    .then_inc(table_out, 16)
                me.need("act", "back", "lt", n)
                for c in range(CH):
                    sp.dma_start(io["logitsT"][:, bass.ds(n * T + c * P, P)], lt[c * E:(c + 1) * E, :])\
                        .then_inc(logits_out, 16)
                me.did(sp.wait_ge(table_out, 16 * (n + 1)), "back", "table")
                me.did(sp.wait_ge(logits_out, 16 * CH * (n + 1)), "back", "logits")

            load(0)
            with sp.Fori(0, NB - 1) as n:
                load(n + 1)
                store(n)
            store(NB - 1)

        @block.gpsimd
        def _(pool):
            me = Steps(pool, "pool")
            g = nc.gpsimd
            me.credit("front", "back")
            g.memset(ident[:, :], 0.0).then_inc(setup_pool, 1)
            g.memset(neghalf[:, :], -0.5).then_inc(setup_pool, 1)
            g.memset(pairones[:, :], 1.0).then_inc(setup_pool, 1)
            g.memset(maskf[:, :, :], 1.0).then_inc(setup_pool, 1)
            pool.wait_ge(setup_pool, 4)
            g.affine_select(out=ident[:, :], in_=ident[:, :], compare_op=ALU.not_equal, fill=1.0, base=0,
                            pattern=[[-1, P]], channel_multiplier=1).then_inc(setup_pool2, 1)
            g.affine_select(out=pairones[:, 0:1], in_=pairones[:, 0:1], compare_op=ALU.is_gt, fill=0.0,
                            base=N, pattern=[[0, 1]], channel_multiplier=-1).then_inc(setup_pool2, 1)
            g.affine_select(out=pairones[:, 1:2], in_=pairones[:, 1:2], compare_op=ALU.is_ge, fill=0.0,
                            base=-N, pattern=[[0, 1]], channel_multiplier=1).then_inc(setup_pool2, 1)
            k = 3
            for q in range(4):
                for li, b in enumerate(LEVELS[:5]):
                    blk = maskf[32 * q:32 * q + 32, li, :].rearrange("p (m o t) -> p m o t", o=2, t=b)
                    k += 1
                    g.memset(blk[:, :, 0, :], 0.0).then_inc(setup_pool2, 1)
                    odd = blk[:, :, 1, :]
                    pat = [[-2 * b, 32 // (2 * b)], [0, b]]
                    k += 1
                    g.affine_select(out=odd, in_=odd, compare_op=ALU.is_ge, fill=0.0, base=0, pattern=pat,
                                    channel_multiplier=1).then_inc(setup_pool2, 1)
                    pool.wait_ge(setup_pool2, k)
                    k += 1
                    g.affine_select(out=odd, in_=odd, compare_op=ALU.is_gt, fill=0.0, base=b,
                                    pattern=[[2 * b, 32 // (2 * b)], [0, b]],
                                    channel_multiplier=-1).then_inc(setup_pool2, 1)
                dq = maskf[32 * q:32 * q + 32, 5, :]
                k += 1
                g.affine_select(out=dq, in_=dq, compare_op=ALU.is_equal, fill=0.0, base=0, pattern=[[-1, 32]],
                                channel_multiplier=1).then_inc(setup_pool2, 1)
            pool.wait_ge(setup_pool2, k)
            g.tensor_copy(masks[:, :, :], maskf[:, :, :]).then_inc(masks_ready, 1)
            pool.wait_ge(consts_in, 16 * 14)
            pool.wait_ge(zeros_ready, 4)

            def front(n):
                for f in MIXES:
                    me.need("dve", "front", f"m_{f}1", n)
                    if f == "w":
                        pool.wait_ge(xT_in, 16 * (n + 1)).then_inc(turns["pool"], 1)
                    me.did(g.tensor_tensor(mix[f][:, :, :], mix[f][:, :, :], xT[:, :, 1:T + 1], ALU.add),
                           "front", f"x{f}")

            def back(n):
                for li, b in enumerate(LEVELS):
                    src = kn_ if b == 1 else K
                    if b == 1:
                        me.need("act", "front", "dec2", n)
                        me.need("act", "front", "k1", n)
                        me.need("pe", "back", "u2", n - 1)
                        me.need("pe", "back", "kt2", n - 1)
                    else:
                        me.need("pe", "back", f"l{b}", n)
                        me.need("dve", "back", f"w{b}", n)
                        if b == 2:
                            me.need("act", "back", "k2", n)
                        me.need("pool", "back", f"k{b}", n)
                    kv = K[:, :, :].rearrange("p h (m o t) -> p (h m) o t", o=2, t=b)
                    sv = src[:, :, :].rearrange("p h (m o t) -> p (h m) o t", o=2, t=b)
                    wv = W[b][:, :, :].rearrange("p h (m o) -> p (h m) o", o=2)
                    m = HP * T // (2 * b)
                    me.did(g.tensor_tensor(kv[:, :, 0, :], sv[:, :, 0, :], wv[:, :, 1:2].broadcast_to([P, m, b]),
                                           ALU.mult), "back", f"k{2*b}")
                for c in range(CH):
                    me.need("dve", "back", f"yv{c}", n)
                    me.did(g.tensor_tensor(yrs[:, c, :], yvar[:, c, :], neghalf[:, :], ALU.pow), "back", f"yr{c}")
                for c in range(CH):
                    me.need("dve", "back", f"z{c}", n)
                    me.need("act", "front", "g1", n)
                    me.did(g.tensor_tensor(z[:, c, :], z[:, c, :], lng, ALU.mult), "back", f"zg{c}")
                    me.need("pool", "back", f"zg{c}", n)
                    me.did(g.tensor_tensor(z[:, c, :], z[:, c, :], lnb, ALU.add), "back", f"zb{c}")
                    me.need("pool", "back", f"zb{c}", n)
                    me.did(g.tensor_tensor(z[:, c, :], z[:, c, :], gn_[:, c, :], ALU.mult), "back", f"z{c}")
                me.need("dve", "back", "ve", n)
                me.did(g.tensor_tensor(rstd[:, :], ve[:, :], neghalf[:, :], ALU.pow), "back", "rstd")
                me.need("dve", "back", "q3", n)
                me.did(g.tensor_tensor(rn[:, :], q3[:, :], neghalf[:, :], ALU.pow), "back", "rn")
                me.need("dve", "back", "x2_3", n)
                me.did(g.tensor_copy(keep["x2all"][:, bass.ds(n * CH, CH), :], x2[:, :, :]), "back", "x2all")

            with pool.Fori(0, NB) as n:
                front(n)
                back(n)

        @block.scalar
        def _(act):
            me = Steps(act, "act")
            a = nc.scalar
            me.credit("front", "back")
            act.wait_ge(consts_in, 16 * 14)
            act.wait_ge(zeros_ready, 4)

            def front(n):
                def take(job, out, rows_=P, func=ACT.Copy, src=None, **kw):
                    me.need("pe", "front", job, n)
                    bank = FB[PE_FRONT.index(job) % 3]
                    return a.activation(out, bank[0:rows_, :] if src is None else src, func, **kw)

                me.need("pe", "front", "m_r1", n - 1)
                me.did(take("lora_a", lora[:, :], func=ACT.Tanh), "front", "lora_a")
                me.need("pe", "front", "m_g1", n - 1)
                me.did(take("lora_b", lorag[:, :], 32, ACT.Tanh), "front", "lora_b")
                me.did(take("dec1", dec1[:, :], 64, ACT.Tanh), "front", "dec1")
                me.need("pool", "back", "k2", n - 1)
                me.need("act", "back", "k2", n - 1)
                me.need("dve", "back", "ruk1", n - 1)
                me.need("pe", "back", "l1", n - 1)
                for hp in range(HP):
                    me.did(take(f"k{hp}", kn_[:, hp, :]), "front", f"k{hp}")
                me.need("dve", "back", "w2", n - 1)
                for hp, job in ((0, "dec0"), (1, "dec2")):
                    if hp:
                        me.need("act", "front", "dec0", n)
                    me.did(take(job, dece[:, :], func=ACT.Exp, bias=col(6, hp)), "front", job + "e")
                    me.need("act", "front", job + "e", n)
                    me.did(a.activation(wn_[:, hp, :], dece[:, :], ACT.Exp, scale=-1.0), "front", job)
                me.need("pe", "back", "y3", n - 1)
                for j in range(2):
                    me.did(take(f"v{j}", vn_[:, 2 * j:2 * j + 2, :].rearrange("p c d -> p (c d)")), "front", f"v{j}")
                me.need("dve", "back", "r2", n - 1)
                me.need("act", "back", "r2", n - 1)
                for hp in range(HP):
                    me.did(take(f"r{hp}", rn_[:, hp, :]), "front", f"r{hp}")
                me.need("pe", "front", "g1", n - 1)
                me.did(take("gate1", gate1[:, :], 64, ACT.Tanh), "front", "gate1")
                me.need("pool", "back", "z3", n - 1)
                for j in range(2):
                    me.did(take(f"g{j}", gn_[:, 2 * j:2 * j + 2, :].rearrange("p c d -> p (c d)")), "front", f"g{j}")

            def back(n):
                def bank(job):
                    me.need("pe", "back", job, n)
                    return BB[BACK_JOBS.index(job) % 3]

                pair = "p h (m o) -> p (h m) o"
                me.need("pe", "back", "y3", n - 1)
                me.need("act", "front", "r1", n)
                me.did(a.activation(R[:, :, :].rearrange(pair, o=2)[:, :, 0:1],
                                    rn_[:, :, :].rearrange(pair, o=2)[:, :, 0:1], ACT.Copy), "back", "r2")
                me.need("pe", "back", "kt2", n - 1)
                me.did(a.activation(K[:, :, :].rearrange(pair, o=2)[:, :, 1:2],
                                    kn_[:, :, :].rearrange(pair, o=2)[:, :, 1:2], ACT.Copy), "back", "k2")
                me.need("pe", "back", "l32", n)
                for name, lo in (("at32a", 0), ("at32b", 64)):
                    for_par = At[lo:lo + 32, :, :, lo + 32:lo + 64]
                    me.did(a.activation(for_par, LV[lo:lo + 32, :, 0:256].rearrange("p b (j t) -> p b j t", t=32),
                                        ACT.Copy), "back", name)
                me.need("pe", "back", "l64", n)
                me.did(a.activation(At[0:64, :, :, 64:128], LV[0:64, :, :].rearrange("p b (j t) -> p b j t", t=64),
                                    ACT.Copy), "back", "at64")
                me.need("dve", "back", "a16", n)
                for q in range(4):
                    s = slice(32 * q, 32 * q + 32)
                    me.did(a.activation(At[s, :, :, s], Ad[s, :, :, :], ACT.Copy), "back", f"at{q}")
                for c in range(CH - 1):
                    me.did(a.activation(KT[:, c, :], bank(f"kt{c}")[:, 0:C], ACT.Copy), "back", f"kt{c}")
                for c in range(CH):
                    me.did(a.activation(zT[:, c, :, :].rearrange("p h t -> p (h t)"), bank(f"zt{c}")[:, 0:C],
                                        ACT.Copy), "back", f"zt{c}")
                for c in range(CH):
                    me.did(a.activation(xnT[:, c, :, :].rearrange("p h t -> p (h t)"), bank(f"xt{c}")[:, 0:C],
                                        ACT.Copy), "back", f"xt{c}")
                me.need("dve", "back", "lsub", n)
                me.did(a.activation(lexp[:, :, :], lsub[:, :, :], ACT.Exp), "back", "exp")
                me.need("sp", "back", "logits", n - 1)
                me.did(a.activation(lt[:, :], bank("lt")[0:CH * E, 0:P], ACT.Copy), "back", "lt")

            with act.Fori(0, NB) as n:
                front(n)
                back(n)

        @block.vector
        def _(dve):
            me = Steps(dve, "dve")
            v = nc.vector
            me.credit("front", "back")
            v.memset(xT[:, :, 0:1], 0.0).then_inc(zeros_ready, 1)
            v.memset(At[:, :, :, :], 0.0).then_inc(zeros_ready, 1)
            v.memset(Ad[:, :, :, :], 0.0).then_inc(zeros_ready, 1)
            v.memset(S[:, :, :, :], 0.0).then_inc(zeros_ready, 1)
            dve.wait_ge(zeros_ready, 4)
            dve.wait_ge(consts_in, 16 * 14)
            dve.wait_ge(masks_ready, 1)

            def front(n):
                dve.wait_ge(xT_in, 16 * (n + 1)).then_inc(turns["dve"], 1)
                me.did(v.tensor_tensor(xx[:, :, :], xT[:, :, 0:T], xT[:, :, 1:T + 1], ALU.subtract), "front", "xx")
                me.need("dve", "front", "xx", n)
                me.need("pe", "front", "lora_b", n - 1)
                for hp in range(HP):
                    me.did(v.scalar_tensor_tensor(xxx[:, hp, :], xx[:, hp, :], col(MAA["x"], hp),
                                                  xT[:, hp, 1:T + 1], ALU.mult, ALU.add), "front", f"xxx{hp}")
                last_use = {"w": "dec1", "k": "k1", "v": "v1", "r": "r1", "g": "gate1"}
                for f in MIXES:
                    me.need("pe", "front", last_use[f], n - 1)
                    for hp in range(HP):
                        me.need("pe", "front", f"m_{f}{hp}", n)
                        bank = FB[PE_FRONT.index(f"m_{f}{hp}") % 3]
                        me.did(v.scalar_tensor_tensor(mix[f][:, hp, :], bank[:, :], col(MAA[f], hp), xx[:, hp, :],
                                                      ALU.add, ALU.mult), "front", f"m_{f}{hp}")

            def back(n):
                def bank(job):
                    me.need("pe", "back", job, n)
                    return BB[BACK_JOBS.index(job) % 3]

                me.need("act", "front", "r1", n)
                me.need("pe", "back", "d", n - 1)
                for hp in range(HP):
                    me.did(v.scalar_tensor_tensor(ruk[:, hp, :], rn_[:, hp, :], col(7, hp), kn_[:, hp, :],
                                                  ALU.mult, ALU.mult), "back", f"ruk{hp}")

                def r_up(b):
                    src = rn_ if b == 1 else R
                    rv = R[:, :, :].rearrange("p h (m o t) -> p (h m) o t", o=2, t=b)
                    sv = src[:, :, :].rearrange("p h (m o t) -> p (h m) o t", o=2, t=b)
                    wv = W[b][:, :, :].rearrange("p h (m o) -> p (h m) o", o=2)
                    m = HP * T // (2 * b)
                    if b > 1:
                        me.need("dve", "back", f"w{b}", n)
                    me.did(v.tensor_tensor(rv[:, :, 1, :], sv[:, :, 1, :], wv[:, :, 0:1].broadcast_to([P, m, b]),
                                           ALU.mult), "back", f"r{2*b}")
                    if 2 * b in LEVELS:
                        me.need("pool", "back", f"k{4*b}", n - 1)
                    me.did(v.tensor_tensor(W[2 * b][:, :, :].rearrange("p h m -> p (h m)"), wv[:, :, 0], wv[:, :, 1],
                                           ALU.mult), "back", f"w{2*b}")

                def a_in(li, data, name):
                    mk = masks[:, li, :].rearrange("p (a j t) -> p a j t", a=1, j=1).broadcast_to([P, 2, CH * HP, 32])
                    me.did(v.copy_predicated(Ad[:, :, :, :], mk, data), "back", name)

                me.need("act", "back", "r2", n)
                me.need("pe", "back", "y3", n - 1)
                r_up(1)
                me.need("act", "back", "at3", n - 1)
                d = bank("d")[:, 0:2 * CH * HP]
                a_in(5, d.rearrange("p (a j o) -> p a j o", a=2, o=1).broadcast_to([P, 2, CH * HP, 32]), "d")
                for li, b in enumerate(LEVELS):
                    me.need("pe", "back", f"l{b}", n)
                    if b > 1:
                        r_up(b)
                    if b <= 16:
                        me.need("dve", "back", "d" if b == 1 else f"a{b//2}", n)
                        a_in(li, LV[:, :, 0:256].rearrange("p b (j t) -> p b j t", t=32), f"a{b}")
                for c in range(CH - 1):
                    u = bank(f"u{c}")
                    if c == 0:
                        me.need("pe", "back", "y3", n - 1)
                        for par, name in ((0, "u0"), (1, "u0b")):
                            s = slice(N * par, N * par + N)
                            me.did(v.tensor_copy(S[s, 0, :, s], u[s, 0:C].rearrange("p (h j) -> p h j", h=HP)[:, :, s]),
                                   "back", name)
                    else:
                        me.need("dve", "back", f"u{c-1}b", n)
                        me.need("dve", "back", "w128", n)
                        for par, name in ((0, f"u{c}"), (1, f"u{c}b")):
                            s = slice(N * par, N * par + N)
                            for hp in range(HP):
                                ins = v.scalar_tensor_tensor(S[s, c, hp, s], S[s, c - 1, hp, s], W[P][s, hp, c:c + 1],
                                                             u[s, hp * P + N * par:hp * P + N * par + N],
                                                             ALU.mult, ALU.add)
                            me.did(ins, "back", name)
                for c in range(CH):
                    y = bank(f"y{c}")[:, 0:C].rearrange("p (h j) -> p h j", h=H)
                    ycv = yc[:, c, :].rearrange("p (h j) -> p h j", h=H)
                    me.did(v.tensor_reduce(ysum[:, c, :], y, AX.X, ALU.add), "back", f"ysum{c}")
                    me.need("dve", "back", f"ysum{c}", n)
                    me.need("pe", "back", f"zt{c}", n - 1)
                    me.did(v.scalar_tensor_tensor(ycv, ysum[:, c, :].rearrange("p (h o) -> p h o", o=1)
                                                  .broadcast_to([P, H, N]), -1.0 / N, y, ALU.mult, ALU.add),
                           "back", f"y{c}")
                    me.need("dve", "back", f"y{c}", n)
                    me.did(v.tensor_tensor(ysq[:, :], yc[:, c, :], yc[:, c, :], ALU.mult), "back", f"sq{c}")
                    me.need("dve", "back", f"sq{c}", n)
                    me.did(v.tensor_reduce(yssq[:, c, :], ysq[:, :].rearrange("p (h j) -> p h j", h=H), AX.X, ALU.add),
                           "back", f"ssq{c}")
                    me.need("dve", "back", f"ssq{c}", n)
                    me.did(v.tensor_scalar(yvar[:, c, :], yssq[:, c, :], 1.0 / N, GN_EPS, ALU.mult, ALU.add),
                           "back", f"yv{c}")
                for c in range(CH):
                    me.need("pool", "back", f"yr{c}", n)
                    ycv = yc[:, c, :].rearrange("p (h j) -> p h j", h=H)
                    me.did(v.tensor_tensor(ycv, ycv, yrs[:, c, :].rearrange("p (h o) -> p h o", o=1)
                                           .broadcast_to([P, H, N]), ALU.mult), "back", f"z{c}")
                dve.wait_ge(xtok_in, 16 * (n + 1)).then_inc(turns["dve"], 1)
                me.need("pool", "back", "x2all", n - 1)
                for c in range(CH):
                    me.did(v.tensor_tensor(x1[:, c, :], bank(f"o{c}")[:, 0:C], xtok[:, c, :], ALU.add), "back", f"o{c}")
                    me.need("dve", "back", f"o{c}", n)
                    me.did(v.bn_stats(st[:, c, :], x1[:, c, :]), "back", f"st{c}")
                    me.need("dve", "back", f"st{c}", n)
                    me.did(v.bn_aggr(mv[:, c, :], st[:, c, :]), "back", f"mv{c}")
                me.need("dve", "back", "mv3", n)
                me.did(v.tensor_scalar(ve[:, :], mv[:, :, 1], LN_EPS, None, ALU.add), "back", "ve")
                me.need("pool", "back", "rstd", n)
                me.did(v.tensor_tensor(q1[:, :], rstd[:, :], rstd[:, :], ALU.mult), "back", "q1")
                me.need("dve", "back", "q1", n)
                me.did(v.tensor_tensor(q2[:, :], q1[:, :], mv[:, :, 1], ALU.mult), "back", "q2")
                me.need("dve", "back", "q2", n)
                me.did(v.tensor_scalar(q3[:, :], q2[:, :], RMS_EPS, None, ALU.add), "back", "q3")
                me.need("pool", "back", "rn", n)
                me.need("sp", "back", "table", n - 1)
                for c in range(CH):
                    me.did(v.tensor_scalar(x2[:, c, :], x1[:, c, :], mv[:, c, 0:1], rstd[:, c:c + 1],
                                           ALU.subtract, ALU.mult), "back", f"x2_{c}")
                    me.need("dve", "back", f"x2_{c}", n)
                    me.did(v.scalar_tensor_tensor(table[:, c, 0:C], x2[:, c, :], rn[:, c:c + 1], nwb,
                                                  ALU.mult, ALU.mult), "back", f"xn{c}")
                lgb = bank("lg")[:, 0:CH * E].rearrange("p (c e) -> p c e", c=CH)
                me.did(v.tensor_tensor(lg[:, :, :], lgb, rb.rearrange("p (o e) -> p o e", o=1)
                                       .broadcast_to([P, CH, E]), ALU.add), "back", "lg")
                me.need("dve", "back", "lg", n)
                me.did(v.tensor_reduce(lmax[:, :], lg[:, :, :], AX.X, ALU.max), "back", "lmax")
                me.need("dve", "back", "lmax", n)

                def per_chunk(t):
                    return t[:, :].rearrange("p (c o) -> p c o", o=1).broadcast_to([P, CH, E])

                me.did(v.tensor_tensor(lsub[:, :, :], lg[:, :, :], per_chunk(lmax), ALU.subtract), "back", "lsub")
                me.need("act", "back", "exp", n)
                me.did(v.tensor_reduce(lsum[:, :], lexp[:, :, :], AX.X, ALU.add), "back", "lsum")
                me.need("dve", "back", "lsum", n)
                me.did(v.reciprocal(lrec[:, :], lsum[:, :]), "back", "lrec")
                me.need("dve", "back", "lrec", n)
                me.did(v.tensor_tensor(table[:, :, C:ROW], lexp[:, :, :], per_chunk(lrec), ALU.mult), "back", "probs")

            with dve.Fori(0, NB) as n:
                front(n)
                back(n)

        @block.tensor
        def _(pe):
            me = Steps(pe, "pe")
            mm = nc.tensor.matmul
            me.credit("front", "back")
            pe.wait_ge(consts_in, 16 * 14)
            pe.wait_ge(setup_pool2, 3)
            pe.wait_ge(zeros_ready, 4)

            def front(n):
                def bank(job):
                    j = PE_FRONT.index(job)
                    old = PE_FRONT[j - 3]
                    me.need(FRONT_READER[old], "front", old + ("e" if old in ("dec0", "dec2") else ""),
                            n if j >= 3 else n - 1)
                    return FB[j % 3]

                def chan_major(job, lhs, src, m=P, lo=0):
                    out = bank(job)
                    for a in range(HP):
                        ins = mm(out[0:m, :], lhs[:, a, lo:lo + m], src[:, a, :], start=(a == 0), stop=(a == HP - 1))
                    me.did(ins, "front", job)

                def mixes(f):
                    j = MIXES.index(f)
                    if f == "w":
                        me.need("act", "front", "lora_a", n)
                    if f == "g":
                        me.need("act", "front", "lora_b", n)
                    for hp in range(HP):
                        out = bank(f"m_{f}{hp}")
                        cs = slice(hp * P, hp * P + P)
                        if j < 4:
                            ins = mm(out[:, :], w2[32 * j:32 * j + 32, cs], lora[32 * j:32 * j + 32, :],
                                     start=True, stop=True, tile_position=(32 * j, 0))
                        else:
                            ins = mm(out[:, :], w2g[:, cs], lorag[:, :], start=True, stop=True)
                        me.did(ins, "front", f"m_{f}{hp}")

                def token_major(name, lhs, rhs):
                    for j in range(2):
                        out = bank(f"{name}{j}")
                        for cc in range(2):
                            t = slice((2 * j + cc) * P, (2 * j + cc + 1) * P)
                            for a in range(len(lhs)):
                                ins = mm(out[:, cc * C:cc * C + C], lhs[a][:, t], rhs[a], start=(a == 0),
                                         stop=(a == len(lhs) - 1))
                        me.did(ins, "front", f"{name}{j}")

                me.need("dve", "front", "xxx1", n)
                chan_major("lora_a", w1, xxx)
                chan_major("lora_b", w1, xxx, m=32, lo=P)
                mixes("w")
                mixes("k")
                me.need("pool", "front", "xw", n)
                chan_major("dec1", W1["w"], mix["w"], m=64)
                mixes("v")
                me.need("pool", "front", "xk", n)
                for hp in range(HP):
                    chan_major(f"k{hp}", Wp["k"], mix["k"], lo=hp * P)
                mixes("r")
                me.need("act", "front", "dec1", n)
                for hp, job in ((0, "dec0"), (1, "dec2")):
                    out = bank(job)
                    me.did(mm(out[:, :], W2["w"][:, hp * P:hp * P + P], dec1[:, :], start=True, stop=True),
                           "front", job)
                mixes("g")
                me.need("pool", "front", "xv", n)
                token_major("v", [mix["v"][:, a, :] for a in range(HP)], [Wp["v"][:, a, :] for a in range(HP)])
                me.need("pool", "front", "xr", n)
                for hp in range(HP):
                    chan_major(f"r{hp}", Wp["r"], mix["r"], lo=hp * P)
                me.need("pool", "front", "xg", n)
                chan_major("gate1", W1["g"], mix["g"], m=64)
                me.need("act", "front", "gate1", n)
                token_major("g", [gate1[:, :]], [W2["g"][:, :]])

            def back(n):
                def bank(job):
                    j = BACK_JOBS.index(job)
                    old = BACK_JOBS[j - 3] if j >= 3 else [o for i, o in enumerate(BACK_JOBS) if i % 3 == j][-1]
                    name = old + "b" if old[0] == "u" else old
                    me.need(BACK_READER[old], "back", name, n if j >= 3 else n - 1)
                    return BB[j % 3]

                me.need("dve", "back", "ruk1", n)
                out = bank("d")
                for c in range(CH):
                    for hp in range(HP):
                        j = c * HP + hp
                        ins = mm(out[:, j:j + CH * HP + 1:CH * HP], ruk[:, hp, c * P:c * P + P], pairones[:, :],
                                 start=True, stop=True)
                me.did(ins, "back", "d")
                for b in LEVELS:
                    if b == 1:
                        me.need("act", "front", "r1", n)
                        me.need("act", "back", "at64", n - 1)
                        r, k = rn_, kn_
                    else:
                        me.need("dve", "back", f"r{b}", n)
                        me.need("pool", "back", f"k{b}", n)
                        if b == 2:
                            me.need("act", "back", "r2", n)
                            me.need("act", "back", "k2", n)
                        if b <= 32:
                            me.need("dve", "back", f"a{b//2}", n)
                        else:
                            me.need("act", "back", "at32b", n)
                        r, k = R, K
                    for par in range(2):
                        i = slice(N * par, N * par + N)
                        for c in range(CH):
                            for hp in range(HP):
                                j = c * HP + hp
                                t0 = c * P
                                if b <= 16:
                                    parts = [(32 * q, 32, 32 * q, 32 * j) for q in range(4)]
                                elif b == 32:
                                    parts = [(32 * q, 32, 32 * q + 32, 32 * j) for q in (0, 2)]
                                else:
                                    parts = [(0, 64, 64, 64 * j)]
                                for s0, w, tt, o in parts:
                                    ins = mm(LV[s0:s0 + w, par, o:o + w], k[i, hp, t0 + s0:t0 + s0 + w],
                                             r[i, hp, t0 + tt:t0 + tt + w], start=True, stop=True,
                                             tile_position=(N * par, s0))
                    me.did(ins, "back", f"l{b}")
                me.need("pool", "back", "k128", n)
                me.need("act", "front", "v1", n)
                for c in range(CH - 1):
                    out = bank(f"kt{c}")
                    for hp in range(HP):
                        ins = nc.tensor.transpose(out[:, hp * P:hp * P + P], K[:, hp, c * P:c * P + P], ident[:, :])
                    me.did(ins, "back", f"kt{c}")
                    out = bank(f"u{c}")
                    me.need("act", "back", f"kt{c}", n)
                    for hp in range(HP):
                        ins = mm(out[:, hp * P:hp * P + P], KT[:, c, hp * P:hp * P + P],
                                 vn_[:, c, hp * P:hp * P + P], start=True, stop=True)
                    me.did(ins, "back", f"u{c}")
                me.need("act", "back", "at3", n)
                me.need("dve", "back", "r128", n)
                for c in range(CH):
                    out = bank(f"y{c}")
                    if c:
                        me.need("dve", "back", f"u{c-1}b", n)
                    for hp in range(HP):
                        if c:
                            mm(out[:, hp * P:hp * P + P], R[:, hp, c * P:c * P + P], S[:, c - 1, hp, :],
                               start=True, stop=False, skip_group_check=True)
                        for par in range(2):
                            o = hp * P + N * par
                            ins = mm(out[:, o:o + N], At[:, par, c * HP + hp, :], vn_[:, c, o:o + N],
                                     start=(c == 0), stop=True, skip_group_check=True)
                    me.did(ins, "back", f"y{c}")
                for c in range(CH):
                    out = bank(f"zt{c}")
                    me.need("pool", "back", f"z{c}", n)
                    for hp in range(HP):
                        ins = nc.tensor.transpose(out[:, hp * P:hp * P + P], z[:, c, hp * P:hp * P + P], ident[:, :])
                    me.did(ins, "back", f"zt{c}")
                    out = bank(f"o{c}")
                    me.need("act", "back", f"zt{c}", n)
                    for hp in range(HP):
                        ins = mm(out[:, 0:C], zT[:, c, hp, :], Wp["o"][:, hp, :], start=(hp == 0), stop=(hp == HP - 1))
                    me.did(ins, "back", f"o{c}")
                for c in range(CH):
                    out = bank(f"xt{c}")
                    me.need("dve", "back", f"xn{c}", n)
                    for hp in range(HP):
                        ins = nc.tensor.transpose(out[:, hp * P:hp * P + P], table[:, c, hp * P:hp * P + P], ident[:, :])
                    me.did(ins, "back", f"xt{c}")
                out = bank("lg")
                for c in range(CH):
                    me.need("act", "back", f"xt{c}", n)
                    for hp in range(HP):
                        ins = mm(out[:, c * E:c * E + E], xnT[:, c, hp, :], rwT[:, hp, :], start=(hp == 0),
                                 stop=(hp == HP - 1))
                me.did(ins, "back", "lg")
                out = bank("lt")
                me.need("dve", "back", "lg", n)
                me.did(nc.tensor.transpose(out[0:CH * E, 0:P], lg[:, :, :].rearrange("p c e -> p (c e)"), ident[:, :]),
                       "back", "lt")

            with pe.Fori(0, NB) as n:
                front(n)
                back(n)


def stage_b(nc, io, keep):
    with ExitStack() as ctx:
        def sb(name, shape, dt=F32):
            return ctx.enter_context(nc.sbuf_tensor(name, shape, dt))

        def sem(name):
            return ctx.enter_context(nc.semaphore(name))

        CLEAR = 4
        zeros = sb("zeros", [P, NT * ARow // P // CLEAR])
        acc_zero, acc_zeroed = sem("acc_zero"), sem("acc_zeroed")
        L = sb("L", [P, ST])
        ones = sb("ones", [P, ST])
        hit = sb("hit", [P, ST])
        gt = sb("gt", [P, ST])
        eq = sb("eq", [P, ST])
        ceq = sb("ceq", [P, ST])
        sel = sb("sel", [P, ST])
        cum = sb("cum", [P, ST])
        ends = sb("ends", [P, SEG])
        allends = sb("allends", [P, E * TILES])
        cmp = sb("cmp", [P, E, G, TILES])
        group = sb("group", [P, P])
        before = sb("before", [P, P])
        gi = sb("gi", [P, P], I32)
        gp = sb("gp", [P, P], I32)
        gj = sb("gj", [P, P], I32)
        slot_i = sb("slot_i", [P, G], I32)
        eoff_i = sb("eoff_i", [P, E * G], I32)
        eoff = sb("eoff", [P, E * G])
        key = sb("key", [P, 1], I32)
        bit = sb("bit", [P, 1], I32)
        cand = sb("cand", [P, 1], I32)
        flip = sb("flip", [P, 1], I32)
        thr = sb("thr", [P, 1], I32)
        take = sb("take", [P, 1], I32)
        cnt = sb("cnt", [P, 1])
        cnt2 = sb("cnt2", [P, 2])
        room = sb("room", [P, 1])
        offs = sb("offs", [P, 1])
        cnt3 = sb("cnt3", [P, 1])
        offs3 = sb("offs3", [P, 1])
        PT = ctx.enter_context(nc.psum_tensor("PT", [P, 512], F32))
        PG = ctx.enter_context(nc.psum_tensor("PG", [P, 512], F32))
        PE2 = ctx.enter_context(nc.psum_tensor("PE2", [P, 512], F32))
        PS = ctx.enter_context(nc.psum_tensor("PS", [P, 512], F32))
        logits_in, iotas, groups_ready = sem("logits_in"), sem("iotas"), sem("groups_ready")
        counted, summed = sem("counted"), sem("summed")
        chain = sem("chain")
        ends_ready, ends_out, ends_in, cum_out = sem("ends_ready"), sem("ends_out"), sem("ends_in"), sem("cum_out")
        dve_turns, pe_turns = sem("dve_turns_b"), sem("pe_turns_b")
        block = ctx.enter_context(nc.Block())

        @block.sync
        def _(sp):
            sp.dma_start(L[:, :], io["logitsT"].rearrange("e (s t) -> (e s) t", t=ST)).then_inc(logits_in, 16)
            sp.wait_ge(ends_ready, 1)
            sp.dma_start(io["ends"].rearrange("o (p t) -> (o p) t", p=P), ends[:, :]).then_inc(ends_out, 16)
            sp.dma_start(io["cum"].rearrange("(p t) j -> p (t j)", p=P), cum[:, :]).then_inc(cum_out, 16)
            sp.wait_ge(ends_out, 16)
            sp.dma_start(allends[:, :], io["ends"].broadcast_to([P, E * TILES])).then_inc(ends_in, 16)
            sp.wait_ge(ends_in, 16)
            sp.wait_ge(cum_out, 16)

        @block.gpsimd
        def _(pool):
            g = nc.gpsimd
            g.memset(zeros[:, :], 0.0).then_inc(acc_zero, 1)
            pool.wait_ge(acc_zero, 1)
            acc = io["acc"].rearrange("(p n) d -> p (n d)", p=P)
            w = zeros.shape[1]
            for j in range(CLEAR):
                pool.dma_start(acc[:, j * w:(j + 1) * w], zeros[:, :]).then_inc(acc_zeroed, 16)
            g.iota(gi[:, :], pattern=[[0, P]], base=0, channel_multiplier=1).then_inc(iotas, 1)
            g.iota(gj[:, :], pattern=[[1, P]], base=0, channel_multiplier=0).then_inc(iotas, 1)
            g.iota(slot_i[:, :], pattern=[[P, G]], base=0, channel_multiplier=1).then_inc(iotas, 1)
            g.iota(eoff_i[:, :], pattern=[[TILES, E], [0, G]], base=0, channel_multiplier=0).then_inc(iotas, 1)
            pool.wait_ge(acc_zeroed, 16 * CLEAR)

        @block.tensor
        def _(pe):
            pe.wait_ge(groups_ready, 1)
            with pe.Fori(0, 32) as i:
                pe.wait_ge(counted, i + 1).then_inc(pe_turns, 1)
                nc.tensor.matmul(PT[:, 0:1], group[:, :], cnt[:, :], start=True, stop=True).then_inc(summed, 1)
            pe.wait_ge(counted, 33)
            nc.tensor.matmul(PG[:, 0:2], group[:, :], cnt2[:, :], start=True, stop=True).then_inc(summed, 1)
            nc.tensor.matmul(PE2[:, 0:2], before[:, :], cnt2[:, :], start=True, stop=True).then_inc(summed, 1)
            pe.wait_ge(counted, 34)
            nc.tensor.matmul(PS[:, 0:1], before[:, :], cnt3[:, :], start=True, stop=True).then_inc(summed, 1)

        @block.vector
        def _(dve):
            v = nc.vector
            PRE, PER = 11, 6
            dve.wait_ge(iotas, 4)
            done = [0]

            def link(ins):
                done[0] += 1
                ins.then_inc(chain, 1)
                dve.wait_ge(chain, done[0])

            link(v.tensor_scalar(gp[:, :], gi[:, :], 3, None, ALU.logical_shift_right))
            link(v.tensor_scalar(eq[:, 0:P].bitcast(I32), gj[:, :], 3, None, ALU.logical_shift_right))
            link(v.tensor_tensor(group[:, :], gp[:, :], eq[:, 0:P].bitcast(I32), ALU.is_equal))
            link(v.tensor_tensor(before[:, :], gi[:, :], gj[:, :], ALU.is_lt))
            link(v.tensor_tensor(before[:, :], before[:, :], group[:, :], ALU.mult))
            link(v.tensor_copy(keep["slot"][:, :], slot_i[:, :]))
            link(v.tensor_copy(eoff[:, :], eoff_i[:, :]))
            link(v.memset(ones[:, :], 1.0))
            link(v.memset(key[:, :], 0))
            link(v.memset(bit[:, :], 1))
            link(v.tensor_scalar(bit[:, :], bit[:, :], 31, None, ALU.logical_shift_left))
            assert done[0] == PRE
            v.engine_nop().then_inc(groups_ready, 1)
            dve.wait_ge(logits_in, 16)
            with dve.Fori(0, 32) as i:
                def after(k):
                    dve.wait_ge(chain, PER * i + PRE + k).then_inc(dve_turns, 1)

                v.tensor_tensor(cand[:, :], key[:, :], bit[:, :], ALU.bitwise_or).then_inc(chain, 1)
                after(1)
                v.tensor_scalar(flip[:, :], cand[:, :], 31, -1, ALU.arith_shift_right, ALU.bitwise_xor)\
                    .then_inc(chain, 1)
                after(2)
                v.scalar_tensor_tensor(thr[:, :], flip[:, :], -2 ** 31, cand[:, :], ALU.bitwise_or, ALU.bitwise_xor)\
                    .then_inc(chain, 1)
                after(3)
                v.tensor_scalar(hit[:, :], L[:, :], thr[:, :].bitcast(F32), None, ALU.is_ge, ALU.add,
                                accum_out=cnt[:, :]).then_inc(counted, 1)
                v.tensor_scalar(bit[:, :], bit[:, :], 1, None, ALU.logical_shift_right).then_inc(chain, 1)
                dve.wait_ge(summed, i + 1).then_inc(dve_turns, 1)
                v.tensor_scalar(take[:, :], PT[:, 0:1], float(CAP), None, ALU.is_ge).then_inc(chain, 1)
                after(5)
                v.copy_predicated(key[:, :], take[:, :], cand[:, :]).then_inc(chain, 1)
                after(6)
            done[0] = 32 * PER + PRE
            link(v.tensor_scalar(flip[:, :], key[:, :], 31, -1, ALU.arith_shift_right, ALU.bitwise_xor))
            link(v.scalar_tensor_tensor(thr[:, :], flip[:, :], -2 ** 31, key[:, :], ALU.bitwise_or, ALU.bitwise_xor))
            T_ = thr[:, :].bitcast(F32)
            link(v.tensor_scalar(gt[:, :], L[:, :], T_, None, ALU.is_gt, ALU.add, accum_out=cnt2[:, 0:1]))
            v.tensor_scalar(eq[:, :], L[:, :], T_, None, ALU.is_equal, ALU.add, accum_out=cnt2[:, 1:2])\
                .then_inc(counted, 1)
            dve.wait_ge(summed, 34)
            link(v.tensor_scalar(room[:, :], PG[:, 0:1], -1.0, float(CAP), ALU.mult, ALU.add))
            link(v.tensor_copy(offs[:, :], PE2[:, 1:2]))
            link(v.tensor_tensor_scan(ceq[:, :], ones[:, :], eq[:, :], offs[:, :], ALU.mult, ALU.add))
            link(v.scalar_tensor_tensor(hit[:, :], ceq[:, :], room[:, :], eq[:, :], ALU.is_le, ALU.mult))
            v.scalar_tensor_tensor(sel[:, :], hit[:, :], 0.0, gt[:, :], ALU.add, ALU.add, accum_out=cnt3[:, :])\
                .then_inc(counted, 1)
            dve.wait_ge(summed, 35)
            link(v.tensor_copy(offs3[:, :], PS[:, 0:1]))
            link(v.tensor_tensor_scan(cum[:, :], ones[:, :], sel[:, :], offs3[:, :], ALU.mult, ALU.add))
            v.tensor_copy(ends[:, :], cum[:, :].rearrange("p (t j) -> p t j", j=P)[:, :, P - 1]).then_inc(ends_ready, 1)
            dve.wait_ge(ends_in, 16)
            e_v = allends[:, :].rearrange("p (e g t) -> p e g t", e=E, g=1).broadcast_to([P, E, G, TILES])
            s_v = keep["slot"][:, :].rearrange("p (e g t) -> p e g t", e=1, t=1).broadcast_to([P, E, G, TILES])
            link(v.tensor_tensor(cmp[:, :, :, :], e_v, s_v, ALU.is_le))
            link(v.tensor_reduce(keep["tile"][:, :], cmp[:, :, :, :].rearrange("p e g t -> p (e g) t"), AX.X, ALU.add))
            link(v.tensor_tensor(keep["cumrow"][:, :], keep["tile"][:, :], eoff[:, :], ALU.add))


C_PE = (["xt0", "xt1"], [f"h{f}" for f in range(FT)] + [f"y{g}" for g in range(G)])
C_ACT = (["xt0"], [f"h{f}" for f in range(FT)])
C_DVE = (["idx", "cmp", "pin", "tok", "xt1", "gate"], [s for g in range(G) for s in (f"yb{g}", f"y{g}", f"g{g}")])
C_POOL = (["cum", "rows"], ["add"])


def stage_c(nc, io, keep):
    with ExitStack() as ctx:
        def sb(name, shape, dt=F32):
            return ctx.enter_context(nc.sbuf_tensor(name, shape, dt))

        def sem(name):
            return ctx.enter_context(nc.semaphore(name))

        ident = sb("identc", [P, P])
        b1 = sb("b1", [P, E, FT])
        b2 = sb("b2", [P, C])
        w1 = sb("fw1", [P, HP, FF])
        w2 = sb("fw2", [P, FT, C])
        idx = sb("idx", [P, G], I32)
        crow = sb("crow", [P, G, P])
        cmp = sb("ccmp", [P, G, P])
        pin = sb("pin", [P, G])
        tok = sb("tok", [P, G], I32)
        tok2 = sb("tok2", [P, G], I32)
        xg = sb("xg", [P, G, ROW])
        xgT = sb("xgT", [P, HP, CAP])
        gate = sb("gate", [P, G])
        hT = sb("hT", [P, FT, CAP])
        yb = sb("yb", [P, C])
        yg = sb("yg", [P, G, ARow])
        XB = [ctx.enter_context(nc.psum_tensor(f"XB{i}", [P, 512], F32)) for i in range(2)]
        HB = [ctx.enter_context(nc.psum_tensor(f"HB{i}", [P, 512], F32)) for i in range(4)]
        YB = [ctx.enter_context(nc.psum_tensor(f"YB{i}", [P, 512], F32)) for i in range(2)]
        ident0, ready = sem("ident0"), sem("ready_c")
        yg_clear, b1_in = sem("yg_clear"), sem("b1_in")
        w1_in, w2_in, b2_in = sem("w1_in"), sem("w2_in"), sem("b2_in")
        crow_in, rows_in, added = sem("crow_in"), sem("rows_in"), sem("added")
        engines = ("pe", "act", "dve", "pool")
        done = {(e, part): sem(f"{e}_{part}_c") for e in engines for part in ("front", "back")}
        order = {(e, part): steps[i] for e, steps in zip(engines, (C_PE, C_ACT, C_DVE, C_POOL))
                 for i, part in enumerate(("front", "back"))}
        counts = Counts(done, order, {e: sem(f"{e}_turns_c") for e in engines + ("sp",)})
        block = ctx.enter_context(nc.Block())

        def rounds(eng, front, back):
            front(0)
            with eng.Fori(0, E - 1) as e:
                back(e)
                front(e + 1)
            back(E - 1)

        @block.sync
        def _(sp):
            me = EngineSteps(sp, "sp", counts)
            sp.dma_start(b1[:, :, :], io["b1"]).then_inc(b1_in, 16)
            with sp.Fori(0, E) as e:
                me.need("pe", "back", f"h{FT-1}", e - 1)
                sp.dma_start(w1[:, :, :], io["fc1T"][bass.ds(e, 1), :, :].rearrange("o (a p) f -> (o p) a f", p=P))\
                    .then_inc(w1_in, 16)
                me.need("dve", "back", f"yb{G-1}", e - 1)
                sp.dma_start(b2[:, :], io["b2"][bass.ds(e, 1), :].broadcast_to([P, C])).then_inc(b2_in, 16)
                me.need("pe", "back", f"y{G-1}", e - 1)
                sp.dma_start(w2[:, :, :], io["fc2T"][bass.ds(e, 1), :, :].rearrange("o (j p) d -> (o p) j d", p=P))\
                    .then_inc(w2_in, 16)

        @block.gpsimd
        def _(pool):
            me = EngineSteps(pool, "pool", counts)
            g = nc.gpsimd
            me.credit("front", "back")
            g.memset(ident[:, :], 0.0).then_inc(ident0, 1)
            pool.wait_ge(ident0, 1)
            g.affine_select(out=ident[:, :], in_=ident[:, :], compare_op=ALU.not_equal, fill=1.0, base=0,
                            pattern=[[-1, P]], channel_multiplier=1).then_inc(ready, 1)

            def front(e):
                me.need("dve", "front", "idx", e)
                me.need("dve", "front", "cmp", e - 1)
                for j in range(G):
                    g.indirect_dma_start(crow[:, j, :], None, io["cum"],
                                         bass.IndirectOffsetOnAxis(ap=idx[:, j:j + 1], axis=0)).then_inc(crow_in, 16)
                me.did(pool.wait_ge(crow_in, 16 * G * (e + 1)), "front", "cum")
                me.need("dve", "front", "tok", e)
                me.need("dve", "front", "gate", e - 1)
                me.need("pe", "front", "xt1", e - 1)
                for j in range(G):
                    g.indirect_dma_start(xg[:, j, :], None, io["table"],
                                         bass.IndirectOffsetOnAxis(ap=tok[:, j:j + 1], axis=0)).then_inc(rows_in, 16)
                me.did(pool.wait_ge(rows_in, 16 * G * (e + 1)), "front", "rows")

            def back(e):
                for j in range(G):
                    me.need("dve", "back", f"g{j}", e)
                    g.indirect_dma_start(io["acc"], bass.IndirectOffsetOnAxis(ap=tok2[:, j:j + 1], axis=0),
                                         yg[:, j, :], None, compute_op=ALU.add).then_inc(added, 16)
                me.did(pool.wait_ge(added, 16 * G * (e + 1)), "back", "add")

            rounds(pool, front, back)

        @block.scalar
        def _(act):
            me = EngineSteps(act, "act", counts)
            a = nc.scalar
            me.credit("front", "back")
            act.wait_ge(b1_in, 16)

            def front(e):
                me.need("pe", "front", "xt0", e)
                me.need("pe", "back", f"h{FT-1}", e - 1)
                me.did(a.activation(xgT[:, 0, :], XB[0][:, :], ACT.Copy), "front", "xt0")

            def back(e):
                me.need("pe", "back", f"y{G-1}", e - 1)
                for f in range(FT):
                    me.need("pe", "back", f"h{f}", e)
                    me.did(a.activation(hT[:, f, :], HB[f % 4][:, :], ACT.Gelu,
                                        bias=b1[:, bass.ds(e, 1), f:f + 1].rearrange("p o f -> p (o f)")),
                           "back", f"h{f}")

            rounds(act, front, back)

        @block.vector
        def _(dve):
            me = EngineSteps(dve, "dve", counts)
            v = nc.vector
            me.credit("front", "back")
            v.memset(yg[:, :, :], 0.0).then_inc(yg_clear, 1)
            dve.wait_ge(yg_clear, 1)
            slot = keep["slot"][:, :].rearrange("p (g o) -> p g o", o=1).broadcast_to([P, G, P])

            def front(e):
                me.need("pool", "front", "cum", e - 1)
                me.did(v.tensor_copy(idx[:, :], keep["cumrow"][:, bass.ds(e * G, G)]), "front", "idx")
                me.need("pool", "front", "cum", e)
                me.did(v.tensor_tensor(cmp[:, :, :], crow[:, :, :], slot, ALU.is_le), "front", "cmp")
                me.need("dve", "front", "cmp", e)
                me.did(v.tensor_reduce(pin[:, :], cmp[:, :, :], AX.X, ALU.add), "front", "pin")
                me.need("dve", "front", "pin", e)
                me.need("pool", "front", "rows", e - 1)
                me.did(v.scalar_tensor_tensor(tok[:, :], keep["tile"][:, bass.ds(e * G, G)], float(P), pin[:, :],
                                              ALU.mult, ALU.add), "front", "tok")
                me.need("pool", "front", "rows", e)
                me.need("pe", "front", "xt1", e)
                me.need("pe", "back", f"h{FT-1}", e - 1)
                me.did(v.tensor_copy(xgT[:, 1, :], XB[1][:, :]), "front", "xt1")
                me.need("dve", "back", f"g{G-1}", e - 1)
                me.did(v.tensor_copy(gate[:, :], xg[:, :, bass.ds(e + C, 1)].rearrange("p g o -> p (g o)")),
                       "front", "gate")

            def back(e):
                me.arrived(b2_in, 16 * (e + 1))
                me.need("pool", "back", "add", e - 1)
                me.need("dve", "front", "gate", e)
                for j in range(G):
                    if j:
                        me.need("dve", "back", f"y{j-1}", e)
                    me.need("pe", "back", f"y{j}", e)
                    me.did(v.tensor_tensor(yb[:, :], YB[j % 2][:, 0:C], b2[:, :], ALU.add), "back", f"yb{j}")
                    me.need("dve", "back", f"yb{j}", e)
                    if j == 0:
                        v.tensor_copy(tok2[:, :], tok[:, :])
                    v.tensor_copy(yg[:, j, C:C + 1], gate[:, j:j + 1])
                    me.did(v.tensor_scalar(yg[:, j, 0:C], yb[:, :], gate[:, j:j + 1], None, ALU.mult), "back", f"y{j}")
                    me.did(v.engine_nop(), "back", f"g{j}")

            rounds(dve, front, back)

        @block.tensor
        def _(pe):
            me = EngineSteps(pe, "pe", counts)
            mm = nc.tensor.matmul
            me.credit("front", "back")
            pe.wait_ge(ready, 1)

            def front(e):
                me.need("pool", "front", "rows", e)
                for hp in range(HP):
                    me.need("act" if hp == 0 else "dve", "front", f"xt{hp}", e - 1)
                    for j in range(G):
                        ins = nc.tensor.transpose(XB[hp][:, j * P:j * P + P], xg[:, j, hp * P:hp * P + P], ident[:, :])
                    me.did(ins, "front", f"xt{hp}")

            def up(e):
                me.arrived(w1_in, 16 * (e + 1))
                me.need("act", "front", "xt0", e)
                me.need("dve", "front", "xt1", e)
                for f in range(FT):
                    me.need("act", "back", f"h{(f-4) % FT}", e if f >= 4 else e - 1)
                    for a in range(HP):
                        ins = mm(HB[f % 4][:, :], w1[:, a, f * P:f * P + P], xgT[:, a, :], start=(a == 0),
                                 stop=(a == HP - 1))
                    me.did(ins, "back", f"h{f}")

            def down(e):
                me.arrived(w2_in, 16 * (e + 1))
                for j in range(G):
                    me.need("dve", "back", f"yb{(j-2) % G}", e if j >= 2 else e - 1)
                    for f in range(FT):
                        if j == 0:
                            me.need("act", "back", f"h{f}", e)
                        ins = mm(YB[j % 2][:, 0:C], hT[:, f, j * P:j * P + P], w2[:, f, :], start=(f == 0),
                                 stop=(f == FT - 1))
                    me.did(ins, "back", f"y{j}")

            front(0)
            with pe.Fori(0, E - 1) as e:
                up(e)
                down(e)
                front(e + 1)
            up(E - 1)
            down(E - 1)


D_SP, D_POOL = ["in"], ["rstd"]
D_DVE = ["den", "rec"] + [s for c in range(CH) for s in (f"x{c}", f"st{c}", f"mv{c}")] + ["ve", "nm"]
D_ACT = [f"o{c}" for c in range(CH)]


def stage_d(nc, io, keep):
    with ExitStack() as ctx:
        def sb(name, shape, dt=F32):
            return ctx.enter_context(nc.sbuf_tensor(name, shape, dt))

        def sem(name):
            return ctx.enter_context(nc.semaphore(name))

        BUF = 2
        acc = sb("accb", [P, BUF, CH, ARow])
        o = sb("ob", [P, BUF, CH, C])
        x3 = sb("x3", [P, BUF, CH, C])
        neghalf = sb("neghalf_d", [P, CH])
        small = {k: sb(k + "_d", [P, BUF, CH]) for k in ("den", "rec", "ve", "rstd", "nm")}
        st = sb("st_d", [P, BUF, CH, 6])
        mv = sb("mv_d", [P, BUF, CH, 2])
        half_ready = sem("half_ready")
        acc_in, out_done = [sem(f"acc_in{b}") for b in range(BUF)], [sem(f"out_done{b}") for b in range(BUF)]
        engines = ("act", "dve", "pool")
        parts = [f"b{b}" for b in range(BUF)]
        done = {(e, p): sem(f"{e}_{p}_d") for e in engines + ("sp",) for p in parts}
        order = {(e, p): s for e, s in (("act", D_ACT), ("dve", D_DVE), ("pool", D_POOL), ("sp", D_SP)) for p in parts}
        counts = Counts(done, order, {e: sem(f"{e}_turns_d") for e in engines + ("sp",)})
        block = ctx.enter_context(nc.Block())

        def rows(b, n):
            return bass.ds((n * BUF + b) * T, T)

        @block.sync
        def _(sp):
            me = EngineSteps(sp, "sp", counts)
            with sp.Fori(0, NB // BUF) as n:
                for b in range(BUF):
                    me.need("dve", f"b{b}", f"x{CH-1}", n - 1)
                    sp.dma_start(acc[:, b, :, :], io["acc"][rows(b, n), :].rearrange("(c p) d -> p c d", p=P))\
                        .then_inc(acc_in[b], 16)

        @block.gpsimd
        def _(pool):
            me = EngineSteps(pool, "pool", counts)
            g = nc.gpsimd
            me.credit(*parts)
            g.memset(neghalf[:, :], -0.5).then_inc(half_ready, 1)
            pool.wait_ge(half_ready, 1)
            with pool.Fori(0, NB // BUF) as n:
                for b in range(BUF):
                    me.need("dve", f"b{b}", "ve", n)
                    me.did(g.tensor_tensor(small["rstd"][:, b, :], small["ve"][:, b, :], neghalf[:, :], ALU.pow),
                           f"b{b}", "rstd")

        @block.vector
        def _(dve):
            me = EngineSteps(dve, "dve", counts)
            v = nc.vector
            me.credit(*parts)
            with dve.Fori(0, NB // BUF) as n:
                for b in range(BUF):
                    p = f"b{b}"
                    me.arrived(acc_in[b], 16 * (n + 1))
                    gs = acc[:, b, :, C]
                    me.did(v.scalar_tensor_tensor(small["den"][:, b, :], gs, 0.0, gs, ALU.is_le, ALU.add), p, "den")
                    me.need("dve", p, "den", n)
                    me.did(v.reciprocal(small["rec"][:, b, :], small["den"][:, b, :]), p, "rec")
                    me.need("dve", p, "rec", n)
                    me.need("act", p, f"o{CH-1}", n - 1)
                    for c in range(CH):
                        x2c = keep["x2all"][:, bass.ds((n * BUF + b) * CH + c, 1), :].rearrange("p o d -> p (o d)")
                        me.did(v.scalar_tensor_tensor(x3[:, b, c, :], acc[:, b, c, 0:C], small["rec"][:, b, c:c + 1],
                                                      x2c, ALU.mult, ALU.add), p, f"x{c}")
                        me.need("dve", p, f"x{c}", n)
                        me.did(v.bn_stats(st[:, b, c, :], x3[:, b, c, :]), p, f"st{c}")
                        me.need("dve", p, f"st{c}", n)
                        me.did(v.bn_aggr(mv[:, b, c, :], st[:, b, c, :]), p, f"mv{c}")
                    me.need("dve", p, f"mv{CH-1}", n)
                    me.did(v.tensor_scalar(small["ve"][:, b, :], mv[:, b, :, 1], LN_EPS, None, ALU.add), p, "ve")
                    me.need("pool", p, "rstd", n)
                    me.did(v.scalar_tensor_tensor(small["nm"][:, b, :], mv[:, b, :, 0], -1.0, small["rstd"][:, b, :],
                                                  ALU.mult, ALU.mult), p, "nm")

        @block.scalar
        def _(act):
            me = EngineSteps(act, "act", counts)
            a = nc.scalar
            me.credit(*parts)
            for b in range(BUF):
                act.sem_inc(done[("sp", f"b{b}")], 1)
            with act.Fori(0, NB // BUF) as n:
                for b in range(BUF):
                    p = f"b{b}"
                    me.need("dve", p, "nm", n)
                    me.need("sp", p, "in", n - 1)
                    for c in range(CH):
                        me.did(a.activation(o[:, b, c, :], x3[:, b, c, :], ACT.Identity, bias=small["nm"][:, b, c:c + 1],
                                            scale=small["rstd"][:, b, c:c + 1]), p, f"o{c}")
                    me.need("act", p, f"o{CH-1}", n)
                    act.dma_start(io["out"][rows(b, n), :].rearrange("(c p) d -> p c d", p=P), o[:, b, :, :])\
                        .then_inc(out_done[b], 16)
                    act.wait_ge(out_done[b], 16 * (n + 1)).then_inc(done[("sp", p)], 1)


def build(nc, io):
    with ExitStack() as ctx:
        keep = {"x2all": ctx.enter_context(nc.sbuf_tensor("x2all", [P, TILES, C], F32)),
                "slot": ctx.enter_context(nc.sbuf_tensor("slot", [P, G], F32)),
                "tile": ctx.enter_context(nc.sbuf_tensor("tile", [P, E * G], F32)),
                "cumrow": ctx.enter_context(nc.sbuf_tensor("cumrow", [P, E * G], F32))}
        stage_a(nc, io, keep)
        stage_b(nc, io, keep)
        stage_c(nc, io, keep)
        stage_d(nc, io, keep)


def kernel(**inputs):
    import numpy as np
    import concourse.bacc as bacc
    from concourse.bass_utils import run_bass_kernel_spmd as run

    g = {k: np.asarray(v) for k, v in inputs.items()}
    A = "L0_attn_"
    x = g[A + "x"].reshape(NT, C)
    cols = np.stack([g[A + k].reshape(HP, P) for k in
                     ("maa_x", "maa_w", "maa_k", "maa_v", "maa_r", "maa_g", "time_decay", "u")])
    F = "L0_ffn_"
    arrays = {
        "x": x, "xT": x.T,
        "cols": cols.reshape(16, P).T,
        "rows": np.concatenate([g[A + "ln_g"], g[A + "ln_b"], g[F + "norm_weight"], g[F + "router_bias"]])[None],
        "maa_w1": g[A + "maa_w1"], "maa_w2": g[A + "maa_w2"].reshape(160, C),
        "Wr": g[A + "Wr"], "Wk": g[A + "Wk"], "Wv": g[A + "Wv"], "Wo": g[A + "Wo"],
        "decay_w1": g[A + "decay_w1"], "decay_w2": g[A + "decay_w2"],
        "gate_w1": g[A + "gate_w1"], "gate_w2": g[A + "gate_w2"],
        "rwT": g[F + "router_weight"].T,
        "fc1T": g[F + "fc1_weight"].transpose(0, 2, 1), "fc2T": g[F + "fc2_weight"].transpose(0, 2, 1),
        "b1": g[F + "fc1_bias"].reshape(E, FT, P).transpose(2, 0, 1), "b2": g[F + "fc2_bias"],
    }
    arrays = {f"in_{k}": np.ascontiguousarray(v) for k, v in arrays.items()}
    nc = bacc.Bacc("TRN2", target_bir_lowering=False, num_devices=1)
    io = {k[3:]: nc.dram_tensor(k, v.shape, mybir.dt.from_np(v.dtype), kind="ExternalInput").ap()
          for k, v in arrays.items()}
    io["out"] = nc.dram_tensor("out_dram", (NT, C), F32, kind="ExternalOutput").ap()
    for name, shape in (("table", (NT, ROW)), ("logitsT", (E, NT)), ("ends", (1, E * TILES)),
                        ("cum", (E * TILES, P)), ("acc", (NT, ARow))):
        io[name] = nc.dram_tensor(f"tmp_{name}", shape, F32, kind="Internal").ap()
    build(nc, io)
    r = run(nc, [arrays], core_ids=[0])
    return r.results[0]["out_dram"].reshape(NB, T, C)
```

```python
import concourse.bass as bass
from concourse import mybir
from contextlib import ExitStack

F32 = mybir.dt.float32
I32 = mybir.dt.int32
U32 = mybir.dt.uint32
ALU = mybir.AluOpType
ACT = mybir.ActivationFunctionType
AX = mybir.AxisListType

P = 128
NB, T, C = 16, 512, 256
H, N = 4, 64
HP = C // P
CH = T // P
NT = NB * T
E = 16
TILES = NT // P
ROW = C + E
ARow = C + 4
CAP = NT // E
SEG = P // E
ST = NT // SEG
FF = 1024
FT = FF // P
G = CAP // P
MIXES = ("w", "k", "v", "r", "g")
LEVELS = (1, 2, 4, 8, 16, 32, 64)
LN_EPS = 1e-5
GN_EPS = 0.00064
RMS_EPS = 1e-5

PE_FRONT = ["lora_a", "lora_b", "m_w0", "m_w1", "m_k0", "m_k1", "dec1", "m_v0", "m_v1", "k0", "k1",
            "m_r0", "m_r1", "dec0", "dec2", "m_g0", "m_g1", "r0", "r1", "gate1", "v0", "v1"]
ACT_FRONT = ["lora_a", "lora_b", "dec1", "k0", "k1", "dec0e", "dec0", "dec2e", "dec2", "r0", "r1", "gate1",
             "v0", "v1", "k2", "r2"]
DVE_PRE = ["xx", "xxx0", "xxx1"]
DVE_FRONT = [f"m_{f}{h}" for f in MIXES for h in range(HP)] + ["ruk0", "ruk1", "r2", "w2"]
POOL_FRONT = [f"x{f}" for f in MIXES] + ["k2"]
FRONT_READER = {j: ("dve", j) if j.startswith("m_") else ("act", j + "e" * (j in ("dec0", "dec2")))
                for j in PE_FRONT}

PE_BACK = ["d", "l1", "l2", "g0", "g1"] + [f"l{b}" for b in LEVELS[2:]] + ["kt0", "kt1", "u0", "u1", "y0", "y1"]
BACK_JOBS = ["d", "g0", "g1", "kt0", "kt1", "u0", "u1", "y0", "y1"]
BACK_READER = {"d": ("dve", "d"), "g0": ("act", "g0"), "g1": ("act", "g1"), "kt0": ("act", "kt0"),
               "kt1": ("act", "kt1"), "u0": ("dve", "s1b"), "u1": ("dve", "s2b"), "y0": ("dve", "y1"),
               "y1": ("dve", "y3")}
ACT_BACK = ["g0", "g1"] + [f"at{q}" for q in range(4)] + ["at32a", "at32b", "at64", "kt0", "kt1"]
DVE_BACK = (["d", "a1"]
            + [s for b in LEVELS[1:5] for s in (f"r{2*b}", f"w{2*b}", f"a{b}")]
            + [s for b in LEVELS[5:] for s in (f"r{2*b}", f"w{2*b}")]
            + ["s0", "s0b", "s1", "s1b", "s2", "s2b"]
            + [s for c in (0, 2) for s in (f"ysum{c}", f"ysum{c+1}", f"y{c}", f"y{c+1}", f"sq{c}", f"sq{c+1}",
                                           f"ssq{c}", f"ssq{c+1}", f"yv{c}")]
            + [s for c in (0, 2) for s in (f"zr{c}", f"zr{c+1}", f"zg{c}", f"zg{c+1}")])
POOL_BACK = ([f"k{2*b}" for b in LEVELS[1:]] + ["yr0", "yr2"]
             + [s for c in (0, 2) for s in (f"zb{c}", f"zb{c+1}", f"z{c}", f"z{c+1}")])

PE_TAIL = ["zt0", "o0", "zt1", "o1", "xt0", "xt1", "lg", "lt"]
TAIL_READER = {"zt0": ("act", "zt0"), "o0": ("dve", "o1"), "zt1": ("act", "zt1"), "o1": ("dve", "o3"),
               "xt0": ("act", "xt0"), "xt1": ("act", "xt1"), "lg": ("dve", "lg"), "lt": ("act", "lt")}
ACT_TAIL = ["zt0", "zt1", "xt0", "xt1", "exp", "lt"]
DVE_TAIL = ([s for c in (0, 2) for s in (f"o{c}", f"o{c+1}", f"st{c}", f"st{c+1}", f"mv{c}", f"mv{c+1}")]
            + ["ve", "q1", "q2", "q3"] + [f"x2_{c}" for c in range(CH)] + [f"xn{c}" for c in range(CH)]
            + ["lg", "lmax", "lsub", "lsum", "lrec", "probs"])
POOL_TAIL = ["rstd", "rn", "x2all"]
PARTS = ("front", "back", "tail")

TURNS = {
    "pe": "BB F B B FT B FT B FTF B TF B FF B FT B FT B FT B F T",
    "act": "F BT F T B F B F B T B F T F T F F T",
    "dve": "B BF BFT BF BT B T F T B F B F T P B F T B",
    "pool": "BF BF BF BT BTF B F T F B B",
}


def take_turns(pattern, **pieces):
    for turn in pattern.replace(" ", ""):
        if pieces.get(turn):
            next(pieces[turn])
    for turn, part in pieces.items():
        assert not part or next(part, "end") == "end", f"{turn} has pieces left"


def rounds(eng, pattern, front, back, tail, pre=None):
    pre = pre or (lambda n: None)

    def alone(part):
        for _ in part or ():
            pass

    alone(pre(0))
    alone(front(0))
    alone(pre(1))
    take_turns(pattern, F=front(1), B=back(0), P=pre(2))
    with eng.Fori(1, NB - 2) as n:
        take_turns(pattern, F=front(n + 1), B=back(n), T=tail(n - 1), P=pre(n + 2))
    take_turns(pattern, F=front(NB - 1), B=back(NB - 2), T=tail(NB - 3))
    take_turns(pattern, B=back(NB - 1), T=tail(NB - 2))
    alone(tail(NB - 1))


class Counts:

    def __init__(self, done, order, turns):
        self.done, self.order, self.turns = done, order, turns
        self.at = {key: 0 for key in order}


class EngineSteps:

    def __init__(self, eng, name, counts):
        self.eng, self.name, self.c = eng, name, counts

    def did(self, ins, part, step):
        key = (self.name, part)
        steps = self.c.order[key]
        assert steps[self.c.at[key] % len(steps)] == step, (key, step, steps[self.c.at[key] % len(steps)])
        self.c.at[key] += 1
        ins.then_inc(self.c.done[key], 1)

    def need(self, who, part, step, n):
        steps = self.c.order[(who, part)]
        self.eng.wait_ge(self.c.done[(who, part)], (n + 1) * len(steps) + steps.index(step) + 1)\
            .then_inc(self.c.turns[self.name], 1)

    def arrived(self, dma_sem, value):
        self.eng.wait_ge(dma_sem, value).then_inc(self.c.turns[self.name], 1)

    def credit(self, *parts):
        for part in parts:
            self.eng.sem_inc(self.c.done[(self.name, part)], len(self.c.order[(self.name, part)]))


def stage_a(nc, io, keep):
    with ExitStack() as ctx:
        def sb(name, shape, dt=F32):
            return ctx.enter_context(nc.sbuf_tensor(name, shape, dt))

        def sem(name):
            return ctx.enter_context(nc.semaphore(name))

        cols = sb("cols", [P, 16])
        rows = sb("rows", [P, 3 * C + E])
        w1 = sb("w1", [P, HP, 160])
        w2 = sb("w2", [P, C])
        w2g = sb("w2g", [32, C])
        Wp = {n: sb(f"W{n}", [P, HP, C]) for n in "rkvo"}
        W1 = {n: sb(f"W1{n}", [P, HP, 64]) for n in "wg"}
        W2 = {n: sb(f"W2{n}", [64, C]) for n in "wg"}
        rwT = sb("rwT", [P, HP, E])
        ident = sb("ident", [P, P])
        pairones = sb("pairones", [P, 2])
        masks = sb("masks", [P, 6, 32], I32)
        maskf = sb("maskf", [P, 6, 32])
        neghalf = sb("neghalf", [P, 2, H])

        def col(n, hp):
            return cols[:, 2 * n + hp:2 * n + hp + 1]

        MAA = {"x": 0, "w": 1, "k": 2, "v": 3, "r": 4, "g": 5}
        lng, lnb, nwb = rows[:, 0:C], rows[:, C:2 * C], rows[:, 2 * C:3 * C]
        rb = rows[:, 3 * C:3 * C + E]

        xT = sb("xT", [P, HP, T + 1])
        xx = sb("xx", [P, HP, T])
        xxx = sb("xxx", [P, HP, T])
        mixbuf = [sb(f"mix{i}", [P, HP, T]) for i in range(3)]
        mix = {f: mixbuf[i % 3] for i, f in enumerate(MIXES)}
        lora = sb("lora", [P, T])
        lorag = sb("lorag", [32, T])
        dec1 = sb("dec1", [64, T])
        dece = sb("dece", [P, T])
        gate1 = sb("gate1", [64, T])
        rn_ = sb("r_next", [P, HP, T])
        kn_ = sb("k_next", [P, HP, T])
        wn_ = sb("w_next", [P, HP, T])
        vn_ = sb("v_tok", [P, CH, C])
        gn_ = sb("g_tok", [P, CH, C])
        ruk = sb("ruk", [P, HP, T])
        R = sb("R", [P, HP, T])
        K = sb("K", [P, HP, T])
        W = {1: wn_}
        for b in LEVELS:
            W[2 * b] = sb(f"Wl{2*b}", [P, HP, T // (2 * b)])
        Ad = sb("Ad", [P, 2, CH * HP, 32])
        At = sb("At", [P, 2, CH * HP, P])
        KT = sb("KT", [P, CH - 1, C])
        S = sb("S", [P, CH - 1, HP, P])
        yc = sb("yc", [P, CH, C])
        ysq = sb("ysq", [P, 2, C])
        ysum = sb("ysum", [P, CH, H])
        yssq = sb("yssq", [P, CH, H])
        yvar = sb("yvar", [P, CH, H])
        yrs = sb("yrs", [P, CH, H])
        z = yc
        zT = sb("zT", [P, CH, HP, P])
        xtok = sb("xtok", [P, CH, C])
        x1 = sb("x1", [P, CH, C])
        x2 = x1
        st = sb("st", [P, CH, 6])
        mv = sb("mv", [P, CH, 2])
        ve = sb("ve", [P, CH])
        rstd = sb("rstd", [P, CH])
        q1 = sb("q1", [P, CH])
        q2 = sb("q2", [P, CH])
        q3 = sb("q3", [P, CH])
        rn = sb("rn", [P, CH])
        table = sb("table", [P, CH, ROW])
        xnT = sb("xnT", [P, CH, HP, P])
        lg = sb("lg", [P, CH, E])
        lsub = sb("lsub", [P, CH, E])
        lexp = sb("lexp", [P, CH, E])
        lmax = sb("lmax", [P, CH])
        lsum = sb("lsum", [P, CH])
        lrec = sb("lrec", [P, CH])
        lt = sb("lt", [CH * E, P])

        LV = ctx.enter_context(nc.psum_tensor("LV", [P, 2, 512], F32))
        FB = [ctx.enter_context(nc.psum_tensor(f"FB{i}", [P, 512], F32)) for i in range(3)]
        BB = [ctx.enter_context(nc.psum_tensor(f"BB{i}", [P, 512], F32)) for i in range(2)]
        TB = ctx.enter_context(nc.psum_tensor("TB", [P, 512], F32))

        consts_in = sem("consts_in")
        setup_pool, setup_pool2 = sem("setup_pool"), sem("setup_pool2")
        masks_ready = sem("masks_ready")
        zeros_ready = sem("zeros_ready")
        xT_in, xtok_in = sem("xT_in"), sem("xtok_in")
        table_out, logits_out = sem("table_out"), sem("logits_out")
        order = {("pe", "front"): PE_FRONT, ("act", "front"): ACT_FRONT, ("dve", "front"): DVE_FRONT,
                 ("pool", "front"): POOL_FRONT, ("pe", "back"): PE_BACK, ("act", "back"): ACT_BACK,
                 ("dve", "back"): DVE_BACK, ("pool", "back"): POOL_BACK, ("pe", "tail"): PE_TAIL,
                 ("act", "tail"): ACT_TAIL, ("dve", "tail"): DVE_TAIL, ("pool", "tail"): POOL_TAIL,
                 ("sp", "tail"): ["table", "logits"], ("dve", "pre"): DVE_PRE}
        done = {key: sem("_".join(key)) for key in order}
        turns = {e: sem(f"{e}_turns") for e in ("pe", "act", "dve", "pool", "sp")}
        counts = Counts(done, order, turns)

        def Steps(eng, name):
            return EngineSteps(eng, name, counts)


        def ring(me, part, banks, jobs, reader, job, n):
            j = jobs.index(job)
            old = jobs[j - len(banks)] if j >= len(banks) else [o for i, o in enumerate(jobs)
                                                                 if i % len(banks) == j][-1]
            who, step = reader[old]
            me.need(who, part, step, n if j >= len(banks) else n - 1)
            return banks[j % len(banks)]

        block = ctx.enter_context(nc.Block())

        @block.sync
        def _(sp):
            me = Steps(sp, "sp")
            sp.dma_start(cols[:, :], io["cols"]).then_inc(consts_in, 16)
            sp.dma_start(rows[:, :], io["rows"].broadcast_to([P, 3 * C + E])).then_inc(consts_in, 16)
            sp.dma_start(w1[:, :, :], io["maa_w1"].rearrange("(a p) n -> p a n", p=P)).then_inc(consts_in, 16)
            sp.dma_start(w2[:, :], io["maa_w2"][0:P, :]).then_inc(consts_in, 16)
            sp.dma_start(w2g[:, :], io["maa_w2"][P:P + 32, :]).then_inc(consts_in, 16)
            for n in "rkvo":
                sp.dma_start(Wp[n][:, :, :], io[f"W{n}"].rearrange("(a p) n -> p a n", p=P)).then_inc(consts_in, 16)
            for n, name in (("w", "decay"), ("g", "gate")):
                sp.dma_start(W1[n][:, :, :], io[f"{name}_w1"].rearrange("(a p) n -> p a n", p=P)).then_inc(consts_in, 16)
                sp.dma_start(W2[n][:, :], io[f"{name}_w2"]).then_inc(consts_in, 16)
            sp.dma_start(rwT[:, :, :], io["rwT"].rearrange("(a p) n -> p a n", p=P)).then_inc(consts_in, 16)
            xT_dram = io["xT"].rearrange("(a p) n -> p a n", p=P)
            me.credit("tail")

            def load_xT(n):
                me.need("pool", "front", "xg", n - 1)
                sp.dma_start(xT[:, :, 1:T + 1], xT_dram[:, :, bass.ds(n * T, T)]).then_inc(xT_in, 16)

            def load_xtok(n):
                me.need("dve", "tail", "o3", n - 1)
                sp.dma_start(xtok[:, :, :], io["x"][bass.ds(n * T, T), :].rearrange("(c p) d -> p c d", p=P))\
                    .then_inc(xtok_in, 16)

            def store(n):
                me.need("dve", "tail", "probs", n)
                sp.dma_start(io["table"][bass.ds(n * T, T), :].rearrange("(c p) d -> p c d", p=P), table[:, :, :])\
                    .then_inc(table_out, 16)
                me.need("act", "tail", "lt", n)
                for c in range(CH):
                    sp.dma_start(io["logitsT"][:, bass.ds(n * T + c * P, P)], lt[c * E:(c + 1) * E, :])\
                        .then_inc(logits_out, 16)
                me.did(sp.wait_ge(table_out, 16 * (n + 1)), "tail", "table")
                me.did(sp.wait_ge(logits_out, 16 * CH * (n + 1)), "tail", "logits")

            load_xT(0)
            load_xtok(0)
            load_xT(1)
            load_xT(2)
            with sp.Fori(1, NB - 2) as n:
                load_xtok(n)
                load_xT(n + 2)
                store(n - 1)
            for n in (NB - 2, NB - 1):
                load_xtok(n)
                store(n - 1)
            store(NB - 1)

        @block.gpsimd
        def _(pool):
            me = Steps(pool, "pool")
            g = nc.gpsimd
            me.credit(*PARTS)
            g.memset(ident[:, :], 0.0).then_inc(setup_pool, 1)
            g.memset(neghalf[:, :, :], -0.5).then_inc(setup_pool, 1)
            g.memset(pairones[:, :], 1.0).then_inc(setup_pool, 1)
            g.memset(maskf[:, :, :], 1.0).then_inc(setup_pool, 1)
            pool.wait_ge(setup_pool, 4)
            g.affine_select(out=ident[:, :], in_=ident[:, :], compare_op=ALU.not_equal, fill=1.0, base=0,
                            pattern=[[-1, P]], channel_multiplier=1).then_inc(setup_pool2, 1)
            g.affine_select(out=pairones[:, 0:1], in_=pairones[:, 0:1], compare_op=ALU.is_gt, fill=0.0,
                            base=N, pattern=[[0, 1]], channel_multiplier=-1).then_inc(setup_pool2, 1)
            g.affine_select(out=pairones[:, 1:2], in_=pairones[:, 1:2], compare_op=ALU.is_ge, fill=0.0,
                            base=-N, pattern=[[0, 1]], channel_multiplier=1).then_inc(setup_pool2, 1)
            k = 3
            for q in range(4):
                for li, b in enumerate(LEVELS[:5]):
                    blk = maskf[32 * q:32 * q + 32, li, :].rearrange("p (m o t) -> p m o t", o=2, t=b)
                    k += 1
                    g.memset(blk[:, :, 0, :], 0.0).then_inc(setup_pool2, 1)
                    odd = blk[:, :, 1, :]
                    pat = [[-2 * b, 32 // (2 * b)], [0, b]]
                    k += 1
                    g.affine_select(out=odd, in_=odd, compare_op=ALU.is_ge, fill=0.0, base=0, pattern=pat,
                                    channel_multiplier=1).then_inc(setup_pool2, 1)
                    pool.wait_ge(setup_pool2, k)
                    k += 1
                    g.affine_select(out=odd, in_=odd, compare_op=ALU.is_gt, fill=0.0, base=b,
                                    pattern=[[2 * b, 32 // (2 * b)], [0, b]],
                                    channel_multiplier=-1).then_inc(setup_pool2, 1)
                dq = maskf[32 * q:32 * q + 32, 5, :]
                k += 1
                g.affine_select(out=dq, in_=dq, compare_op=ALU.is_equal, fill=0.0, base=0, pattern=[[-1, 32]],
                                channel_multiplier=1).then_inc(setup_pool2, 1)
            pool.wait_ge(setup_pool2, k)
            g.tensor_copy(masks[:, :, :], maskf[:, :, :]).then_inc(masks_ready, 1)
            pool.wait_ge(consts_in, 16 * 14)
            pool.wait_ge(zeros_ready, 4)

            def front(n):
                for f in MIXES:
                    me.need("dve", "front", f"m_{f}1", n)
                    if f == "w":
                        me.arrived(xT_in, 16 * (n + 1))
                    me.did(g.tensor_tensor(mix[f][:, :, :], mix[f][:, :, :], xT[:, :, 1:T + 1], ALU.add),
                           "front", f"x{f}")
                    yield
                me.need("act", "front", "dec2", n)
                me.need("pe", "back", "kt1", n - 1)
                k_up(1, kn_, "front")
                yield

            def k_up(b, src, part):
                kv = K[:, :, :].rearrange("p h (m o t) -> p (h m) o t", o=2, t=b)
                sv = src[:, :, :].rearrange("p h (m o t) -> p (h m) o t", o=2, t=b)
                wv = W[b][:, :, :].rearrange("p h (m o) -> p (h m) o", o=2)
                m = HP * T // (2 * b)
                me.did(g.tensor_tensor(kv[:, :, 0, :], sv[:, :, 0, :], wv[:, :, 1:2].broadcast_to([P, m, b]),
                                       ALU.mult), part, f"k{2*b}")

            def back(n):
                for b in LEVELS[1:]:
                    me.need("pe", "back", f"l{b}", n)
                    me.need("dve", "front" if b == 2 else "back", f"w{b}", n)
                    if b == 2:
                        me.need("act", "front", "k2", n)
                    me.need("pool", "front" if b == 2 else "back", f"k{b}", n)
                    k_up(b, K, "back")
                    yield
                for c in (0, 2):
                    me.need("dve", "back", f"yv{c}", n)
                    me.did(g.tensor_tensor(yrs[:, c:c + 2, :], yvar[:, c:c + 2, :], neghalf[:, :, :], ALU.pow),
                           "back", f"yr{c}")
                yield
                me.need("act", "back", "g1", n)
                for c2 in (0, 2):
                    pair = (c2, c2 + 1)
                    for c in pair:
                        me.need("dve", "back", f"zg{c}", n)
                        me.did(g.tensor_tensor(z[:, c, :], z[:, c, :], lnb, ALU.add), "back", f"zb{c}")
                    for c in pair:
                        me.need("pool", "back", f"zb{c}", n)
                        me.did(g.tensor_tensor(z[:, c, :], z[:, c, :], gn_[:, c, :], ALU.mult), "back", f"z{c}")
                yield

            def tail(n):
                nh = neghalf[:, :, :].rearrange("p a b -> p (a b)")[:, 0:CH]
                me.need("dve", "tail", "ve", n)
                me.did(g.tensor_tensor(rstd[:, :], ve[:, :], nh, ALU.pow), "tail", "rstd")
                yield
                me.need("dve", "tail", "q3", n)
                me.did(g.tensor_tensor(rn[:, :], q3[:, :], nh, ALU.pow), "tail", "rn")
                yield
                me.need("dve", "tail", "x2_3", n)
                me.did(g.tensor_copy(keep["x2all"][:, bass.ds(n * CH, CH), :], x2[:, :, :]), "tail", "x2all")
                yield

            rounds(pool, TURNS["pool"], front, back, tail)

        @block.scalar
        def _(act):
            me = Steps(act, "act")
            a = nc.scalar
            me.credit(*PARTS)
            act.wait_ge(consts_in, 16 * 14)
            act.wait_ge(zeros_ready, 4)

            def front(n):
                def take(job, out, rows_=P, func=ACT.Copy, step=None, **kw):
                    me.need("pe", "front", job, n)
                    me.did(a.activation(out, FB[PE_FRONT.index(job) % 3][0:rows_, :], func, **kw), "front",
                           step or job)

                me.need("pe", "front", "m_g1", n - 1)
                take("lora_a", lora[:, :], func=ACT.Tanh)
                take("lora_b", lorag[:, :], 32, ACT.Tanh)
                yield
                take("dec1", dec1[:, :], 64, ACT.Tanh)
                yield
                me.need("pool", "front", "k2", n - 1)
                me.need("act", "front", "r2", n - 1)
                me.need("dve", "front", "w2", n - 1)
                me.need("pe", "back", "l1", n - 1)
                for hp in range(HP):
                    take(f"k{hp}", kn_[:, hp, :])
                yield
                for hp, job in ((0, "dec0"), (1, "dec2")):
                    if hp:
                        me.need("act", "front", "dec0", n)
                    take(job, dece[:, :], func=ACT.Exp, step=job + "e", bias=col(6, hp))
                    me.need("act", "front", job + "e", n)
                    me.did(a.activation(wn_[:, hp, :], dece[:, :], ACT.Exp, scale=-1.0), "front", job)
                yield
                for hp in range(HP):
                    take(f"r{hp}", rn_[:, hp, :])
                yield
                me.need("pe", "back", "g1", n - 1)
                take("gate1", gate1[:, :], 64, ACT.Tanh)
                yield
                me.need("pe", "back", "y1", n - 1)
                for j in range(2):
                    take(f"v{j}", vn_[:, 2 * j:2 * j + 2, :].rearrange("p c d -> p (c d)"))
                yield
                pair = "p h (m o) -> p (h m) o"
                me.need("act", "front", "r1", n)
                me.did(a.activation(K[:, :, :].rearrange(pair, o=2)[:, :, 1:2],
                                    kn_[:, :, :].rearrange(pair, o=2)[:, :, 1:2], ACT.Copy), "front", "k2")
                me.did(a.activation(R[:, :, :].rearrange(pair, o=2)[:, :, 0:1],
                                    rn_[:, :, :].rearrange(pair, o=2)[:, :, 0:1], ACT.Copy), "front", "r2")
                yield

            def back(n):
                def bank(job):
                    me.need("pe", "back", job, n)
                    return BB[BACK_JOBS.index(job) % 2]

                me.need("pool", "back", "z3", n - 1)
                for j in range(2):
                    me.did(a.activation(gn_[:, 2 * j:2 * j + 2, :].rearrange("p c d -> p (c d)"),
                                        bank(f"g{j}")[:, :], ACT.Copy), "back", f"g{j}")
                yield
                me.need("dve", "back", "a16", n)
                for q in range(4):
                    s = slice(32 * q, 32 * q + 32)
                    me.did(a.activation(At[s, :, :, s], Ad[s, :, :, :], ACT.Copy), "back", f"at{q}")
                yield
                me.need("pe", "back", "l32", n)
                for name, lo in (("at32a", 0), ("at32b", 64)):
                    me.did(a.activation(At[lo:lo + 32, :, :, lo + 32:lo + 64],
                                        LV[lo:lo + 32, :, 0:256].rearrange("p b (j t) -> p b j t", t=32),
                                        ACT.Copy), "back", name)
                yield
                me.need("pe", "back", "l64", n)
                me.did(a.activation(At[0:64, :, :, 64:128], LV[0:64, :, :].rearrange("p b (j t) -> p b j t", t=64),
                                    ACT.Copy), "back", "at64")
                yield
                me.did(a.activation(KT[:, 0:2, :].rearrange("p c d -> p (c d)"), bank("kt0")[:, :], ACT.Copy),
                       "back", "kt0")
                me.did(a.activation(KT[:, 2, :], bank("kt1")[:, 0:C], ACT.Copy), "back", "kt1")
                yield

            def tail(n):
                for name, dst in (("zt", zT), ("xt", xnT)):
                    for j in range(2):
                        me.need("pe", "tail", f"{name}{j}", n)
                        me.did(a.activation(dst[:, 2 * j:2 * j + 2, :, :].rearrange("p c h t -> p (c h t)"),
                                            TB[:, :], ACT.Copy), "tail", f"{name}{j}")
                        yield
                me.need("dve", "tail", "lsub", n)
                me.did(a.activation(lexp[:, :, :], lsub[:, :, :], ACT.Exp), "tail", "exp")
                yield
                me.need("sp", "tail", "logits", n - 1)
                me.need("pe", "tail", "lt", n)
                me.did(a.activation(lt[:, :], TB[0:CH * E, 0:P], ACT.Copy), "tail", "lt")
                yield

            rounds(act, TURNS["act"], front, back, tail)

        @block.vector
        def _(dve):
            me = Steps(dve, "dve")
            v = nc.vector
            me.credit("pre", *PARTS)
            v.memset(xT[:, :, 0:1], 0.0).then_inc(zeros_ready, 1)
            v.memset(At[:, :, :, :], 0.0).then_inc(zeros_ready, 1)
            v.memset(Ad[:, :, :, :], 0.0).then_inc(zeros_ready, 1)
            v.memset(S[:, :, :, :], 0.0).then_inc(zeros_ready, 1)
            dve.wait_ge(zeros_ready, 4)
            dve.wait_ge(consts_in, 16 * 14)
            dve.wait_ge(masks_ready, 1)

            def pre(n):
                me.arrived(xT_in, 16 * (n + 1))
                me.need("dve", "front", "m_g1", n - 1)
                me.did(v.tensor_tensor(xx[:, :, :], xT[:, :, 0:T], xT[:, :, 1:T + 1], ALU.subtract), "pre", "xx")
                me.need("dve", "pre", "xx", n)
                me.need("pe", "front", "lora_b", n - 1)
                for hp in range(HP):
                    me.did(v.scalar_tensor_tensor(xxx[:, hp, :], xx[:, hp, :], col(MAA["x"], hp),
                                                  xT[:, hp, 1:T + 1], ALU.mult, ALU.add), "pre", f"xxx{hp}")
                yield

            def front(n):
                used = {"w": ("r1", n - 1), "k": ("gate1", n - 1), "v": ("v1", n - 1), "r": ("dec1", n), "g": ("k1", n)}
                for f in MIXES:
                    me.need("pe", "front", *used[f])
                    for hp in range(HP):
                        me.need("pe", "front", f"m_{f}{hp}", n)
                        bank = FB[PE_FRONT.index(f"m_{f}{hp}") % 3]
                        me.did(v.scalar_tensor_tensor(mix[f][:, hp, :], bank[:, :], col(MAA[f], hp), xx[:, hp, :],
                                                      ALU.add, ALU.mult), "front", f"m_{f}{hp}")
                    yield
                me.need("act", "front", "r1", n)
                me.need("pe", "back", "d", n - 1)
                for hp in range(HP):
                    me.did(v.scalar_tensor_tensor(ruk[:, hp, :], rn_[:, hp, :], col(7, hp), kn_[:, hp, :],
                                                  ALU.mult, ALU.mult), "front", f"ruk{hp}")
                yield
                me.need("pe", "back", "y1", n - 1)
                r_up(1, rn_, "front", n)
                yield

            def r_up(b, src, part, n):
                rv = R[:, :, :].rearrange("p h (m o t) -> p (h m) o t", o=2, t=b)
                sv = src[:, :, :].rearrange("p h (m o t) -> p (h m) o t", o=2, t=b)
                wv = W[b][:, :, :].rearrange("p h (m o) -> p (h m) o", o=2)
                m = HP * T // (2 * b)
                if b > 1:
                    me.need("dve", "front" if b == 2 else "back", f"w{b}", n)
                me.did(v.tensor_tensor(rv[:, :, 1, :], sv[:, :, 1, :], wv[:, :, 0:1].broadcast_to([P, m, b]),
                                       ALU.mult), part, f"r{2*b}")
                if 2 * b in LEVELS:
                    me.need("pool", "back", f"k{4*b}", n - 1)
                me.did(v.tensor_tensor(W[2 * b][:, :, :].rearrange("p h m -> p (h m)"), wv[:, :, 0], wv[:, :, 1],
                                       ALU.mult), part, f"w{2*b}")

            def back(n):
                def bank(job):
                    me.need("pe", "back", job, n)
                    return BB[BACK_JOBS.index(job) % 2]

                def a_in(li, data, name):
                    mk = masks[:, li, :].rearrange("p (a j t) -> p a j t", a=1, j=1).broadcast_to([P, 2, CH * HP, 32])
                    me.did(v.copy_predicated(Ad[:, :, :, :], mk, data), "back", name)

                me.need("act", "back", "at3", n - 1)
                d = bank("d")[:, 0:2 * CH * HP]
                a_in(5, d.rearrange("p (a j o) -> p a j o", a=2, o=1).broadcast_to([P, 2, CH * HP, 32]), "d")
                for li, b in enumerate(LEVELS):
                    me.need("pe", "back", f"l{b}", n)
                    if b > 1:
                        me.need("act", "front", "r2", n)
                        r_up(b, R, "back", n)
                    if b <= 16:
                        me.need("dve", "back", "d" if b == 1 else f"a{b//2}", n)
                        a_in(li, LV[:, :, 0:256].rearrange("p b (j t) -> p b j t", t=32), f"a{b}")
                    yield
                heads = [slice(N * par, N * par + N) for par in range(2)]
                for c in range(CH - 1):
                    u = bank(f"u{c//2}")[:, c % 2 * C:c % 2 * C + C]
                    if c == 0:
                        for s, name in zip(heads, ("s0", "s0b")):
                            me.did(v.tensor_copy(S[s, 0, :, s], u[s, :].rearrange("p (h j) -> p h j", h=HP)[:, :, s]),
                                   "back", name)
                    else:
                        me.need("dve", "back", f"s{c-1}b", n)
                        for s, name in zip(heads, (f"s{c}", f"s{c}b")):
                            for hp in range(HP):
                                ins = v.scalar_tensor_tensor(S[s, c, hp, s], S[s, c - 1, hp, s], W[P][s, hp, c:c + 1],
                                                             u[s, hp * P + s.start:hp * P + s.stop],
                                                             ALU.mult, ALU.add)
                            me.did(ins, "back", name)
                yield
                me.need("pe", "tail", "zt1", n - 1)
                for c2 in (0, 2):
                    pair = (c2, c2 + 1)
                    y = bank(f"y{c2//2}")

                    def head(t, c):
                        return t[:, c, :].rearrange("p (h j) -> p h j", h=H)

                    def ych(c):
                        return y[:, c % 2 * C:c % 2 * C + C].rearrange("p (h j) -> p h j", h=H)

                    for c in pair:
                        me.did(v.tensor_reduce(ysum[:, c, :], ych(c), AX.X, ALU.add), "back", f"ysum{c}")
                    for c in pair:
                        me.need("dve", "back", f"ysum{c}", n)
                        me.did(v.scalar_tensor_tensor(head(yc, c), ysum[:, c, :].rearrange("p (h o) -> p h o", o=1)
                                                      .broadcast_to([P, H, N]), -1.0 / N, ych(c), ALU.mult, ALU.add),
                               "back", f"y{c}")
                    for c in pair:
                        me.need("dve", "back", f"y{c}", n)
                        me.did(v.tensor_tensor(ysq[:, c % 2, :], yc[:, c, :], yc[:, c, :], ALU.mult), "back", f"sq{c}")
                    for c in pair:
                        me.need("dve", "back", f"sq{c}", n)
                        me.did(v.tensor_reduce(yssq[:, c, :], head(ysq, c % 2), AX.X, ALU.add), "back", f"ssq{c}")
                    me.need("dve", "back", f"ssq{c2+1}", n)
                    me.did(v.tensor_scalar(yvar[:, c2:c2 + 2, :], yssq[:, c2:c2 + 2, :], 1.0 / N, GN_EPS,
                                           ALU.mult, ALU.add), "back", f"yv{c2}")
                yield
                for c2 in (0, 2):
                    me.need("pool", "back", f"yr{c2}", n)
                    for c in (c2, c2 + 1):
                        me.did(v.tensor_tensor(head(yc, c), head(yc, c), yrs[:, c, :].rearrange("p (h o) -> p h o", o=1)
                                               .broadcast_to([P, H, N]), ALU.mult), "back", f"zr{c}")
                    for c in (c2, c2 + 1):
                        me.need("dve", "back", f"zr{c}", n)
                        me.did(v.tensor_tensor(z[:, c, :], z[:, c, :], lng, ALU.mult), "back", f"zg{c}")
                yield

            def tail(n):
                me.arrived(xtok_in, 16 * (n + 1))
                me.need("pool", "tail", "x2all", n - 1)
                for c2 in (0, 2):
                    me.need("pe", "tail", f"o{c2//2}", n)
                    for c in (c2, c2 + 1):
                        me.did(v.tensor_tensor(x1[:, c, :], TB[:, c % 2 * C:c % 2 * C + C], xtok[:, c, :], ALU.add),
                               "tail", f"o{c}")
                    for c in (c2, c2 + 1):
                        me.need("dve", "tail", f"o{c}", n)
                        me.did(v.bn_stats(st[:, c, :], x1[:, c, :]), "tail", f"st{c}")
                    for c in (c2, c2 + 1):
                        me.need("dve", "tail", f"st{c}", n)
                        me.did(v.bn_aggr(mv[:, c, :], st[:, c, :]), "tail", f"mv{c}")
                    if c2:
                        me.need("dve", "tail", "mv3", n)
                        me.did(v.tensor_scalar(ve[:, :], mv[:, :, 1], LN_EPS, None, ALU.add), "tail", "ve")
                    yield
                me.need("pool", "tail", "rstd", n)
                me.did(v.tensor_tensor(q1[:, :], rstd[:, :], rstd[:, :], ALU.mult), "tail", "q1")
                me.need("dve", "tail", "q1", n)
                me.did(v.tensor_tensor(q2[:, :], q1[:, :], mv[:, :, 1], ALU.mult), "tail", "q2")
                me.need("dve", "tail", "q2", n)
                me.did(v.tensor_scalar(q3[:, :], q2[:, :], RMS_EPS, None, ALU.add), "tail", "q3")
                yield
                me.need("pool", "tail", "rn", n)
                me.need("sp", "tail", "table", n - 1)
                for c in range(CH):
                    me.did(v.tensor_scalar(x2[:, c, :], x1[:, c, :], mv[:, c, 0:1], rstd[:, c:c + 1],
                                           ALU.subtract, ALU.mult), "tail", f"x2_{c}")
                for c in range(CH):
                    me.need("dve", "tail", f"x2_{c}", n)
                    me.did(v.scalar_tensor_tensor(table[:, c, 0:C], x2[:, c, :], rn[:, c:c + 1], nwb,
                                                  ALU.mult, ALU.mult), "tail", f"xn{c}")
                yield

                def per_chunk(t):
                    return t[:, :].rearrange("p (c o) -> p c o", o=1).broadcast_to([P, CH, E])

                me.need("pe", "tail", "lt", n - 1)
                me.need("pe", "tail", "lg", n)
                me.did(v.tensor_tensor(lg[:, :, :], TB[:, 0:CH * E].rearrange("p (c e) -> p c e", c=CH),
                                       rb.rearrange("p (o e) -> p o e", o=1).broadcast_to([P, CH, E]), ALU.add),
                       "tail", "lg")
                me.need("dve", "tail", "lg", n)
                me.did(v.tensor_reduce(lmax[:, :], lg[:, :, :], AX.X, ALU.max), "tail", "lmax")
                me.need("dve", "tail", "lmax", n)
                me.did(v.tensor_tensor(lsub[:, :, :], lg[:, :, :], per_chunk(lmax), ALU.subtract), "tail", "lsub")
                yield
                me.need("act", "tail", "exp", n)
                me.did(v.tensor_reduce(lsum[:, :], lexp[:, :, :], AX.X, ALU.add), "tail", "lsum")
                me.need("dve", "tail", "lsum", n)
                me.did(v.reciprocal(lrec[:, :], lsum[:, :]), "tail", "lrec")
                me.need("dve", "tail", "lrec", n)
                me.did(v.tensor_tensor(table[:, :, C:ROW], lexp[:, :, :], per_chunk(lrec), ALU.mult), "tail", "probs")
                yield

            rounds(dve, TURNS["dve"], front, back, tail, pre)

        @block.tensor
        def _(pe):
            me = Steps(pe, "pe")
            mm = nc.tensor.matmul
            me.credit(*PARTS)
            pe.wait_ge(consts_in, 16 * 14)
            pe.wait_ge(setup_pool2, 3)
            pe.wait_ge(zeros_ready, 4)

            def front(n):
                def bank(job):
                    return ring(me, "front", FB, PE_FRONT, FRONT_READER, job, n)

                def chan_major(job, lhs, src, m=P, lo=0):
                    out = bank(job)
                    for a in range(HP):
                        ins = mm(out[0:m, :], lhs[:, a, lo:lo + m], src[:, a, :], start=(a == 0), stop=(a == HP - 1))
                    me.did(ins, "front", job)

                def mixes(f):
                    j = MIXES.index(f)
                    me.need("act", "front", "lora_b", n)
                    for hp in range(HP):
                        out = bank(f"m_{f}{hp}")
                        cs = slice(hp * P, hp * P + P)
                        if j < 4:
                            ins = mm(out[:, :], w2[32 * j:32 * j + 32, cs], lora[32 * j:32 * j + 32, :],
                                     start=True, stop=True, tile_position=(32 * j, 0))
                        else:
                            ins = mm(out[:, :], w2g[:, cs], lorag[:, :], start=True, stop=True)
                        me.did(ins, "front", f"m_{f}{hp}")

                me.need("dve", "pre", "xxx1", n)
                chan_major("lora_a", w1, xxx)
                chan_major("lora_b", w1, xxx, m=32, lo=P)
                yield
                mixes("w")
                yield
                mixes("k")
                yield
                me.need("pool", "front", "xw", n)
                chan_major("dec1", W1["w"], mix["w"], m=64)
                yield
                mixes("v")
                yield
                me.need("pool", "front", "xk", n)
                for hp in range(HP):
                    chan_major(f"k{hp}", Wp["k"], mix["k"], lo=hp * P)
                yield
                mixes("r")
                yield
                me.need("act", "front", "dec1", n)
                for hp, job in ((0, "dec0"), (1, "dec2")):
                    out = bank(job)
                    me.did(mm(out[:, :], W2["w"][:, hp * P:hp * P + P], dec1[:, :], start=True, stop=True),
                           "front", job)
                yield
                mixes("g")
                yield
                me.need("pool", "front", "xr", n)
                for hp in range(HP):
                    chan_major(f"r{hp}", Wp["r"], mix["r"], lo=hp * P)
                yield
                me.need("pool", "front", "xg", n)
                chan_major("gate1", W1["g"], mix["g"], m=64)
                yield
                for j in range(2):
                    out = bank(f"v{j}")
                    for cc in range(2):
                        t = slice((2 * j + cc) * P, (2 * j + cc + 1) * P)
                        for a in range(HP):
                            ins = mm(out[:, cc * C:cc * C + C], mix["v"][:, a, t], Wp["v"][:, a, :], start=(a == 0),
                                     stop=(a == HP - 1))
                    me.did(ins, "front", f"v{j}")
                yield

            def back(n):
                def bank(job):
                    return ring(me, "back", BB, BACK_JOBS, BACK_READER, job, n)

                def gates():
                    me.need("act", "front", "gate1", n)
                    for j in range(2):
                        out = bank(f"g{j}")
                        for cc in range(2):
                            t = slice((2 * j + cc) * P, (2 * j + cc + 1) * P)
                            ins = mm(out[:, cc * C:cc * C + C], gate1[:, t], W2["g"][:, :], start=True, stop=True)
                        me.did(ins, "back", f"g{j}")

                me.need("dve", "front", "ruk1", n)
                out = bank("d")
                for c in range(CH):
                    for hp in range(HP):
                        j = c * HP + hp
                        ins = mm(out[:, j:j + CH * HP + 1:CH * HP], ruk[:, hp, c * P:c * P + P], pairones[:, :],
                                 start=True, stop=True)
                me.did(ins, "back", "d")
                yield
                for b in LEVELS:
                    if b == 1:
                        me.need("act", "front", "r1", n)
                        me.need("act", "back", "at64", n - 1)
                        r, k = rn_, kn_
                    else:
                        me.need("dve", "front" if b == 2 else "back", f"r{b}", n)
                        me.need("pool", "front" if b == 2 else "back", f"k{b}", n)
                        if b == 2:
                            me.need("act", "front", "r2", n)
                        if b <= 32:
                            me.need("dve", "back", f"a{b//2}", n)
                        else:
                            me.need("act", "back", "at32b", n)
                        r, k = R, K
                    for par in range(2):
                        i = slice(N * par, N * par + N)
                        for c in range(CH):
                            for hp in range(HP):
                                j = c * HP + hp
                                t0 = c * P
                                if b <= 16:
                                    parts = [(32 * q, 32, 32 * q, 32 * j) for q in range(4)]
                                elif b == 32:
                                    parts = [(32 * q, 32, 32 * q + 32, 32 * j) for q in (0, 2)]
                                else:
                                    parts = [(0, 64, 64, 64 * j)]
                                for s0, w, tt, o in parts:
                                    ins = mm(LV[s0:s0 + w, par, o:o + w], k[i, hp, t0 + s0:t0 + s0 + w],
                                             r[i, hp, t0 + tt:t0 + tt + w], start=True, stop=True,
                                             tile_position=(N * par, s0))
                    me.did(ins, "back", f"l{b}")
                    yield
                    if b == 2:
                        gates()
                        yield
                me.need("pool", "back", "k128", n)
                for j in range(2):
                    out = bank(f"kt{j}")
                    for c in range(2 * j, min(2 * j + 2, CH - 1)):
                        for hp in range(HP):
                            o = c % 2 * C + hp * P
                            ins = nc.tensor.transpose(out[:, o:o + P], K[:, hp, c * P:c * P + P], ident[:, :])
                    me.did(ins, "back", f"kt{j}")
                yield
                me.need("act", "front", "v1", n)
                for j in range(2):
                    out = bank(f"u{j}")
                    me.need("act", "back", f"kt{j}", n)
                    for c in range(2 * j, min(2 * j + 2, CH - 1)):
                        for hp in range(HP):
                            o = c % 2 * C + hp * P
                            ins = mm(out[:, o:o + P], KT[:, c, hp * P:hp * P + P],
                                     vn_[:, c, hp * P:hp * P + P], start=True, stop=True)
                    me.did(ins, "back", f"u{j}")
                yield
                me.need("act", "back", "at64", n)
                me.need("dve", "back", "r128", n)
                for c in range(CH):
                    if c % 2 == 0:
                        out = bank(f"y{c//2}")
                    if c:
                        me.need("dve", "back", f"s{c-1}b", n)
                    for hp in range(HP):
                        o = c % 2 * C + hp * P
                        if c:
                            mm(out[:, o:o + P], R[:, hp, c * P:c * P + P], S[:, c - 1, hp, :],
                               start=True, stop=False, skip_group_check=True)
                        for par in range(2):
                            ins = mm(out[:, o + N * par:o + N * par + N], At[:, par, c * HP + hp, :],
                                     vn_[:, c, hp * P + N * par:hp * P + N * par + N],
                                     start=(c == 0), stop=True, skip_group_check=True)
                    if c % 2:
                        me.did(ins, "back", f"y{c//2}")
                yield

            def tail(n):
                def bank(job):
                    return ring(me, "tail", [TB], PE_TAIL, TAIL_READER, job, n)

                def turned(job, src, chunks):
                    out = bank(job)
                    for c in chunks:
                        for hp in range(HP):
                            o = c % 2 * C + hp * P
                            ins = nc.tensor.transpose(out[:, o:o + P], src[:, c, hp * P:hp * P + P], ident[:, :])
                    me.did(ins, "tail", job)

                for j in range(2):
                    me.need("pool", "back", f"z{2*j+1}", n)
                    turned(f"zt{j}", z, (2 * j, 2 * j + 1))
                    yield
                    out = bank(f"o{j}")
                    for c in (2 * j, 2 * j + 1):
                        for hp in range(HP):
                            ins = mm(out[:, c % 2 * C:c % 2 * C + C], zT[:, c, hp, :], Wp["o"][:, hp, :],
                                     start=(hp == 0), stop=(hp == HP - 1))
                    me.did(ins, "tail", f"o{j}")
                    yield
                for j in range(2):
                    me.need("dve", "tail", f"xn{2*j+1}", n)
                    turned(f"xt{j}", table, (2 * j, 2 * j + 1))
                    yield
                out = bank("lg")
                for c in range(CH):
                    for hp in range(HP):
                        ins = mm(out[:, c * E:c * E + E], xnT[:, c, hp, :], rwT[:, hp, :], start=(hp == 0),
                                 stop=(hp == HP - 1))
                me.did(ins, "tail", "lg")
                yield
                out = bank("lt")
                me.did(nc.tensor.transpose(out[0:CH * E, 0:P], lg[:, :, :].rearrange("p c e -> p (c e)"), ident[:, :]),
                       "tail", "lt")
                yield

            rounds(pe, TURNS["pe"], front, back, tail)


def stage_b(nc, io, keep):
    with ExitStack() as ctx:
        def sb(name, shape, dt=F32):
            return ctx.enter_context(nc.sbuf_tensor(name, shape, dt))

        def sem(name):
            return ctx.enter_context(nc.semaphore(name))

        CLEAR = 4
        zeros = sb("zeros", [P, NT * ARow // P // CLEAR])
        acc_zero, acc_zeroed = sem("acc_zero"), sem("acc_zeroed")
        L = sb("L", [P, ST])
        ones = sb("ones", [P, ST])
        hit = sb("hit", [P, ST])
        gt = sb("gt", [P, ST])
        eq = sb("eq", [P, ST])
        ceq = sb("ceq", [P, ST])
        sel = sb("sel", [P, ST])
        cum = sb("cum", [P, ST])
        ends = sb("ends", [P, SEG])
        allends = sb("allends", [P, E * TILES])
        cmp = sb("cmp", [P, E, G, TILES])
        group = sb("group", [P, P])
        before = sb("before", [P, P])
        gi = sb("gi", [P, P], I32)
        gp = sb("gp", [P, P], I32)
        gj = sb("gj", [P, P], I32)
        slot_i = sb("slot_i", [P, G], I32)
        eoff_i = sb("eoff_i", [P, E * G], I32)
        eoff = sb("eoff", [P, E * G])
        now = sb("now", [P, 3], I32)
        both = sb("both", [P, 6], I32)
        bit = sb("bit", [P, 1], I32)
        flip2 = sb("flip2", [P, 2], I32)
        flip = sb("flip", [P, 1], I32)
        thr = sb("thr", [P, 1], I32)
        take = sb("take", [P, 1], I32)
        cnt = sb("cnt", [P, 1])
        cnt2 = sb("cnt2", [P, 2])
        room = sb("room", [P, 1])
        offs = sb("offs", [P, 1])
        cnt3 = sb("cnt3", [P, 1])
        offs3 = sb("offs3", [P, 1])
        PT = ctx.enter_context(nc.psum_tensor("PT", [P, 512], F32))
        PG = ctx.enter_context(nc.psum_tensor("PG", [P, 512], F32))
        PE2 = ctx.enter_context(nc.psum_tensor("PE2", [P, 512], F32))
        PS = ctx.enter_context(nc.psum_tensor("PS", [P, 512], F32))
        logits_in, iotas, groups_ready = sem("logits_in"), sem("iotas"), sem("groups_ready")
        counted, summed = sem("counted"), sem("summed")
        chain, decided = sem("chain"), sem("decided")
        ends_ready, ends_out, ends_in, cum_out = sem("ends_ready"), sem("ends_out"), sem("ends_in"), sem("cum_out")
        dve_turns, pe_turns = sem("dve_turns_b"), sem("pe_turns_b")
        block = ctx.enter_context(nc.Block())

        @block.sync
        def _(sp):
            sp.dma_start(L[:, :], io["logitsT"].rearrange("e (s t) -> (e s) t", t=ST)).then_inc(logits_in, 16)
            sp.wait_ge(ends_ready, 1)
            sp.dma_start(io["ends"].rearrange("o (p t) -> (o p) t", p=P), ends[:, :]).then_inc(ends_out, 16)
            sp.dma_start(io["cum"].rearrange("(p t) j -> p (t j)", p=P), cum[:, :]).then_inc(cum_out, 16)
            sp.wait_ge(ends_out, 16)
            sp.dma_start(allends[:, :], io["ends"].broadcast_to([P, E * TILES])).then_inc(ends_in, 16)
            sp.wait_ge(ends_in, 16)
            sp.wait_ge(cum_out, 16)

        @block.gpsimd
        def _(pool):
            g = nc.gpsimd
            g.memset(zeros[:, :], 0.0).then_inc(acc_zero, 1)
            pool.wait_ge(acc_zero, 1)
            acc = io["acc"].rearrange("(p n) d -> p (n d)", p=P)
            w = zeros.shape[1]
            for j in range(CLEAR):
                pool.dma_start(acc[:, j * w:(j + 1) * w], zeros[:, :]).then_inc(acc_zeroed, 16)
            g.iota(gi[:, :], pattern=[[0, P]], base=0, channel_multiplier=1).then_inc(iotas, 1)
            g.iota(gj[:, :], pattern=[[1, P]], base=0, channel_multiplier=0).then_inc(iotas, 1)
            g.iota(slot_i[:, :], pattern=[[P, G]], base=0, channel_multiplier=1).then_inc(iotas, 1)
            g.iota(eoff_i[:, :], pattern=[[TILES, E], [0, G]], base=0, channel_multiplier=0).then_inc(iotas, 1)
            pool.wait_ge(acc_zeroed, 16 * CLEAR)

        @block.tensor
        def _(pe):
            pe.wait_ge(groups_ready, 1)
            with pe.Fori(0, 32) as i:
                pe.wait_ge(counted, i + 1).then_inc(pe_turns, 1)
                nc.tensor.matmul(PT[:, 0:1], group[:, :], cnt[:, :], start=True, stop=True).then_inc(summed, 1)
            pe.wait_ge(counted, 33)
            nc.tensor.matmul(PG[:, 0:2], group[:, :], cnt2[:, :], start=True, stop=True).then_inc(summed, 1)
            nc.tensor.matmul(PE2[:, 0:2], before[:, :], cnt2[:, :], start=True, stop=True).then_inc(summed, 1)
            pe.wait_ge(counted, 34)
            nc.tensor.matmul(PS[:, 0:1], before[:, :], cnt3[:, :], start=True, stop=True).then_inc(summed, 1)

        @block.vector
        def _(dve):
            v = nc.vector
            PRE, PER = 16, 5
            dve.wait_ge(iotas, 4)
            done = [0]

            def link(ins):
                done[0] += 1
                ins.then_inc(chain, 1)
                dve.wait_ge(chain, done[0])

            link(v.tensor_scalar(gp[:, :], gi[:, :], 3, None, ALU.logical_shift_right))
            link(v.tensor_scalar(eq[:, 0:P].bitcast(I32), gj[:, :], 3, None, ALU.logical_shift_right))
            link(v.tensor_tensor(group[:, :], gp[:, :], eq[:, 0:P].bitcast(I32), ALU.is_equal))
            link(v.tensor_tensor(before[:, :], gi[:, :], gj[:, :], ALU.is_lt))
            link(v.tensor_tensor(before[:, :], before[:, :], group[:, :], ALU.mult))
            link(v.tensor_copy(keep["slot"][:, :], slot_i[:, :]))
            link(v.tensor_copy(eoff[:, :], eoff_i[:, :]))
            link(v.memset(ones[:, :], 1.0))
            link(v.memset(keep["tile"][:, E * G:], 0.0))
            link(v.memset(keep["cumrow"][:, E * G:], 0.0))
            link(v.memset(now[:, :], 0))
            link(v.memset(bit[:, :], 1))
            link(v.tensor_scalar(bit[:, :], bit[:, :], 30, None, ALU.logical_shift_left))
            link(v.tensor_scalar(now[:, 1:2], bit[:, :], 1, None, ALU.logical_shift_left))

            def as_float(out, key_):
                yield v.tensor_scalar(flip[:, :], key_, 31, -1, ALU.arith_shift_right, ALU.bitwise_xor)
                yield v.scalar_tensor_tensor(out, flip[:, :], -2 ** 31, key_, ALU.bitwise_or, ALU.bitwise_xor)

            for ins in as_float(now[:, 2:3], now[:, 1:2]):
                link(ins)
            assert done[0] == PRE, done
            v.engine_nop().then_inc(groups_ready, 1)
            dve.wait_ge(logits_in, 16)
            with dve.Fori(0, 32) as i:
                def after(k):
                    dve.wait_ge(chain, PER * i + PRE + k).then_inc(dve_turns, 1)

                v.tensor_scalar(hit[:, :], L[:, :], now[:, 2:3].bitcast(F32), None, ALU.is_ge, ALU.add,
                                accum_out=cnt[:, :]).then_inc(counted, 1)
                v.tensor_copy(both[:, 0:2], now[:, 0:2])
                v.tensor_scalar(both[:, 2:4], now[:, 0:2], bit[:, :], None, ALU.bitwise_or).then_inc(chain, 1)
                after(1)
                v.tensor_scalar(flip2[:, :], both[:, 2:4], 31, -1, ALU.arith_shift_right, ALU.bitwise_xor)\
                    .then_inc(chain, 1)
                v.tensor_scalar(bit[:, :], bit[:, :], 1, None, ALU.logical_shift_right)
                after(2)
                v.scalar_tensor_tensor(both[:, 4:6], flip2[:, :], -2 ** 31, both[:, 2:4], ALU.bitwise_or,
                                       ALU.bitwise_xor).then_inc(chain, 1)
                after(3)
                v.tensor_copy(now[:, :], both[:, 0:6:2]).then_inc(chain, 1)
                dve.wait_ge(summed, i + 1).then_inc(dve_turns, 1)
                v.tensor_scalar(take[:, :], PT[:, 0:1], float(CAP), None, ALU.is_ge).then_inc(chain, 1)
                after(5)
                v.copy_predicated(now[:, :], take[:, :].broadcast_to([P, 3]), both[:, 1:6:2]).then_inc(decided, 1)
                dve.wait_ge(decided, i + 1).then_inc(dve_turns, 1)
            done[0] = 32 * PER + PRE
            key = now[:, 0:1]
            for ins in as_float(thr[:, :], key):
                link(ins)
            T_ = thr[:, :].bitcast(F32)
            link(v.tensor_scalar(gt[:, :], L[:, :], T_, None, ALU.is_gt, ALU.add, accum_out=cnt2[:, 0:1]))
            v.tensor_scalar(eq[:, :], L[:, :], T_, None, ALU.is_equal, ALU.add, accum_out=cnt2[:, 1:2])\
                .then_inc(counted, 1)
            dve.wait_ge(summed, 34)
            link(v.tensor_scalar(room[:, :], PG[:, 0:1], -1.0, float(CAP), ALU.mult, ALU.add))
            link(v.tensor_copy(offs[:, :], PE2[:, 1:2]))
            link(v.tensor_tensor_scan(ceq[:, :], ones[:, :], eq[:, :], offs[:, :], ALU.mult, ALU.add))
            link(v.scalar_tensor_tensor(hit[:, :], ceq[:, :], room[:, :], eq[:, :], ALU.is_le, ALU.mult))
            v.scalar_tensor_tensor(sel[:, :], hit[:, :], 0.0, gt[:, :], ALU.add, ALU.add, accum_out=cnt3[:, :])\
                .then_inc(counted, 1)
            dve.wait_ge(summed, 35)
            link(v.tensor_copy(offs3[:, :], PS[:, 0:1]))
            link(v.tensor_tensor_scan(cum[:, :], ones[:, :], sel[:, :], offs3[:, :], ALU.mult, ALU.add))
            v.tensor_copy(ends[:, :], cum[:, :].rearrange("p (t j) -> p t j", j=P)[:, :, P - 1]).then_inc(ends_ready, 1)
            dve.wait_ge(ends_in, 16)
            e_v = allends[:, :].rearrange("p (e g t) -> p e g t", e=E, g=1).broadcast_to([P, E, G, TILES])
            s_v = keep["slot"][:, :].rearrange("p (e g t) -> p e g t", e=1, t=1).broadcast_to([P, E, G, TILES])
            link(v.tensor_tensor(cmp[:, :, :, :], e_v, s_v, ALU.is_le))
            link(v.tensor_reduce(keep["tile"][:, 0:E * G], cmp[:, :, :, :].rearrange("p e g t -> p (e g) t"), AX.X, ALU.add))
            link(v.tensor_tensor(keep["cumrow"][:, 0:E * G], keep["tile"][:, 0:E * G], eoff[:, :], ALU.add))


C_ORDER = {
    ("pe", "front"): ["xt0", "xt1"],
    ("pe", "back"): [f"h{f}" for f in range(FT)] + [f"y{g}" for g in range(G)],
    ("act", "front"): ["xt0"],
    ("act", "back"): [f"h{f}" for f in range(FT)],
    ("dve", "find"): ["idx", "cmp", "pin", "tok", "all"],
    ("dve", "front"): ["xt1", "gate"],
    ("dve", "back"): ["add_idx"] + [s for g in range(G) for s in (f"yb{g}", f"c{g}", f"y{g}")],
    ("pool", "find"): ["cum"],
    ("pool", "front"): ["rows"],
    ("pool", "back"): ["add"],
}


def stage_c(nc, io, keep):
    with ExitStack() as ctx:
        def sb(name, shape, dt=F32):
            return ctx.enter_context(nc.sbuf_tensor(name, shape, dt))

        def sem(name):
            return ctx.enter_context(nc.semaphore(name))

        ident = sb("identc", [P, P])
        b1 = sb("b1", [P, E, FT])
        b2 = sb("b2", [P, C])
        w1 = sb("fw1", [P, HP, FF])
        w2 = sb("fw2", [P, FT, C])
        idx = sb("idx", [P, G], I32)
        crow = sb("crow", [P, G, P])
        cmp = sb("ccmp", [P, G, P])
        pin = sb("pin", [P, G])
        tok = sb("tok", [P, G], I32)
        tokall = sb("tokall", [P, (E + 2) * G], I32)
        tokadd = sb("tokadd", [P, G], I32)
        xg = sb("xg", [P, G, ROW])
        xgT = sb("xgT", [P, HP, CAP])
        gate = sb("gate", [P, G])
        hT = sb("hT", [P, FT, CAP])
        yb = sb("yb", [P, 2, C])
        yg = sb("yg", [P, G, ARow])
        XB = [ctx.enter_context(nc.psum_tensor(f"XB{i}", [P, 512], F32)) for i in range(2)]
        HB = [ctx.enter_context(nc.psum_tensor(f"HB{i}", [P, 512], F32)) for i in range(4)]
        YB = [ctx.enter_context(nc.psum_tensor(f"YB{i}", [P, 512], F32)) for i in range(2)]
        ident0, ready = sem("ident0"), sem("ready_c")
        yg_clear, b1_in = sem("yg_clear"), sem("b1_in")
        w1_in, w2_in, b2_in = sem("w1_in"), sem("w2_in"), sem("b2_in")
        crow_in, rows_in, added = sem("crow_in"), sem("rows_in"), sem("added")
        done = {key: sem("_".join(key) + "_c") for key in C_ORDER}
        counts = Counts(done, C_ORDER, {e: sem(f"{e}_turns_c") for e in ("pe", "act", "dve", "pool", "sp")})
        block = ctx.enter_context(nc.Block())

        @block.sync
        def _(sp):
            me = EngineSteps(sp, "sp", counts)
            sp.dma_start(b1[:, :, :], io["b1"]).then_inc(b1_in, 16)
            with sp.Fori(0, E) as e:
                me.need("pe", "back", f"h{FT-1}", e - 1)
                sp.dma_start(w1[:, :, :], io["fc1T"][bass.ds(e, 1), :, :].rearrange("o (a p) f -> (o p) a f", p=P))\
                    .then_inc(w1_in, 16)
                me.need("pe", "back", f"y{G-1}", e - 1)
                sp.dma_start(w2[:, :, :], io["fc2T"][bass.ds(e, 1), :, :].rearrange("o (j p) d -> (o p) j d", p=P))\
                    .then_inc(w2_in, 16)
                me.need("dve", "back", f"yb{G-1}", e - 1)
                sp.dma_start(b2[:, :], io["b2"][bass.ds(e, 1), :].broadcast_to([P, C])).then_inc(b2_in, 16)

        @block.gpsimd
        def _(pool):
            me = EngineSteps(pool, "pool", counts)
            g = nc.gpsimd
            me.credit("find", "front", "back")
            g.memset(ident[:, :], 0.0).then_inc(ident0, 1)
            pool.wait_ge(ident0, 1)
            g.affine_select(out=ident[:, :], in_=ident[:, :], compare_op=ALU.not_equal, fill=1.0, base=0,
                            pattern=[[-1, P]], channel_multiplier=1).then_inc(ready, 1)

            def find(e):
                me.need("dve", "find", "idx", e)
                me.need("dve", "find", "cmp", e - 1)
                for j in range(G):
                    g.indirect_dma_start(crow[:, j, :], None, io["cum"],
                                         bass.IndirectOffsetOnAxis(ap=idx[:, j:j + 1], axis=0)).then_inc(crow_in, 16)
                me.did(pool.wait_ge(crow_in, 16 * G * (e + 1)), "find", "cum")

            def front(e):
                me.need("dve", "find", "tok", e)
                me.need("dve", "front", "gate", e - 1)
                me.need("pe", "front", "xt1", e - 1)
                for j in range(G):
                    g.indirect_dma_start(xg[:, j, :], None, io["table"],
                                         bass.IndirectOffsetOnAxis(ap=tok[:, j:j + 1], axis=0)).then_inc(rows_in, 16)
                me.did(pool.wait_ge(rows_in, 16 * G * (e + 1)), "front", "rows")

            def back(e):
                for j in range(G):
                    me.need("dve", "back", f"y{j}", e)
                    g.indirect_dma_start(io["acc"], bass.IndirectOffsetOnAxis(ap=tokadd[:, j:j + 1], axis=0),
                                         yg[:, j, :], None, compute_op=ALU.add).then_inc(added, 16)
                me.did(pool.wait_ge(added, 16 * G * (e + 1)), "back", "add")

            find(0)
            front(0)
            find(1)
            with pool.Fori(0, E - 1) as e:
                front(e + 1)
                find(e + 2)
                back(e)
            back(E - 1)

        @block.scalar
        def _(act):
            me = EngineSteps(act, "act", counts)
            a = nc.scalar
            me.credit("front", "back")
            act.wait_ge(b1_in, 16)

            def front(e):
                me.need("pe", "front", "xt0", e)
                me.need("pe", "back", f"h{FT-1}", e - 1)
                me.did(a.activation(xgT[:, 0, :], XB[0][:, :], ACT.Copy), "front", "xt0")

            def back(e):
                me.need("pe", "back", f"y{G-1}", e - 1)
                for f in range(FT):
                    me.need("pe", "back", f"h{f}", e)
                    me.did(a.activation(hT[:, f, :], HB[f % 4][:, :], ACT.Gelu,
                                        bias=b1[:, bass.ds(e, 1), f:f + 1].rearrange("p o f -> p (o f)")),
                           "back", f"h{f}")

            front(0)
            with act.Fori(0, E - 1) as e:
                back(e)
                front(e + 1)
            back(E - 1)

        @block.vector
        def _(dve):
            me = EngineSteps(dve, "dve", counts)
            v = nc.vector
            me.credit("find", "front", "back")
            v.memset(yg[:, :, :], 0.0).then_inc(yg_clear, 1)
            dve.wait_ge(yg_clear, 1)
            slot = keep["slot"][:, :].rearrange("p (g o) -> p g o", o=1).broadcast_to([P, G, P])

            def index(e):
                me.need("pool", "find", "cum", e - 1)
                me.did(v.tensor_copy(idx[:, :], keep["cumrow"][:, bass.ds(e * G, G)]), "find", "idx")

            def find(e):
                me.need("pool", "find", "cum", e)
                me.did(v.tensor_tensor(cmp[:, :, :], crow[:, :, :], slot, ALU.is_le), "find", "cmp")
                me.need("dve", "find", "cmp", e)
                me.did(v.tensor_reduce(pin[:, :], cmp[:, :, :], AX.X, ALU.add), "find", "pin")
                me.need("dve", "find", "pin", e)
                me.need("pool", "front", "rows", e - 1)
                me.did(v.scalar_tensor_tensor(tok[:, :], keep["tile"][:, bass.ds(e * G, G)], float(P), pin[:, :],
                                              ALU.mult, ALU.add), "find", "tok")
                me.need("dve", "find", "tok", e)
                me.did(v.tensor_copy(tokall[:, bass.ds(e * G, G)], tok[:, :]), "find", "all")

            def turned(e):
                me.need("pe", "front", "xt1", e)
                me.need("pe", "back", f"h{FT-1}", e - 1)
                me.did(v.tensor_copy(xgT[:, 1, :], XB[1][:, :]), "front", "xt1")

            def gates(e):
                me.need("pool", "front", "rows", e)
                me.need("dve", "back", f"y{G-1}", e - 1)
                me.did(v.tensor_copy(gate[:, :], xg[:, :, bass.ds(e + C, 1)].rearrange("p g o -> p (g o)")),
                       "front", "gate")

            def back(e):
                me.need("pool", "back", "add", e - 1)
                me.did(v.tensor_copy(tokadd[:, :], tokall[:, bass.ds(e * G, G)]), "back", "add_idx")
                me.arrived(b2_in, 16 * (e + 1))
                me.need("dve", "front", "gate", e)
                for j in range(G):
                    if j >= 2:
                        me.need("dve", "back", f"y{j-2}", e)
                    me.need("pe", "back", f"y{j}", e)
                    me.did(v.tensor_tensor(yb[:, j % 2, :], YB[j % 2][:, 0:C], b2[:, :], ALU.add), "back", f"yb{j}")
                    me.did(v.tensor_copy(yg[:, j, C:C + 1], gate[:, j:j + 1]), "back", f"c{j}")
                    me.need("dve", "back", f"yb{j}", e)
                    me.did(v.tensor_scalar(yg[:, j, 0:C], yb[:, j % 2, :], gate[:, j:j + 1], None, ALU.mult),
                           "back", f"y{j}")

            index(0)
            find(0)
            index(1)
            find(1)
            turned(0)
            gates(0)
            index(2)
            with dve.Fori(0, E - 1) as e:
                find(e + 2)
                turned(e + 1)
                back(e)
                gates(e + 1)
                index(e + 3)
            back(E - 1)

        @block.tensor
        def _(pe):
            me = EngineSteps(pe, "pe", counts)
            mm = nc.tensor.matmul
            me.credit("front", "back")
            pe.wait_ge(ready, 1)

            def front(e):
                me.need("pool", "front", "rows", e)
                for hp in range(HP):
                    me.need("act" if hp == 0 else "dve", "front", f"xt{hp}", e - 1)
                    for j in range(G):
                        ins = nc.tensor.transpose(XB[hp][:, j * P:j * P + P], xg[:, j, hp * P:hp * P + P], ident[:, :])
                    me.did(ins, "front", f"xt{hp}")

            def up(e):
                me.arrived(w1_in, 16 * (e + 1))
                me.need("act", "front", "xt0", e)
                me.need("dve", "front", "xt1", e)
                for f in range(FT):
                    me.need("act", "back", f"h{(f-4) % FT}", e if f >= 4 else e - 1)
                    for a in range(HP):
                        ins = mm(HB[f % 4][:, :], w1[:, a, f * P:f * P + P], xgT[:, a, :], start=(a == 0),
                                 stop=(a == HP - 1))
                    me.did(ins, "back", f"h{f}")

            def down(e):
                me.arrived(w2_in, 16 * (e + 1))
                for j in range(G):
                    me.need("dve", "back", f"yb{(j-2) % G}", e if j >= 2 else e - 1)
                    for f in range(FT):
                        if j == 0:
                            me.need("act", "back", f"h{f}", e)
                        ins = mm(YB[j % 2][:, 0:C], hT[:, f, j * P:j * P + P], w2[:, f, :], start=(f == 0),
                                 stop=(f == FT - 1))
                    me.did(ins, "back", f"y{j}")

            front(0)
            with pe.Fori(0, E - 1) as e:
                up(e)
                front(e + 1)
                down(e)
            up(E - 1)
            down(E - 1)


D_SP, D_POOL = ["in"], ["rstd"]
D_DVE = ["den", "rec"] + [s for c in range(CH) for s in (f"x{c}", f"st{c}", f"mv{c}")] + ["ve", "nm"]
D_ACT = [f"o{c}" for c in range(CH)]


def stage_d(nc, io, keep):
    with ExitStack() as ctx:
        def sb(name, shape, dt=F32):
            return ctx.enter_context(nc.sbuf_tensor(name, shape, dt))

        def sem(name):
            return ctx.enter_context(nc.semaphore(name))

        BUF = 2
        acc = sb("accb", [P, BUF, CH, ARow])
        o = sb("ob", [P, BUF, CH, C])
        x3 = sb("x3", [P, BUF, CH, C])
        neghalf = sb("neghalf_d", [P, CH])
        small = {k: sb(k + "_d", [P, BUF, CH]) for k in ("den", "rec", "ve", "rstd", "nm")}
        st = sb("st_d", [P, BUF, CH, 6])
        mv = sb("mv_d", [P, BUF, CH, 2])
        half_ready = sem("half_ready")
        acc_in, out_done = [sem(f"acc_in{b}") for b in range(BUF)], [sem(f"out_done{b}") for b in range(BUF)]
        engines = ("act", "dve", "pool")
        parts = [f"b{b}" for b in range(BUF)]
        done = {(e, p): sem(f"{e}_{p}_d") for e in engines + ("sp",) for p in parts}
        order = {(e, p): s for e, s in (("act", D_ACT), ("dve", D_DVE), ("pool", D_POOL), ("sp", D_SP)) for p in parts}
        counts = Counts(done, order, {e: sem(f"{e}_turns_d") for e in engines + ("sp",)})
        block = ctx.enter_context(nc.Block())

        def rows(b, n):
            return bass.ds((n * BUF + b) * T, T)

        @block.sync
        def _(sp):
            me = EngineSteps(sp, "sp", counts)
            with sp.Fori(0, NB // BUF) as n:
                for b in range(BUF):
                    me.need("dve", f"b{b}", f"x{CH-1}", n - 1)
                    sp.dma_start(acc[:, b, :, :], io["acc"][rows(b, n), :].rearrange("(c p) d -> p c d", p=P))\
                        .then_inc(acc_in[b], 16)

        @block.gpsimd
        def _(pool):
            me = EngineSteps(pool, "pool", counts)
            g = nc.gpsimd
            me.credit(*parts)
            g.memset(neghalf[:, :], -0.5).then_inc(half_ready, 1)
            pool.wait_ge(half_ready, 1)
            with pool.Fori(0, NB // BUF) as n:
                for b in range(BUF):
                    me.need("dve", f"b{b}", "ve", n)
                    me.did(g.tensor_tensor(small["rstd"][:, b, :], small["ve"][:, b, :], neghalf[:, :], ALU.pow),
                           f"b{b}", "rstd")

        @block.vector
        def _(dve):
            me = EngineSteps(dve, "dve", counts)
            v = nc.vector
            me.credit(*parts)
            with dve.Fori(0, NB // BUF) as n:
                for b in range(BUF):
                    p = f"b{b}"
                    me.arrived(acc_in[b], 16 * (n + 1))
                    gs = acc[:, b, :, C]
                    me.did(v.scalar_tensor_tensor(small["den"][:, b, :], gs, 0.0, gs, ALU.is_le, ALU.add), p, "den")
                    me.need("dve", p, "den", n)
                    me.did(v.reciprocal(small["rec"][:, b, :], small["den"][:, b, :]), p, "rec")
                    me.need("dve", p, "rec", n)
                    me.need("act", p, f"o{CH-1}", n - 1)
                    for c in range(CH):
                        x2c = keep["x2all"][:, bass.ds((n * BUF + b) * CH + c, 1), :].rearrange("p o d -> p (o d)")
                        me.did(v.scalar_tensor_tensor(x3[:, b, c, :], acc[:, b, c, 0:C], small["rec"][:, b, c:c + 1],
                                                      x2c, ALU.mult, ALU.add), p, f"x{c}")
                        me.need("dve", p, f"x{c}", n)
                        me.did(v.bn_stats(st[:, b, c, :], x3[:, b, c, :]), p, f"st{c}")
                        me.need("dve", p, f"st{c}", n)
                        me.did(v.bn_aggr(mv[:, b, c, :], st[:, b, c, :]), p, f"mv{c}")
                    me.need("dve", p, f"mv{CH-1}", n)
                    me.did(v.tensor_scalar(small["ve"][:, b, :], mv[:, b, :, 1], LN_EPS, None, ALU.add), p, "ve")
                    me.need("pool", p, "rstd", n)
                    me.did(v.scalar_tensor_tensor(small["nm"][:, b, :], mv[:, b, :, 0], -1.0, small["rstd"][:, b, :],
                                                  ALU.mult, ALU.mult), p, "nm")

        @block.scalar
        def _(act):
            me = EngineSteps(act, "act", counts)
            a = nc.scalar
            me.credit(*parts)
            for b in range(BUF):
                act.sem_inc(done[("sp", f"b{b}")], 1)
            with act.Fori(0, NB // BUF) as n:
                for b in range(BUF):
                    p = f"b{b}"
                    me.need("dve", p, "nm", n)
                    me.need("sp", p, "in", n - 1)
                    for c in range(CH):
                        me.did(a.activation(o[:, b, c, :], x3[:, b, c, :], ACT.Identity, bias=small["nm"][:, b, c:c + 1],
                                            scale=small["rstd"][:, b, c:c + 1]), p, f"o{c}")
                    me.need("act", p, f"o{CH-1}", n)
                    act.dma_start(io["out"][rows(b, n), :].rearrange("(c p) d -> p c d", p=P), o[:, b, :, :])\
                        .then_inc(out_done[b], 16)
                    act.wait_ge(out_done[b], 16 * (n + 1)).then_inc(done[("sp", p)], 1)


def build(nc, io):
    with ExitStack() as ctx:
        keep = {"x2all": ctx.enter_context(nc.sbuf_tensor("x2all", [P, TILES, C], F32)),
                "slot": ctx.enter_context(nc.sbuf_tensor("slot", [P, G], F32)),
                "tile": ctx.enter_context(nc.sbuf_tensor("tile", [P, (E + 2) * G], F32)),
                "cumrow": ctx.enter_context(nc.sbuf_tensor("cumrow", [P, (E + 2) * G], F32))}
        stage_a(nc, io, keep)
        stage_b(nc, io, keep)
        stage_c(nc, io, keep)
        stage_d(nc, io, keep)


def kernel(**inputs):
    import numpy as np
    import concourse.bacc as bacc
    from concourse.bass_utils import run_bass_kernel_spmd as run

    g = {k: np.asarray(v) for k, v in inputs.items()}
    A = "L0_attn_"
    x = g[A + "x"].reshape(NT, C)
    cols = np.stack([g[A + k].reshape(HP, P) for k in
                     ("maa_x", "maa_w", "maa_k", "maa_v", "maa_r", "maa_g", "time_decay", "u")])
    F = "L0_ffn_"
    arrays = {
        "x": x, "xT": x.T,
        "cols": cols.reshape(16, P).T,
        "rows": np.concatenate([g[A + "ln_g"], g[A + "ln_b"], g[F + "norm_weight"], g[F + "router_bias"]])[None],
        "maa_w1": g[A + "maa_w1"], "maa_w2": g[A + "maa_w2"].reshape(160, C),
        "Wr": g[A + "Wr"], "Wk": g[A + "Wk"], "Wv": g[A + "Wv"], "Wo": g[A + "Wo"],
        "decay_w1": g[A + "decay_w1"], "decay_w2": g[A + "decay_w2"],
        "gate_w1": g[A + "gate_w1"], "gate_w2": g[A + "gate_w2"],
        "rwT": g[F + "router_weight"].T,
        "fc1T": g[F + "fc1_weight"].transpose(0, 2, 1), "fc2T": g[F + "fc2_weight"].transpose(0, 2, 1),
        "b1": g[F + "fc1_bias"].reshape(E, FT, P).transpose(2, 0, 1), "b2": g[F + "fc2_bias"],
    }
    arrays = {f"in_{k}": np.ascontiguousarray(v) for k, v in arrays.items()}
    nc = bacc.Bacc("TRN2", target_bir_lowering=False, num_devices=1)
    io = {k[3:]: nc.dram_tensor(k, v.shape, mybir.dt.from_np(v.dtype), kind="ExternalInput").ap()
          for k, v in arrays.items()}
    io["out"] = nc.dram_tensor("out_dram", (NT, C), F32, kind="ExternalOutput").ap()
    for name, shape in (("table", (NT, ROW)), ("logitsT", (E, NT)), ("ends", (1, E * TILES)),
                        ("cum", (E * TILES, P)), ("acc", (NT, ARow))):
        io[name] = nc.dram_tensor(f"tmp_{name}", shape, F32, kind="Internal").ap()
    build(nc, io)
    r = run(nc, [arrays], core_ids=[0])
    return r.results[0]["out_dram"].reshape(NB, T, C)
```

```python
import concourse.bass as bass
from concourse import mybir
from contextlib import ExitStack

F32 = mybir.dt.float32
F32R = mybir.dt.float32r
I32 = mybir.dt.int32
U32 = mybir.dt.uint32
ALU = mybir.AluOpType
ACT = mybir.ActivationFunctionType
AX = mybir.AxisListType

P = 128
NB, T, C = 16, 512, 256
H, N = 4, 64
HP = C // P
CH = T // P
NT = NB * T
E = 16
TILES = NT // P
ROW = C + E
ARow = C + 4
CAP = NT // E
SEG = P // E
ST = NT // SEG
FF = 1024
FT = FF // P
G = CAP // P
MIXES = ("w", "k", "v", "r", "g")
LEVELS = (1, 2, 4, 8, 16, 32, 64)
LN_EPS = 1e-5
GN_EPS = 0.00064
RMS_EPS = 1e-5

PE_FRONT = ["lora_a", "lora_b", "m_w0", "m_w1", "m_k0", "m_k1", "dec1", "m_v0", "m_v1", "k0", "k1",
            "m_r0", "m_r1", "dec0", "dec2", "m_g0", "m_g1", "r0", "r1", "d", "l1", "gate1", "v0", "v1"]
FRONT_JOBS = [j for j in PE_FRONT if j != "l1"]
ACT_FRONT = ["lora_a", "lora_ah", "lora_b", "lora_bh", "dec1", "k0", "k1", "dec0e", "dec0", "dec2e", "dec2", "r0", "r1", "gate1",
             "k2", "r2", "v0", "v1"]
DVE_PRE = ["xx", "xxx0", "xxx1"]
DVE_FRONT = ["lora_al", "lora_bl"] + [f"m_{f}{h}" for f in MIXES for h in range(HP)] + ["ruk0", "ruk1", "d", "a1", "r2", "w2"]
POOL_FRONT = [f"x{f}" for f in MIXES] + ["k2"]
FRONT_READER = {j: ("dve", j) if j.startswith("m_") or j == "d" else ("act", j + "e" * (j in ("dec0", "dec2")) +
                                                           "h" * j.startswith("lora")) for j in FRONT_JOBS}

PE_BACK = ["l2", "l4", "l8", "g0", "g1"] + [f"l{b}" for b in LEVELS[4:]] + ["kt0", "kt1", "u0", "u1", "y0", "y1"]
BACK_JOBS = ["g0", "g1", "kt0", "kt1", "u0", "u1", "y0", "y1"]
BACK_READER = {"g0": ("act", "g0"), "g1": ("act", "g1"), "kt0": ("act", "kt0"),
               "kt1": ("act", "kt1"), "u0": ("dve", "s1b"), "u1": ("dve", "s2b"), "y0": ("dve", "y1", "tail"),
               "y1": ("dve", "y3", "tail")}
ACT_BACK = ["g0", "g1"] + [f"at{q}" for q in range(4)] + ["at32a", "at32b", "at64", "kt0", "kt1"]
DVE_BACK = ([s for b in LEVELS[1:5] for s in (f"r{2*b}", f"w{2*b}", f"a{b}")]
            + [s for b in LEVELS[5:] for s in (f"r{2*b}", f"w{2*b}")]
            + ["s0", "s0b", "s1", "s1b", "s2", "s2b"])
POOL_BACK = [f"k{2*b}" for b in LEVELS[1:]]

PE_TAIL = ["zt0", "o0", "zt1", "o1", "xt0", "xt1", "lg", "lt"]
TAIL_READER = {"zt0": ("act", "zt0"), "o0": ("dve", "o1"), "zt1": ("act", "zt1"), "o1": ("dve", "o3"),
               "xt0": ("act", "xt0"), "xt1": ("act", "xt1"), "lg": ("dve", "lg"), "lt": ("act", "lt")}
ACT_TAIL = ["zt0", "zt1", "xt0", "xt1", "exp", "lt"]
DVE_TAIL = ([s for c in (0, 2) for s in (f"ysum{c}", f"ysum{c+1}", f"y{c}", f"y{c+1}", f"sq{c}", f"sq{c+1}",
                                         f"ssq{c}", f"ssq{c+1}", f"yv{c}")]
            + [s for c in (0, 2) for s in (f"zr{c}", f"zr{c+1}", f"zg{c}", f"zg{c+1}")]
            + [s for c in (0, 2) for s in (f"o{c}", f"o{c+1}", f"st{c}", f"st{c+1}", f"mv{c}", f"mv{c+1}")]
            + ["ve", "q1", "q2", "q3"] + [f"x2_{c}" for c in range(CH)] + [f"xn{c}" for c in range(CH)]
            + ["lg", "lmax", "lsub", "lsum", "lrec", "probs"])
POOL_TAIL = ["yr0", "yr2"] + [s for c in (0, 2) for s in (f"zb{c}", f"zb{c+1}", f"z{c}", f"z{c+1}")] + ["rstd", "rn", "x2all"]
PARTS = ("front", "back", "tail")

TURNS = {
    "pe": "BFBT BTFF BTTB FFBF BTFF BTFF TBFB FFTF",
    "act": "FTTF BBBF TBFB TFTF FFT",
    "dve": "TTBT FBTF TBFT BFTB TBFF FBTT PFF",
    "pool": "TBTT BBTF BTFT FBBF FFT",
}


def take_turns(pattern, **pieces):
    for turn in pattern.replace(" ", ""):
        if pieces.get(turn):
            next(pieces[turn])
    for turn, part in pieces.items():
        assert not part or next(part, "end") == "end", f"{turn} has pieces left"


def rounds(eng, pattern, front, back, tail, pre=None):
    pre = pre or (lambda n: None)

    def alone(part):
        for _ in part or ():
            pass

    alone(pre(0))
    alone(front(0))
    alone(pre(1))
    take_turns(pattern, F=front(1), B=back(0), P=pre(2))
    with eng.Fori(1, NB - 2) as n:
        take_turns(pattern, F=front(n + 1), B=back(n), T=tail(n - 1), P=pre(n + 2))
    take_turns(pattern, F=front(NB - 1), B=back(NB - 2), T=tail(NB - 3))
    take_turns(pattern, B=back(NB - 1), T=tail(NB - 2))
    alone(tail(NB - 1))


class Counts:

    def __init__(self, done, order, turns):
        self.done, self.order, self.turns = done, order, turns
        self.at = {key: 0 for key in order}


class EngineSteps:

    def __init__(self, eng, name, counts):
        self.eng, self.name, self.c = eng, name, counts

    def did(self, ins, part, step):
        key = (self.name, part)
        steps = self.c.order[key]
        assert steps[self.c.at[key] % len(steps)] == step, (key, step, steps[self.c.at[key] % len(steps)])
        self.c.at[key] += 1
        ins.then_inc(self.c.done[key], 1)

    def need(self, who, part, step, n):
        steps = self.c.order[(who, part)]
        self.eng.wait_ge(self.c.done[(who, part)], (n + 1) * len(steps) + steps.index(step) + 1)\
            .then_inc(self.c.turns[self.name], 1)

    def arrived(self, dma_sem, value):
        self.eng.wait_ge(dma_sem, value).then_inc(self.c.turns[self.name], 1)

    def credit(self, *parts):
        for part in parts:
            self.eng.sem_inc(self.c.done[(self.name, part)], len(self.c.order[(self.name, part)]))


def stage_a(nc, io, keep):
    with ExitStack() as ctx:
        def sb(name, shape, dt=F32):
            return ctx.enter_context(nc.sbuf_tensor(name, shape, dt))

        def sem(name):
            return ctx.enter_context(nc.semaphore(name))

        cols = sb("cols", [P, 16])
        rows = sb("rows", [P, 3 * C + E])
        w1 = sb("w1", [P, HP, 2 * P])
        w2s = sb("w2s", [P, 5, C], F32R)
        Wp = {n: sb(f"W{n}", [P, HP, C]) for n in "rkvo"}
        W1 = {n: sb(f"W1{n}", [P, HP, 64]) for n in "wg"}
        W2 = {n: sb(f"W2{n}", [64, C]) for n in "wg"}
        rwT = sb("rwT", [P, HP, E])
        ident = sb("ident", [P, P])
        pairones = sb("pairones", [P, 2])
        masks = sb("masks", [P, 6, 32], I32)
        neghalf = sb("neghalf", [P, 2, H])

        def col(n, hp):
            return cols[:, 2 * n + hp:2 * n + hp + 1]

        MAA = {"x": 0, "w": 1, "k": 2, "v": 3, "r": 4, "g": 5}
        lng, lnb, nwb = rows[:, 0:C], rows[:, C:2 * C], rows[:, 2 * C:3 * C]
        rb = rows[:, 3 * C:3 * C + E]

        xT = sb("xT", [P, HP, T + 1])
        xx = sb("xx", [P, HP, T])
        xxx = sb("xxx", [P, HP, T])
        mixbuf = [sb(f"mix{i}", [P, HP, T]) for i in range(3)]
        mix = {f: mixbuf[i % 3] for i, f in enumerate(MIXES)}
        lora = sb("lora", [P, T])
        lorag = sb("lorag", [P, T])
        lora_h, lora_l = sb("lora_h", [P, T], F32R), sb("lora_l", [P, T], F32R)
        loras = sb("loras", [P, 5, T], F32R)
        dec1 = sb("dec1", [64, T])
        dece = sb("dece", [P, T])
        gate1 = sb("gate1", [64, T])
        rn_ = sb("r_next", [P, HP, T])
        kn_ = sb("k_next", [P, HP, T])
        wn_ = sb("w_next", [P, HP, T])
        vn_ = sb("v_tok", [P, CH, C])
        gn_ = sb("g_tok", [P, CH, C])
        ruk = sb("ruk", [P, HP, T])
        maskf = ruk[:, :, :].rearrange("p h t -> p (h t)")[:, 0:6 * 32].rearrange("p (l t) -> p l t", l=6)
        R = sb("R", [P, HP, T])
        K = sb("K", [P, HP, T])
        W = {1: wn_}
        for b in LEVELS:
            W[2 * b] = sb(f"Wl{2*b}", [P, HP, T // (2 * b)])
        Ad = sb("Ad", [P, 2, CH * HP, 32])
        At = sb("At", [P, 2, CH * HP, P])
        w2 = At[:, :, :, :].rearrange("p a j t -> p (a j t)")[:, 0:5 * C].rearrange("p (f n) -> p f n", f=5)
        KT = sb("KT", [P, CH - 1, C])
        S = sb("S", [P, CH - 1, HP, P])
        yc = sb("yc", [P, CH, C])
        ysq = sb("ysq", [P, 2, C])
        ysum = sb("ysum", [P, CH, H])
        yssq = sb("yssq", [P, CH, H])
        yvar = sb("yvar", [P, CH, H])
        yrs = sb("yrs", [P, CH, H])
        z = yc
        zT = sb("zT", [P, CH, HP, P])
        xtok = sb("xtok", [P, CH, C])
        x2 = x1 = xtok
        st = sb("st", [P, CH, 6])
        mv = sb("mv", [P, CH, 2])
        ve = sb("ve", [P, CH])
        rstd = sb("rstd", [P, CH])
        q1 = sb("q1", [P, CH])
        q2 = sb("q2", [P, CH])
        q3 = sb("q3", [P, CH])
        rn = sb("rn", [P, CH])
        table = sb("table", [P, CH, ROW])
        xnT = zT
        lg = sb("lg", [P, CH, E])
        lsub = sb("lsub", [P, CH, E])
        lexp = sb("lexp", [P, CH, E])
        lmax = sb("lmax", [P, CH])
        lsum = sb("lsum", [P, CH])
        lrec = sb("lrec", [P, CH])
        lt = sb("lt", [CH * E, P])

        LV = ctx.enter_context(nc.psum_tensor("LV", [P, 2, 512], F32))
        FB = [ctx.enter_context(nc.psum_tensor(f"FB{i}", [P, 512], F32)) for i in range(3)]
        BB = [ctx.enter_context(nc.psum_tensor(f"BB{i}", [P, 512], F32)) for i in range(2)]
        TB = ctx.enter_context(nc.psum_tensor("TB", [P, 512], F32))

        FIRST, CONSTS = 6, 14
        first_in, consts_in = sem("first_in"), sem("consts_in")
        setup_pool, setup_pool2 = sem("setup_pool"), sem("setup_pool2")
        masks_ready = sem("masks_ready")
        zeros_ready = sem("zeros_ready")
        xT_in, xtok_in = sem("xT_in"), sem("xtok_in")
        w2_split = sem("w2_split")
        stack_in = [sem(f"stack_in_{f}") for f in MIXES[:4]]
        table_out, logits_out = sem("table_out"), sem("logits_out")
        order = {("pe", "front"): PE_FRONT, ("act", "front"): ACT_FRONT, ("dve", "front"): DVE_FRONT,
                 ("pool", "front"): POOL_FRONT, ("pe", "back"): PE_BACK, ("act", "back"): ACT_BACK,
                 ("dve", "back"): DVE_BACK, ("pool", "back"): POOL_BACK, ("pe", "tail"): PE_TAIL,
                 ("act", "tail"): ACT_TAIL, ("dve", "tail"): DVE_TAIL, ("pool", "tail"): POOL_TAIL,
                 ("sp", "tail"): ["table", "logits"], ("dve", "pre"): DVE_PRE}
        done = {key: sem("_".join(key)) for key in order}
        turns = {e: sem(f"{e}_turns") for e in ("pe", "act", "dve", "pool", "sp")}
        counts = Counts(done, order, turns)

        def Steps(eng, name):
            return EngineSteps(eng, name, counts)

        def ring(me, part, banks, jobs, reader, job, n):
            j = jobs.index(job)
            old = jobs[j - len(banks)] if j >= len(banks) else [o for i, o in enumerate(jobs)
                                                                 if i % len(banks) == j][-1]
            who, step, part = (*reader[old], part)[0:3]
            me.need(who, part, step, n if j >= len(banks) else n - 1)
            return banks[j % len(banks)]

        block = ctx.enter_context(nc.Block())

        @block.sync
        def _(sp):
            me = Steps(sp, "sp")
            xT_dram = io["xT"].rearrange("(a p) n -> p a n", p=P)
            me.credit("tail")

            def load_xT(n):
                me.need("pool", "front", "xg", n - 1)
                sp.dma_start(xT[:, :, 1:T + 1], xT_dram[:, :, bass.ds(n * T, T)]).then_inc(xT_in, 16)

            load_xT(0)
            sp.dma_start(cols[:, :], io["cols"]).then_inc(first_in, 16)
            w1_dram = io["maa_w1"].rearrange("(a p) n -> p a n", p=P)
            sp.dma_start(w1[:, :, 0:P], w1_dram[:, :, 0:P]).then_inc(first_in, 16)
            for q in range(4):
                sp.dma_start(w1[:, :, P + 32 * q:P + 32 * q + 32], w1_dram[:, :, P:P + 32]).then_inc(first_in, 16)
            sp.dma_start(rows[:, :], io["rows"].broadcast_to([P, 3 * C + E])).then_inc(consts_in, 16)
            for q in range(4):
                sp.dma_start(w2[32 * q:32 * q + 32, :, :], io["maa_w2"].rearrange("(f p) n -> p f n", p=32))\
                    .then_inc(consts_in, 16)
            for n in "rkvo":
                sp.dma_start(Wp[n][:, :, :], io[f"W{n}"].rearrange("(a p) n -> p a n", p=P)).then_inc(consts_in, 16)
            for n, name in (("w", "decay"), ("g", "gate")):
                sp.dma_start(W1[n][:, :, :], io[f"{name}_w1"].rearrange("(a p) n -> p a n", p=P)).then_inc(consts_in, 16)
                sp.dma_start(W2[n][:, :], io[f"{name}_w2"]).then_inc(consts_in, 16)
            sp.dma_start(rwT[:, :, :], io["rwT"].rearrange("(a p) n -> p a n", p=P)).then_inc(consts_in, 16)
            def load_xtok(n):
                me.need("dve", "tail", "xn3", n - 1)
                me.need("pool", "tail", "x2all", n - 1)
                sp.dma_start(xtok[:, :, :], io["x"][bass.ds(n * T, T), :].rearrange("(c p) d -> p c d", p=P))\
                    .then_inc(xtok_in, 16)

            def store(n):
                me.need("dve", "tail", "probs", n)
                sp.dma_start(io["table"][bass.ds(n * T, T), :].rearrange("(c p) d -> p c d", p=P), table[:, :, :])\
                    .then_inc(table_out, 16)
                me.need("act", "tail", "lt", n)
                for c in range(CH):
                    sp.dma_start(io["logitsT"][:, bass.ds(n * T + c * P, P)], lt[c * E:(c + 1) * E, :])\
                        .then_inc(logits_out, 16)
                me.did(sp.wait_ge(table_out, 16 * (n + 1)), "tail", "table")
                me.did(sp.wait_ge(logits_out, 16 * CH * (n + 1)), "tail", "logits")

            def stack(n):
                me.need("pe", "front", "m_g1", n - 1)
                me.need("act", "front", "lora_ah", n)
                me.need("dve", "front", "lora_al", n)
                for i in range(4):
                    for q, part in enumerate((lora_h, lora_h, lora_l, lora_l)):
                        sp.dma_start(loras[32 * q:32 * q + 32, i, :].bitcast(F32), part[32 * i:32 * i + 32, :].bitcast(F32))\
                            .then_inc(stack_in[i], 16)

            load_xtok(0)
            stack(0)
            load_xT(1)
            stack(1)
            load_xT(2)
            with sp.Fori(1, NB - 2) as n:
                stack(n + 1)
                load_xtok(n)
                load_xT(n + 2)
                store(n - 1)
            stack(NB - 1)
            for n in (NB - 2, NB - 1):
                load_xtok(n)
                store(n - 1)
            store(NB - 1)

        @block.gpsimd
        def _(pool):
            me = Steps(pool, "pool")
            g = nc.gpsimd
            me.credit(*PARTS)
            g.memset(ident[:, :], 0.0).then_inc(setup_pool, 1)
            g.memset(neghalf[:, :, :], -0.5).then_inc(setup_pool, 1)
            g.memset(pairones[:, :], 1.0).then_inc(setup_pool, 1)
            g.memset(maskf[:, :, :], 1.0).then_inc(setup_pool, 1)
            pool.wait_ge(setup_pool, 4)
            g.affine_select(out=ident[:, :], in_=ident[:, :], compare_op=ALU.not_equal, fill=1.0, base=0,
                            pattern=[[-1, P]], channel_multiplier=1).then_inc(setup_pool2, 1)
            g.affine_select(out=pairones[:, 0:1], in_=pairones[:, 0:1], compare_op=ALU.is_gt, fill=0.0,
                            base=N, pattern=[[0, 1]], channel_multiplier=-1).then_inc(setup_pool2, 1)
            g.affine_select(out=pairones[:, 1:2], in_=pairones[:, 1:2], compare_op=ALU.is_ge, fill=0.0,
                            base=-N, pattern=[[0, 1]], channel_multiplier=1).then_inc(setup_pool2, 1)
            k = 3
            for q in range(4):
                for li, b in enumerate(LEVELS[:5]):
                    blk = maskf[32 * q:32 * q + 32, li, :].rearrange("p (m o t) -> p m o t", o=2, t=b)
                    k += 1
                    g.memset(blk[:, :, 0, :], 0.0).then_inc(setup_pool2, 1)
                    odd = blk[:, :, 1, :]
                    pat = [[-2 * b, 32 // (2 * b)], [0, b]]
                    k += 1
                    g.affine_select(out=odd, in_=odd, compare_op=ALU.is_ge, fill=0.0, base=0, pattern=pat,
                                    channel_multiplier=1).then_inc(setup_pool2, 1)
                    pool.wait_ge(setup_pool2, k)
                    k += 1
                    g.affine_select(out=odd, in_=odd, compare_op=ALU.is_gt, fill=0.0, base=b,
                                    pattern=[[2 * b, 32 // (2 * b)], [0, b]],
                                    channel_multiplier=-1).then_inc(setup_pool2, 1)
                dq = maskf[32 * q:32 * q + 32, 5, :]
                k += 1
                g.affine_select(out=dq, in_=dq, compare_op=ALU.is_equal, fill=0.0, base=0, pattern=[[-1, 32]],
                                channel_multiplier=1).then_inc(setup_pool2, 1)
            pool.wait_ge(setup_pool2, k)
            g.tensor_copy(masks[:, :, :], maskf[:, :, :]).then_inc(masks_ready, 1)
            pool.wait_ge(consts_in, 16 * CONSTS)
            pool.wait_ge(zeros_ready, 4)

            def front(n):
                for f in MIXES:
                    me.need("dve", "front", f"m_{f}1", n)
                    if f == "w":
                        me.arrived(xT_in, 16 * (n + 1))
                    me.did(g.tensor_tensor(mix[f][:, :, :], mix[f][:, :, :], xT[:, :, 1:T + 1], ALU.add),
                           "front", f"x{f}")
                    yield
                me.need("act", "front", "dec2", n)
                me.need("pe", "back", "kt1", n - 1)
                k_up(1, kn_, "front")
                yield

            def k_up(b, src, part):
                kv = K[:, :, :].rearrange("p h (m o t) -> p (h m) o t", o=2, t=b)
                sv = src[:, :, :].rearrange("p h (m o t) -> p (h m) o t", o=2, t=b)
                wv = W[b][:, :, :].rearrange("p h (m o) -> p (h m) o", o=2)
                m = HP * T // (2 * b)
                me.did(g.tensor_tensor(kv[:, :, 0, :], sv[:, :, 0, :], wv[:, :, 1:2].broadcast_to([P, m, b]),
                                       ALU.mult), part, f"k{2*b}")

            def back(n):
                for b in LEVELS[1:]:
                    me.need("pe", "back", f"l{b}", n)
                    me.need("dve", "front" if b == 2 else "back", f"w{b}", n)
                    if b == 2:
                        me.need("act", "front", "k2", n)
                    me.need("pool", "front" if b == 2 else "back", f"k{b}", n)
                    k_up(b, K, "back")
                    yield

            def tail(n):
                for c in (0, 2):
                    me.need("dve", "tail", f"yv{c}", n)
                    me.did(g.tensor_tensor(yrs[:, c:c + 2, :], yvar[:, c:c + 2, :], neghalf[:, :, :], ALU.pow),
                           "tail", f"yr{c}")
                    yield
                for c2 in (0, 2):
                    pair = (c2, c2 + 1)
                    for c in pair:
                        me.need("dve", "tail", f"zg{c}", n)
                        me.did(g.tensor_tensor(z[:, c, :], z[:, c, :], lnb, ALU.add), "tail", f"zb{c}")
                    me.need("act", "back", f"g{c2//2}", n)
                    for c in pair:
                        me.need("pool", "tail", f"zb{c}", n)
                        me.did(g.tensor_tensor(z[:, c, :], z[:, c, :], gn_[:, c, :], ALU.mult), "tail", f"z{c}")
                    yield
                nh = neghalf[:, :, :].rearrange("p a b -> p (a b)")[:, 0:CH]
                me.need("dve", "tail", "ve", n)
                me.did(g.tensor_tensor(rstd[:, :], ve[:, :], nh, ALU.pow), "tail", "rstd")
                yield
                me.need("dve", "tail", "q3", n)
                me.did(g.tensor_tensor(rn[:, :], q3[:, :], nh, ALU.pow), "tail", "rn")
                yield
                me.need("dve", "tail", "x2_3", n)
                me.did(g.tensor_copy(keep["x2all"][:, bass.ds(n * CH, CH), :], x2[:, :, :]), "tail", "x2all")
                yield

            rounds(pool, TURNS["pool"], front, back, tail)

        @block.scalar
        def _(act):
            me = Steps(act, "act")
            a = nc.scalar
            me.credit(*PARTS)

            def front(n):
                def take(job, out, rows_=P, func=ACT.Copy, step=None, **kw):
                    me.need("pe", "front", job, n)
                    me.did(a.activation(out, FB[FRONT_JOBS.index(job) % 3][0:rows_, :], func, **kw), "front",
                           step or job)

                me.need("pe", "front", "m_g1", n - 1)
                take("lora_a", lora[:, :], func=ACT.Tanh)
                take("lora_a", lora_h[:, :], func=ACT.Tanh, step="lora_ah")
                take("lora_b", lorag[:, :], func=ACT.Tanh)
                take("lora_b", loras[:, 4, :], func=ACT.Tanh, step="lora_bh")
                if isinstance(n, int) and n == 0:
                    act.wait_ge(consts_in, 16 * CONSTS)
                    act.wait_ge(zeros_ready, 4)
                yield
                take("dec1", dec1[:, :], 64, ACT.Tanh)
                yield
                me.need("pool", "front", "k2", n - 1)
                me.need("act", "front", "r2", n - 1)
                me.need("dve", "front", "w2", n - 1)
                me.need("pe", "front", "l1", n - 1)
                for hp in range(HP):
                    take(f"k{hp}", kn_[:, hp, :])
                yield
                for hp, job in ((0, "dec0"), (1, "dec2")):
                    if hp:
                        me.need("act", "front", "dec0", n)
                    take(job, dece[:, :], func=ACT.Exp, step=job + "e", bias=col(6, hp))
                    me.need("act", "front", job + "e", n)
                    me.did(a.activation(wn_[:, hp, :], dece[:, :], ACT.Exp, scale=-1.0), "front", job)
                yield
                for hp in range(HP):
                    take(f"r{hp}", rn_[:, hp, :])
                yield
                me.need("pe", "back", "g1", n - 1)
                take("gate1", gate1[:, :], 64, ACT.Tanh)
                yield
                pair = "p h (m o) -> p (h m) o"
                me.need("pe", "back", "y1", n - 1)
                me.need("act", "front", "r1", n)
                me.did(a.activation(K[:, :, :].rearrange(pair, o=2)[:, :, 1:2],
                                    kn_[:, :, :].rearrange(pair, o=2)[:, :, 1:2], ACT.Copy), "front", "k2")
                me.did(a.activation(R[:, :, :].rearrange(pair, o=2)[:, :, 0:1],
                                    rn_[:, :, :].rearrange(pair, o=2)[:, :, 0:1], ACT.Copy), "front", "r2")
                yield
                me.need("pe", "back", "y1", n - 1)
                for j in range(2):
                    take(f"v{j}", vn_[:, 2 * j:2 * j + 2, :].rearrange("p c d -> p (c d)"))
                yield

            def back(n):
                def bank(job):
                    me.need("pe", "back", job, n)
                    return BB[BACK_JOBS.index(job) % 2]

                me.need("pool", "tail", "z3", n - 1)
                for j in range(2):
                    me.did(a.activation(gn_[:, 2 * j:2 * j + 2, :].rearrange("p c d -> p (c d)"),
                                        bank(f"g{j}")[:, :], ACT.Copy), "back", f"g{j}")
                yield
                me.need("dve", "back", "a16", n)
                for q in range(4):
                    s = slice(32 * q, 32 * q + 32)
                    me.did(a.activation(At[s, :, :, s], Ad[s, :, :, :], ACT.Copy), "back", f"at{q}")
                yield
                me.need("pe", "back", "l32", n)
                for name, lo in (("at32a", 0), ("at32b", 64)):
                    me.did(a.activation(At[lo:lo + 32, :, :, lo + 32:lo + 64],
                                        LV[lo:lo + 32, :, 0:256].rearrange("p b (j t) -> p b j t", t=32),
                                        ACT.Copy), "back", name)
                yield
                me.need("pe", "back", "l64", n)
                me.did(a.activation(At[0:64, :, :, 64:128], LV[0:64, :, :].rearrange("p b (j t) -> p b j t", t=64),
                                    ACT.Copy), "back", "at64")
                yield
                me.did(a.activation(KT[:, 0:2, :].rearrange("p c d -> p (c d)"), bank("kt0")[:, :], ACT.Copy),
                       "back", "kt0")
                me.did(a.activation(KT[:, 2, :], bank("kt1")[:, 0:C], ACT.Copy), "back", "kt1")
                yield

            def tail(n):
                for name, dst in (("zt", zT), ("xt", xnT)):
                    for j in range(2):
                        me.need("pe", "tail", f"{name}{j}", n)
                        me.did(a.activation(dst[:, 2 * j:2 * j + 2, :, :].rearrange("p c h t -> p (c h t)"),
                                            TB[:, :], ACT.Copy), "tail", f"{name}{j}")
                        yield
                me.need("dve", "tail", "lsub", n)
                me.did(a.activation(lexp[:, :, :], lsub[:, :, :], ACT.Exp), "tail", "exp")
                yield
                me.need("sp", "tail", "logits", n - 1)
                me.need("pe", "tail", "lt", n)
                me.did(a.activation(lt[:, :], TB[0:CH * E, 0:P], ACT.Copy), "tail", "lt")
                yield

            rounds(act, TURNS["act"], front, back, tail)

        @block.vector
        def _(dve):
            me = Steps(dve, "dve")
            v = nc.vector
            me.credit("pre", *PARTS)
            v.memset(xT[:, :, 0:1], 0.0).then_inc(zeros_ready, 1)
            v.memset(Ad[:, :, :, :], 0.0).then_inc(zeros_ready, 1)
            v.memset(S[:, :, :, :], 0.0).then_inc(zeros_ready, 1)
            dve.wait_ge(zeros_ready, 3)
            dve.wait_ge(first_in, 16 * FIRST)

            def setup():
                dve.wait_ge(consts_in, 16 * CONSTS)
                v.tensor_copy(w2s[:, :, :], w2[:, :, :]).then_inc(w2_split, 1)
                dve.wait_ge(w2_split, 1)
                for q in (32, 96):
                    v.tensor_tensor(w2s[q:q + 32, :, :], w2[q:q + 32, :, :], w2s[q:q + 32, :, :].bitcast(F32),
                                    ALU.subtract).then_inc(w2_split, 1)
                dve.wait_ge(w2_split, 3)
                v.memset(At[:, :, :, :], 0.0).then_inc(zeros_ready, 1)
                dve.wait_ge(zeros_ready, 4)
                dve.wait_ge(masks_ready, 1)

            def pre(n):
                me.arrived(xT_in, 16 * (n + 1))
                me.need("dve", "front", "m_g1", n - 1)
                me.did(v.tensor_tensor(xx[:, :, :], xT[:, :, 0:T], xT[:, :, 1:T + 1], ALU.subtract), "pre", "xx")
                me.need("dve", "pre", "xx", n)
                me.need("pe", "front", "lora_b", n - 1)
                for hp in range(HP):
                    me.did(v.scalar_tensor_tensor(xxx[:, hp, :], xx[:, hp, :], col(MAA["x"], hp),
                                                  xT[:, hp, 1:T + 1], ALU.mult, ALU.add), "pre", f"xxx{hp}")
                yield

            def front(n):
                me.need("pe", "front", "m_g1", n - 1)
                if isinstance(n, int) and n == 0:
                    setup()
                me.need("act", "front", "lora_ah", n)
                me.did(v.tensor_tensor(lora_l[:, :], lora[:, :], lora_h[:, :].bitcast(F32), ALU.subtract), "front",
                       "lora_al")
                me.need("act", "front", "lora_bh", n)
                me.did(v.tensor_tensor(loras[P // 2:P, 4, :], lorag[P // 2:P, :], loras[P // 2:P, 4, :].bitcast(F32),
                                       ALU.subtract), "front", "lora_bl")
                yield
                used = {"w": ("r1", n - 1), "k": ("gate1", n - 1), "v": ("v1", n - 1), "r": ("dec1", n), "g": ("k1", n)}
                for f in MIXES:
                    me.need("pe", "front", *used[f])
                    for hp in range(HP):
                        me.need("pe", "front", f"m_{f}{hp}", n)
                        bank = FB[FRONT_JOBS.index(f"m_{f}{hp}") % 3]
                        me.did(v.scalar_tensor_tensor(mix[f][:, hp, :], bank[:, :], col(MAA[f], hp), xx[:, hp, :],
                                                      ALU.add, ALU.mult), "front", f"m_{f}{hp}")
                    yield
                me.need("act", "front", "r1", n)
                me.need("pe", "front", "d", n - 1)
                for hp in range(HP):
                    me.did(v.scalar_tensor_tensor(ruk[:, hp, :], rn_[:, hp, :], col(7, hp), kn_[:, hp, :],
                                                  ALU.mult, ALU.mult), "front", f"ruk{hp}")
                yield
                me.need("act", "back", "at3", n - 1)
                me.need("pe", "front", "d", n)
                d = FB[FRONT_JOBS.index("d") % 3][:, 0:2 * CH * HP]
                a_in(5, d.rearrange("p (a j o) -> p a j o", a=2, o=1).broadcast_to([P, 2, CH * HP, 32]), "front", "d")
                me.need("pe", "front", "l1", n)
                me.need("dve", "front", "d", n)
                a_in(0, LV[:, :, 0:256].rearrange("p b (j t) -> p b j t", t=32), "front", "a1")
                yield
                me.need("pe", "back", "y1", n - 1)
                r_up(1, rn_, "front", n)
                yield

            def a_in(li, data, part, name):
                mk = masks[:, li, :].rearrange("p (a j t) -> p a j t", a=1, j=1).broadcast_to([P, 2, CH * HP, 32])
                me.did(v.copy_predicated(Ad[:, :, :, :], mk, data), part, name)

            def r_up(b, src, part, n):
                rv = R[:, :, :].rearrange("p h (m o t) -> p (h m) o t", o=2, t=b)
                sv = src[:, :, :].rearrange("p h (m o t) -> p (h m) o t", o=2, t=b)
                wv = W[b][:, :, :].rearrange("p h (m o) -> p (h m) o", o=2)
                m = HP * T // (2 * b)
                if b > 1:
                    me.need("dve", "front" if b == 2 else "back", f"w{b}", n)
                me.did(v.tensor_tensor(rv[:, :, 1, :], sv[:, :, 1, :], wv[:, :, 0:1].broadcast_to([P, m, b]),
                                       ALU.mult), part, f"r{2*b}")
                if 2 * b in LEVELS:
                    me.need("pool", "back", f"k{4*b}", n - 1)
                me.did(v.tensor_tensor(W[2 * b][:, :, :].rearrange("p h m -> p (h m)"), wv[:, :, 0], wv[:, :, 1],
                                       ALU.mult), part, f"w{2*b}")

            def back(n):
                def bank(job):
                    me.need("pe", "back", job, n)
                    return BB[BACK_JOBS.index(job) % 2]

                for li, b in enumerate(LEVELS):
                    if b == 1:
                        continue
                    me.need("pe", "back", f"l{b}", n)
                    me.need("act", "front", "r2", n)
                    r_up(b, R, "back", n)
                    if b <= 16:
                        me.need("dve", "front" if b == 2 else "back", f"a{b//2}", n)
                        a_in(li, LV[:, :, 0:256].rearrange("p b (j t) -> p b j t", t=32), "back", f"a{b}")
                    yield
                heads = [slice(N * par, N * par + N) for par in range(2)]
                for c in range(CH - 1):
                    u = bank(f"u{c//2}")[:, c % 2 * C:c % 2 * C + C]
                    if c == 0:
                        for s, name in zip(heads, ("s0", "s0b")):
                            me.did(v.tensor_copy(S[s, 0, :, s], u[s, :].rearrange("p (h j) -> p h j", h=HP)[:, :, s]),
                                   "back", name)
                    else:
                        me.need("dve", "back", f"s{c-1}b", n)
                        for s, name in zip(heads, (f"s{c}", f"s{c}b")):
                            for hp in range(HP):
                                ins = v.scalar_tensor_tensor(S[s, c, hp, s], S[s, c - 1, hp, s], W[P][s, hp, c:c + 1],
                                                             u[s, hp * P + s.start:hp * P + s.stop],
                                                             ALU.mult, ALU.add)
                            me.did(ins, "back", name)
                yield

            def tail(n):
                me.need("pe", "tail", "zt1", n - 1)
                for c2 in (0, 2):
                    pair = (c2, c2 + 1)
                    me.need("pe", "back", f"y{c2//2}", n)
                    y = BB[BACK_JOBS.index(f"y{c2//2}") % 2]

                    def head(t, c):
                        return t[:, c, :].rearrange("p (h j) -> p h j", h=H)

                    def ych(c):
                        return y[:, c % 2 * C:c % 2 * C + C].rearrange("p (h j) -> p h j", h=H)

                    for c in pair:
                        me.did(v.tensor_reduce(ysum[:, c, :], ych(c), AX.X, ALU.add), "tail", f"ysum{c}")
                    for c in pair:
                        me.need("dve", "tail", f"ysum{c}", n)
                        me.did(v.scalar_tensor_tensor(head(yc, c), ysum[:, c, :].rearrange("p (h o) -> p h o", o=1)
                                                      .broadcast_to([P, H, N]), -1.0 / N, ych(c), ALU.mult, ALU.add),
                               "tail", f"y{c}")
                    for c in pair:
                        me.need("dve", "tail", f"y{c}", n)
                        me.did(v.tensor_tensor(ysq[:, c % 2, :], yc[:, c, :], yc[:, c, :], ALU.mult), "tail", f"sq{c}")
                    for c in pair:
                        me.need("dve", "tail", f"sq{c}", n)
                        me.did(v.tensor_reduce(yssq[:, c, :], head(ysq, c % 2), AX.X, ALU.add), "tail", f"ssq{c}")
                    me.need("dve", "tail", f"ssq{c2+1}", n)
                    me.did(v.tensor_scalar(yvar[:, c2:c2 + 2, :], yssq[:, c2:c2 + 2, :], 1.0 / N, GN_EPS,
                                           ALU.mult, ALU.add), "tail", f"yv{c2}")
                    yield
                for c2 in (0, 2):
                    me.need("pool", "tail", f"yr{c2}", n)
                    for c in (c2, c2 + 1):
                        me.did(v.tensor_tensor(head(yc, c), head(yc, c), yrs[:, c, :].rearrange("p (h o) -> p h o", o=1)
                                               .broadcast_to([P, H, N]), ALU.mult), "tail", f"zr{c}")
                    for c in (c2, c2 + 1):
                        me.need("dve", "tail", f"zr{c}", n)
                        me.did(v.tensor_tensor(z[:, c, :], z[:, c, :], lng, ALU.mult), "tail", f"zg{c}")
                    yield
                me.arrived(xtok_in, 16 * (n + 1))
                for c2 in (0, 2):
                    me.need("pe", "tail", f"o{c2//2}", n)
                    for c in (c2, c2 + 1):
                        me.did(v.tensor_tensor(x1[:, c, :], TB[:, c % 2 * C:c % 2 * C + C], xtok[:, c, :], ALU.add),
                               "tail", f"o{c}")
                    for c in (c2, c2 + 1):
                        me.need("dve", "tail", f"o{c}", n)
                        me.did(v.bn_stats(st[:, c, :], x1[:, c, :]), "tail", f"st{c}")
                    for c in (c2, c2 + 1):
                        me.need("dve", "tail", f"st{c}", n)
                        me.did(v.bn_aggr(mv[:, c, :], st[:, c, :]), "tail", f"mv{c}")
                    if c2:
                        me.need("dve", "tail", "mv3", n)
                        me.did(v.tensor_scalar(ve[:, :], mv[:, :, 1], LN_EPS, None, ALU.add), "tail", "ve")
                    yield
                me.need("pool", "tail", "rstd", n)
                me.did(v.tensor_tensor(q1[:, :], rstd[:, :], rstd[:, :], ALU.mult), "tail", "q1")
                me.need("dve", "tail", "q1", n)
                me.did(v.tensor_tensor(q2[:, :], q1[:, :], mv[:, :, 1], ALU.mult), "tail", "q2")
                me.need("dve", "tail", "q2", n)
                me.did(v.tensor_scalar(q3[:, :], q2[:, :], RMS_EPS, None, ALU.add), "tail", "q3")
                yield
                me.need("pool", "tail", "rn", n)
                me.need("sp", "tail", "table", n - 1)
                for c in range(CH):
                    me.did(v.tensor_scalar(x2[:, c, :], x1[:, c, :], mv[:, c, 0:1], rstd[:, c:c + 1],
                                           ALU.subtract, ALU.mult), "tail", f"x2_{c}")
                for c in range(CH):
                    me.need("dve", "tail", f"x2_{c}", n)
                    me.did(v.scalar_tensor_tensor(table[:, c, 0:C], x2[:, c, :], rn[:, c:c + 1], nwb,
                                                  ALU.mult, ALU.mult), "tail", f"xn{c}")
                yield

                def per_chunk(t):
                    return t[:, :].rearrange("p (c o) -> p c o", o=1).broadcast_to([P, CH, E])

                me.need("pe", "tail", "lt", n - 1)
                me.need("pe", "tail", "lg", n)
                me.did(v.tensor_tensor(lg[:, :, :], TB[:, 0:CH * E].rearrange("p (c e) -> p c e", c=CH),
                                       rb.rearrange("p (o e) -> p o e", o=1).broadcast_to([P, CH, E]), ALU.add),
                       "tail", "lg")
                me.need("dve", "tail", "lg", n)
                me.did(v.tensor_reduce(lmax[:, :], lg[:, :, :], AX.X, ALU.max), "tail", "lmax")
                me.need("dve", "tail", "lmax", n)
                me.did(v.tensor_tensor(lsub[:, :, :], lg[:, :, :], per_chunk(lmax), ALU.subtract), "tail", "lsub")
                yield
                me.need("act", "tail", "exp", n)
                me.did(v.tensor_reduce(lsum[:, :], lexp[:, :, :], AX.X, ALU.add), "tail", "lsum")
                me.need("dve", "tail", "lsum", n)
                me.did(v.reciprocal(lrec[:, :], lsum[:, :]), "tail", "lrec")
                me.need("dve", "tail", "lrec", n)
                me.did(v.tensor_tensor(table[:, :, C:ROW], lexp[:, :, :], per_chunk(lrec), ALU.mult), "tail", "probs")
                yield

            rounds(dve, TURNS["dve"], front, back, tail, pre)

        @block.tensor
        def _(pe):
            me = Steps(pe, "pe")
            mm = nc.tensor.matmul
            me.credit(*PARTS)
            pe.wait_ge(first_in, 16 * FIRST)

            def level(b, r, k):
                for par in range(2):
                    i = slice(N * par, N * par + N)
                    for c in range(CH):
                        for hp in range(HP):
                            j = c * HP + hp
                            t0 = c * P
                            if b <= 16:
                                parts = [(32 * q, 32, 32 * q, 32 * j) for q in range(4)]
                            elif b == 32:
                                parts = [(32 * q, 32, 32 * q + 32, 32 * j) for q in (0, 2)]
                            else:
                                parts = [(0, 64, 64, 64 * j)]
                            for s0, w, tt, o in parts:
                                ins = mm(LV[s0:s0 + w, par, o:o + w], k[i, hp, t0 + s0:t0 + s0 + w],
                                         r[i, hp, t0 + tt:t0 + tt + w], start=True, stop=True,
                                         tile_position=(N * par, s0))
                return ins

            def front(n):
                def bank(job):
                    return ring(me, "front", FB, FRONT_JOBS, FRONT_READER, job, n)

                def chan_major(job, lhs, src, m=P, lo=0):
                    out = bank(job)
                    for a in range(HP):
                        ins = mm(out[0:m, :], lhs[:, a, lo:lo + m], src[:, a, :], start=(a == 0), stop=(a == HP - 1))
                    me.did(ins, "front", job)

                def mixes(f):
                    j = MIXES.index(f)
                    if f == "g":
                        me.need("dve", "front", "lora_bl", n)
                    else:
                        me.arrived(stack_in[j], 64 * (n + 1))
                    for hp in range(HP):
                        me.did(mm(bank(f"m_{f}{hp}")[:, :], w2s[:, j, hp * P:hp * P + P], loras[:, j, :],
                                  start=True, stop=True), "front", f"m_{f}{hp}")

                me.need("dve", "pre", "xxx1", n)
                chan_major("lora_a", w1, xxx)
                chan_major("lora_b", w1, xxx, lo=P)
                if isinstance(n, int) and n == 0:
                    pe.wait_ge(consts_in, 16 * CONSTS)
                    pe.wait_ge(setup_pool2, 3)
                    pe.wait_ge(w2_split, 3)
                    pe.wait_ge(zeros_ready, 4)
                yield
                mixes("w")
                yield
                mixes("k")
                yield
                me.need("pool", "front", "xw", n)
                chan_major("dec1", W1["w"], mix["w"], m=64)
                yield
                mixes("v")
                yield
                me.need("pool", "front", "xk", n)
                for hp in range(HP):
                    chan_major(f"k{hp}", Wp["k"], mix["k"], lo=hp * P)
                yield
                mixes("r")
                yield
                me.need("act", "front", "dec1", n)
                for hp, job in ((0, "dec0"), (1, "dec2")):
                    out = bank(job)
                    me.did(mm(out[:, :], W2["w"][:, hp * P:hp * P + P], dec1[:, :], start=True, stop=True),
                           "front", job)
                yield
                mixes("g")
                yield
                me.need("pool", "front", "xr", n)
                for hp in range(HP):
                    chan_major(f"r{hp}", Wp["r"], mix["r"], lo=hp * P)
                yield
                me.need("dve", "front", "ruk1", n)
                out = bank("d")
                for c in range(CH):
                    for hp in range(HP):
                        j = c * HP + hp
                        ins = mm(out[:, j:j + CH * HP + 1:CH * HP], ruk[:, hp, c * P:c * P + P], pairones[:, :],
                                 start=True, stop=True)
                me.did(ins, "front", "d")
                yield
                me.need("act", "front", "r1", n)
                me.need("act", "back", "at64", n - 1)
                me.did(level(1, rn_, kn_), "front", "l1")
                yield
                me.need("pool", "front", "xg", n)
                chan_major("gate1", W1["g"], mix["g"], m=64)
                yield
                for j in range(2):
                    out = bank(f"v{j}")
                    for cc in range(2):
                        t = slice((2 * j + cc) * P, (2 * j + cc + 1) * P)
                        for a in range(HP):
                            ins = mm(out[:, cc * C:cc * C + C], mix["v"][:, a, t], Wp["v"][:, a, :], start=(a == 0),
                                     stop=(a == HP - 1))
                    me.did(ins, "front", f"v{j}")
                yield

            def back(n):
                def bank(job):
                    return ring(me, "back", BB, BACK_JOBS, BACK_READER, job, n)

                def gates():
                    me.need("act", "front", "gate1", n)
                    for j in range(2):
                        out = bank(f"g{j}")
                        for cc in range(2):
                            t = slice((2 * j + cc) * P, (2 * j + cc + 1) * P)
                            ins = mm(out[:, cc * C:cc * C + C], gate1[:, t], W2["g"][:, :], start=True, stop=True)
                        me.did(ins, "back", f"g{j}")

                for b in LEVELS[1:]:
                    me.need("dve", "front" if b == 2 else "back", f"r{b}", n)
                    me.need("pool", "front" if b == 2 else "back", f"k{b}", n)
                    if b == 2:
                        me.need("act", "front", "r2", n)
                        me.need("dve", "front", "a1", n)
                    elif b <= 32:
                        me.need("dve", "back", f"a{b//2}", n)
                    else:
                        me.need("act", "back", "at32b", n)
                    me.did(level(b, R, K), "back", f"l{b}")
                    yield
                    if b == 8:
                        gates()
                        yield
                me.need("pool", "back", "k128", n)
                for j in range(2):
                    out = bank(f"kt{j}")
                    for c in range(2 * j, min(2 * j + 2, CH - 1)):
                        for hp in range(HP):
                            o = c % 2 * C + hp * P
                            ins = nc.tensor.transpose(out[:, o:o + P], K[:, hp, c * P:c * P + P], ident[:, :])
                    me.did(ins, "back", f"kt{j}")
                yield
                me.need("act", "front", "v1", n)
                for j in range(2):
                    out = bank(f"u{j}")
                    me.need("act", "back", f"kt{j}", n)
                    for c in range(2 * j, min(2 * j + 2, CH - 1)):
                        for hp in range(HP):
                            o = c % 2 * C + hp * P
                            ins = mm(out[:, o:o + P], KT[:, c, hp * P:hp * P + P],
                                     vn_[:, c, hp * P:hp * P + P], start=True, stop=True)
                    me.did(ins, "back", f"u{j}")
                yield
                me.need("act", "back", "at64", n)
                me.need("dve", "back", "r128", n)
                for c in range(CH):
                    if c % 2 == 0:
                        out = bank(f"y{c//2}")
                    if c:
                        me.need("dve", "back", f"s{c-1}b", n)
                    for hp in range(HP):
                        o = c % 2 * C + hp * P
                        if c:
                            mm(out[:, o:o + P], R[:, hp, c * P:c * P + P], S[:, c - 1, hp, :],
                               start=True, stop=False, skip_group_check=True)
                        for par in range(2):
                            ins = mm(out[:, o + N * par:o + N * par + N], At[:, par, c * HP + hp, :],
                                     vn_[:, c, hp * P + N * par:hp * P + N * par + N],
                                     start=(c == 0), stop=True, skip_group_check=True)
                    if c % 2:
                        me.did(ins, "back", f"y{c//2}")
                yield

            def tail(n):
                def bank(job):
                    return ring(me, "tail", [TB], PE_TAIL, TAIL_READER, job, n)

                def turned(job, src, chunks):
                    out = bank(job)
                    for c in chunks:
                        for hp in range(HP):
                            o = c % 2 * C + hp * P
                            ins = nc.tensor.transpose(out[:, o:o + P], src[:, c, hp * P:hp * P + P], ident[:, :])
                    me.did(ins, "tail", job)

                for j in range(2):
                    me.need("pool", "tail", f"z{2*j+1}", n)
                    turned(f"zt{j}", z, (2 * j, 2 * j + 1))
                    yield
                    out = bank(f"o{j}")
                    for c in (2 * j, 2 * j + 1):
                        for hp in range(HP):
                            ins = mm(out[:, c % 2 * C:c % 2 * C + C], zT[:, c, hp, :], Wp["o"][:, hp, :],
                                     start=(hp == 0), stop=(hp == HP - 1))
                    me.did(ins, "tail", f"o{j}")
                    yield
                for j in range(2):
                    me.need("dve", "tail", f"xn{2*j+1}", n)
                    turned(f"xt{j}", table, (2 * j, 2 * j + 1))
                    yield
                out = bank("lg")
                for c in range(CH):
                    for hp in range(HP):
                        ins = mm(out[:, c * E:c * E + E], xnT[:, c, hp, :], rwT[:, hp, :], start=(hp == 0),
                                 stop=(hp == HP - 1))
                me.did(ins, "tail", "lg")
                yield
                out = bank("lt")
                me.did(nc.tensor.transpose(out[0:CH * E, 0:P], lg[:, :, :].rearrange("p c e -> p (c e)"), ident[:, :]),
                       "tail", "lt")
                yield

            rounds(pe, TURNS["pe"], front, back, tail)


def stage_b(nc, io, keep):
    with ExitStack() as ctx:
        def sb(name, shape, dt=F32):
            return ctx.enter_context(nc.sbuf_tensor(name, shape, dt))

        def sem(name):
            return ctx.enter_context(nc.semaphore(name))

        CLEAR = 4
        zeros = sb("zeros", [P, NT * ARow // P // CLEAR])
        acc_zero, acc_zeroed = sem("acc_zero"), sem("acc_zeroed")
        L = sb("L", [P, ST])
        ones = sb("ones", [P, ST])
        hit = sb("hit", [P, ST])
        gt = sb("gt", [P, ST])
        eq = sb("eq", [P, ST])
        ceq = sb("ceq", [P, ST])
        sel = sb("sel", [P, ST])
        cum = sb("cum", [P, ST])
        ends = sb("ends", [P, SEG])
        allends, eoff = keep["allends"], keep["eoff"]
        group = sb("group", [P, P])
        before = sb("before", [P, P])
        gi = sb("gi", [P, P], I32)
        gp = sb("gp", [P, P], I32)
        gj = sb("gj", [P, P], I32)
        slot_i = sb("slot_i", [P, G], I32)
        eoff_i = sb("eoff_i", [P, E * G], I32)
        now = sb("now", [P, 3], I32)
        both = sb("both", [P, 6], I32)
        bit = sb("bit", [P, 1], I32)
        flip2 = sb("flip2", [P, 2], I32)
        flip = sb("flip", [P, 1], I32)
        thr = sb("thr", [P, 1], I32)
        take = sb("take", [P, 1], I32)
        cnt = sb("cnt", [P, 1])
        cnt2 = sb("cnt2", [P, 2])
        room = sb("room", [P, 1])
        offs = sb("offs", [P, 1])
        cnt3 = sb("cnt3", [P, 1])
        offs3 = sb("offs3", [P, 1])
        PT = ctx.enter_context(nc.psum_tensor("PT", [P, 512], F32))
        PG = ctx.enter_context(nc.psum_tensor("PG", [P, 512], F32))
        PE2 = ctx.enter_context(nc.psum_tensor("PE2", [P, 512], F32))
        PS = ctx.enter_context(nc.psum_tensor("PS", [P, 512], F32))
        logits_in, iotas, groups_ready = sem("logits_in"), sem("iotas"), sem("groups_ready")
        counted, summed = sem("counted"), sem("summed")
        chain, decided = sem("chain"), sem("decided")
        ends_ready, ends_out, ends_in, cum_out = sem("ends_ready"), sem("ends_out"), sem("ends_in"), sem("cum_out")
        dve_turns, pe_turns = sem("dve_turns_b"), sem("pe_turns_b")
        block = ctx.enter_context(nc.Block())

        @block.sync
        def _(sp):
            sp.dma_start(L[:, :], io["logitsT"].rearrange("e (s t) -> (e s) t", t=ST)).then_inc(logits_in, 16)
            sp.dma_start(keep["b1"][:, :, :], io["b1"]).then_inc(keep["b1_in"], 16)
            load_w1(sp, io, keep, 0)
            load_w2(sp, io, keep, 0)
            sp.wait_ge(ends_ready, 1)
            sp.dma_start(io["ends"].rearrange("o (p t) -> (o p) t", p=P), ends[:, :]).then_inc(ends_out, 16)
            sp.dma_start(io["cum"].rearrange("(p t) j -> p (t j)", p=P), cum[:, :]).then_inc(cum_out, 16)
            sp.wait_ge(ends_out, 16)
            sp.dma_start(allends[:, :], io["ends"].broadcast_to([P, E * TILES])).then_inc(ends_in, 16)
            sp.wait_ge(ends_in, 16)
            sp.wait_ge(cum_out, 16)

        @block.gpsimd
        def _(pool):
            g = nc.gpsimd
            g.memset(zeros[:, :], 0.0).then_inc(acc_zero, 1)
            pool.wait_ge(acc_zero, 1)
            acc = io["acc"].rearrange("(p n) d -> p (n d)", p=P)
            w = zeros.shape[1]
            for j in range(CLEAR):
                pool.dma_start(acc[:, j * w:(j + 1) * w], zeros[:, :]).then_inc(acc_zeroed, 16)
            g.iota(gi[:, :], pattern=[[0, P]], base=0, channel_multiplier=1).then_inc(iotas, 1)
            g.iota(gj[:, :], pattern=[[1, P]], base=0, channel_multiplier=0).then_inc(iotas, 1)
            g.iota(slot_i[:, :], pattern=[[P, G]], base=0, channel_multiplier=1).then_inc(iotas, 1)
            g.iota(eoff_i[:, :], pattern=[[TILES, E], [0, G]], base=0, channel_multiplier=0).then_inc(iotas, 1)
            pool.wait_ge(acc_zeroed, 16 * CLEAR)

        @block.tensor
        def _(pe):
            pe.wait_ge(groups_ready, 1)
            with pe.Fori(0, 32) as i:
                pe.wait_ge(counted, i + 1).then_inc(pe_turns, 1)
                nc.tensor.matmul(PT[:, 0:1], group[:, :], cnt[:, :], start=True, stop=True).then_inc(summed, 1)
            pe.wait_ge(counted, 33)
            nc.tensor.matmul(PG[:, 0:2], group[:, :], cnt2[:, :], start=True, stop=True).then_inc(summed, 1)
            nc.tensor.matmul(PE2[:, 0:2], before[:, :], cnt2[:, :], start=True, stop=True).then_inc(summed, 1)
            pe.wait_ge(counted, 34)
            nc.tensor.matmul(PS[:, 0:1], before[:, :], cnt3[:, :], start=True, stop=True).then_inc(summed, 1)

        @block.vector
        def _(dve):
            v = nc.vector
            PRE, PER = 16, 5
            dve.wait_ge(iotas, 4)
            done = [0]

            def link(ins):
                done[0] += 1
                ins.then_inc(chain, 1)
                dve.wait_ge(chain, done[0])

            link(v.tensor_scalar(gp[:, :], gi[:, :], 3, None, ALU.logical_shift_right))
            link(v.tensor_scalar(eq[:, 0:P].bitcast(I32), gj[:, :], 3, None, ALU.logical_shift_right))
            link(v.tensor_tensor(group[:, :], gp[:, :], eq[:, 0:P].bitcast(I32), ALU.is_equal))
            link(v.tensor_tensor(before[:, :], gi[:, :], gj[:, :], ALU.is_lt))
            link(v.tensor_tensor(before[:, :], before[:, :], group[:, :], ALU.mult))
            link(v.tensor_copy(keep["slot"][:, :], slot_i[:, :]))
            link(v.tensor_copy(eoff[:, :], eoff_i[:, :]))
            link(v.memset(ones[:, :], 1.0))
            link(v.memset(keep["tile"][:, E * G:], 0.0))
            link(v.memset(keep["cumrow"][:, E * G:], 0.0))
            link(v.memset(now[:, :], 0))
            link(v.memset(bit[:, :], 1))
            link(v.tensor_scalar(bit[:, :], bit[:, :], 30, None, ALU.logical_shift_left))
            link(v.tensor_scalar(now[:, 1:2], bit[:, :], 1, None, ALU.logical_shift_left))

            def as_float(out, key_):
                yield v.tensor_scalar(flip[:, :], key_, 31, -1, ALU.arith_shift_right, ALU.bitwise_xor)
                yield v.scalar_tensor_tensor(out, flip[:, :], -2 ** 31, key_, ALU.bitwise_or, ALU.bitwise_xor)

            for ins in as_float(now[:, 2:3], now[:, 1:2]):
                link(ins)
            assert done[0] == PRE, done
            v.engine_nop().then_inc(groups_ready, 1)
            dve.wait_ge(logits_in, 16)
            with dve.Fori(0, 32) as i:
                def after(k):
                    dve.wait_ge(chain, PER * i + PRE + k).then_inc(dve_turns, 1)

                v.tensor_scalar(hit[:, :], L[:, :], now[:, 2:3].bitcast(F32), None, ALU.is_ge, ALU.add,
                                accum_out=cnt[:, :]).then_inc(counted, 1)
                v.tensor_copy(both[:, 0:2], now[:, 0:2])
                v.tensor_scalar(both[:, 2:4], now[:, 0:2], bit[:, :], None, ALU.bitwise_or).then_inc(chain, 1)
                after(1)
                v.tensor_scalar(flip2[:, :], both[:, 2:4], 31, -1, ALU.arith_shift_right, ALU.bitwise_xor)\
                    .then_inc(chain, 1)
                v.tensor_scalar(bit[:, :], bit[:, :], 1, None, ALU.logical_shift_right)
                after(2)
                v.scalar_tensor_tensor(both[:, 4:6], flip2[:, :], -2 ** 31, both[:, 2:4], ALU.bitwise_or,
                                       ALU.bitwise_xor).then_inc(chain, 1)
                after(3)
                v.tensor_copy(now[:, :], both[:, 0:6:2]).then_inc(chain, 1)
                dve.wait_ge(summed, i + 1).then_inc(dve_turns, 1)
                v.tensor_scalar(take[:, :], PT[:, 0:1], float(CAP), None, ALU.is_ge).then_inc(chain, 1)
                after(5)
                v.copy_predicated(now[:, :], take[:, :].broadcast_to([P, 3]), both[:, 1:6:2]).then_inc(decided, 1)
                dve.wait_ge(decided, i + 1).then_inc(dve_turns, 1)
            done[0] = 32 * PER + PRE
            key = now[:, 0:1]
            for ins in as_float(thr[:, :], key):
                link(ins)
            T_ = thr[:, :].bitcast(F32)
            link(v.tensor_scalar(gt[:, :], L[:, :], T_, None, ALU.is_gt, ALU.add, accum_out=cnt2[:, 0:1]))
            v.tensor_scalar(eq[:, :], L[:, :], T_, None, ALU.is_equal, ALU.add, accum_out=cnt2[:, 1:2])\
                .then_inc(counted, 1)
            dve.wait_ge(summed, 34)
            link(v.tensor_scalar(room[:, :], PG[:, 0:1], -1.0, float(CAP), ALU.mult, ALU.add))
            link(v.tensor_copy(offs[:, :], PE2[:, 1:2]))
            link(v.tensor_tensor_scan(ceq[:, :], ones[:, :], eq[:, :], offs[:, :], ALU.mult, ALU.add))
            link(v.scalar_tensor_tensor(hit[:, :], ceq[:, :], room[:, :], eq[:, :], ALU.is_le, ALU.mult))
            v.scalar_tensor_tensor(sel[:, :], hit[:, :], 0.0, gt[:, :], ALU.add, ALU.add, accum_out=cnt3[:, :])\
                .then_inc(counted, 1)
            dve.wait_ge(summed, 35)
            link(v.tensor_copy(offs3[:, :], PS[:, 0:1]))
            link(v.tensor_tensor_scan(cum[:, :], ones[:, :], sel[:, :], offs3[:, :], ALU.mult, ALU.add))
            v.tensor_copy(ends[:, :], cum[:, :].rearrange("p (t j) -> p t j", j=P)[:, :, P - 1]).then_inc(ends_ready, 1)
            dve.wait_ge(ends_in, 16)
            for ins in slot_tiles(nc, keep, 0, 1):
                link(ins)


def slot_tiles(nc, keep, first, last):
    v = nc.vector
    shape = [P, last - first, G, TILES]
    slots = slice(first * G, last * G)
    e_v = keep["allends"][:, first * TILES:last * TILES].rearrange("p (e g t) -> p e g t", e=last - first, g=1)
    s_v = keep["slot"][:, :].rearrange("p (e g t) -> p e g t", e=1, t=1)
    cmp = keep["tile_cmp"]
    yield v.tensor_tensor(cmp[:, first:last, :, :], e_v.broadcast_to(shape), s_v.broadcast_to(shape), ALU.is_le)
    yield v.tensor_reduce(keep["tile"][:, slots], cmp[:, first:last, :, :].rearrange("p e g t -> p (e g) t"), AX.X, ALU.add)
    yield v.tensor_tensor(keep["cumrow"][:, slots], keep["tile"][:, slots], keep["eoff"][:, slots], ALU.add)


C_ORDER = {
    ("pe", "front"): ["xt0", "xt1"],
    ("pe", "back"): [f"h{f}" for f in range(FT)] + [f"y{g}" for g in range(G)],
    ("act", "front"): ["xh0", "xh1"],
    ("act", "back"): [f"h{f}" for f in range(FT)],
    ("act", "split1"): ["w1h"],
    ("act", "split2"): ["w2h"],
    ("dve", "hidden"): [s for f in range(FT + 1)
                          for s in [f"hh{f}"] * (f < FT) + [f"hl{f-1}"] * (f > 0)],
    ("dve", "find"): ["idx", "cmp", "pin", "tok", "all"],
    ("dve", "front"): ["xl0", "xl1"],
    ("dve", "gate"): ["gate"],
    ("dve", "back"): ["add_idx"] + [s for g in range(G) for s in (f"yb{g}", f"c{g}", f"y{g}")],
    ("dve", "split1"): ["w1l"],
    ("pool", "split2"): ["w2l"],
    ("pool", "back"): ["add"],
}


def load_w1(sp, io, keep, e):
    sp.dma_start(keep["fw1"][:, :, :], io["fc1T"][bass.ds(e, 1), :, :].rearrange("o (a p) f -> (o p) a f", p=P))\
        .then_inc(keep["w1_in"], 16)


def load_w2(sp, io, keep, e):
    sp.dma_start(keep["fw2"][:, :, :], io["fc2T"][bass.ds(e, 1), :, :].rearrange("o (j p) d -> (o p) j d", p=P))\
        .then_inc(keep["w2_in"], 16)


def stage_c(nc, io, keep):
    with ExitStack() as ctx:
        def sb(name, shape, dt=F32):
            return ctx.enter_context(nc.sbuf_tensor(name, shape, dt))

        def sem(name):
            return ctx.enter_context(nc.semaphore(name))

        ident = sb("identc", [P, P])
        b2 = sb("b2", [P, C])
        w1, w2, b1 = keep["fw1"], keep["fw2"], keep["b1"]
        idx = sb("idx", [P, G], I32)
        crow = sb("crow", [P, G, P])
        cmp = sb("ccmp", [P, G, P])
        pin = sb("pin", [P, G])
        tok = sb("tok", [P, G], I32)
        tokall = sb("tokall", [P, (E + 2) * G], I32)
        tokadd = sb("tokadd", [P, G], I32)
        xg = sb("xg", [P, G, ROW])
        w1h, w1l = sb("w1h", [P, HP, FF], F32R), sb("w1l", [P, HP, FF], F32R)
        w2h, w2l = sb("w2h", [P, FT, C], F32R), sb("w2l", [P, FT, C], F32R)
        xh, xl = sb("xh", [P, HP, CAP], F32R), sb("xl", [P, HP, CAP], F32R)
        gate = sb("gate", [P, G])
        hid = sb("hid", [P, 4, CAP])
        hh, hl = sb("hh", [P, FT, CAP], F32R), sb("hl", [P, FT, CAP], F32R)
        yb = sb("yb", [P, 2, C])
        yg = sb("yg", [P, G, ARow])
        XB = [ctx.enter_context(nc.psum_tensor(f"XB{i}", [P, 512], F32)) for i in range(2)]
        HB = [ctx.enter_context(nc.psum_tensor(f"HB{i}", [P, 512], F32)) for i in range(4)]
        YB = [ctx.enter_context(nc.psum_tensor(f"YB{i}", [P, 512], F32)) for i in range(2)]
        ident0, ready = sem("ident0"), sem("ready_c")
        yg_clear, b2_in, tiles_made = sem("yg_clear"), sem("b2_in"), sem("tiles_made")
        w1_in, w2_in, b1_in = keep["w1_in"], keep["w2_in"], keep["b1_in"]
        crow_in, rows_in, added = sem("crow_in"), sem("rows_in"), sem("added")
        done = {key: sem("_".join(key) + "_c") for key in C_ORDER}
        counts = Counts(done, C_ORDER, {e: sem(f"{e}_turns_c") for e in ("pe", "act", "dve", "pool", "sp")})
        block = ctx.enter_context(nc.Block())

        def gathered(me, dma_sem, e):
            me.arrived(dma_sem, 16 * G * (e + 1))

        @block.sync
        def _(sp):
            me = EngineSteps(sp, "sp", counts)
            def bias(e):
                me.need("dve", "back", f"yb{G-1}", e - 1)
                sp.dma_start(b2[:, :], io["b2"][bass.ds(e, 1), :].broadcast_to([P, C])).then_inc(b2_in, 16)

            bias(0)
            with sp.Fori(1, E) as e:
                me.need("dve", "split1", "w1l", e - 1)
                load_w1(sp, io, keep, e)
                me.need("pool", "split2", "w2l", e - 1)
                load_w2(sp, io, keep, e)
                bias(e)

        @block.gpsimd
        def _(pool):
            me = EngineSteps(pool, "pool", counts)
            g = nc.gpsimd
            me.credit("split2", "back")
            g.memset(ident[:, :], 0.0).then_inc(ident0, 1)
            pool.wait_ge(ident0, 1)
            g.affine_select(out=ident[:, :], in_=ident[:, :], compare_op=ALU.not_equal, fill=1.0, base=0,
                            pattern=[[-1, P]], channel_multiplier=1).then_inc(ready, 1)

            def find(e):
                me.need("dve", "find", "idx", e)
                me.need("dve", "find", "cmp", e - 1)
                for j in range(G):
                    g.indirect_dma_start(crow[:, j, :], None, io["cum"],
                                         bass.IndirectOffsetOnAxis(ap=idx[:, j:j + 1], axis=0)).then_inc(crow_in, 16)

            def front(e):
                me.need("dve", "find", "tok", e)
                me.need("dve", "gate", "gate", e - 1)
                me.need("pe", "front", "xt1", e - 1)
                for j in range(G):
                    g.indirect_dma_start(xg[:, j, :], None, io["table"],
                                         bass.IndirectOffsetOnAxis(ap=tok[:, j:j + 1], axis=0)).then_inc(rows_in, 16)

            def back(e):
                for j in range(G):
                    me.need("dve", "back", f"y{j}", e)
                    g.indirect_dma_start(io["acc"], bass.IndirectOffsetOnAxis(ap=tokadd[:, j:j + 1], axis=0),
                                         yg[:, j, :], None, compute_op=ALU.add).then_inc(added, 16)

            def low2(e):
                me.need("act", "split2", "w2h", e)
                me.did(g.tensor_tensor(w2l[:, :, :], w2[:, :, :], w2h[:, :, :].bitcast(F32), ALU.subtract), "split2", "w2l")

            def adds_end(e):
                me.did(pool.wait_ge(added, 16 * G * (e + 1)), "back", "add")

            find(0)
            front(0)
            find(1)
            low2(0)
            with pool.Fori(0, E - 1) as e:
                front(e + 1)
                find(e + 2)
                back(e)
                low2(e + 1)
                adds_end(e)
            back(E - 1)
            adds_end(E - 1)

        @block.scalar
        def _(act):
            me = EngineSteps(act, "act", counts)
            a = nc.scalar
            me.credit("front", "back", "split1", "split2")
            act.wait_ge(b1_in, 16)

            def front(e):
                for hp in range(HP):
                    me.need("pe", "front", f"xt{hp}", e)
                    me.need("pe", "back", f"h{FT-1}", e - 1)
                    me.did(a.activation(xh[:, hp, :], XB[hp][:, :], ACT.Copy), "front", f"xh{hp}")

            def high1(e):
                me.arrived(w1_in, 16 * (e + 1))
                me.need("pe", "back", f"h{FT-1}", e - 1)
                me.did(a.activation(w1h[:, :, :], w1[:, :, :], ACT.Copy), "split1", "w1h")

            def high2(e):
                me.arrived(w2_in, 16 * (e + 1))
                me.need("pe", "back", f"y{G-1}", e - 1)
                me.did(a.activation(w2h[:, :, :], w2[:, :, :], ACT.Copy), "split2", "w2h")

            def back(e):
                for f in range(FT):
                    if f == 1:
                        high2(e)
                    me.need("dve", "hidden", f"hl{(f-4) % FT}", e if f >= 4 else e - 1)
                    me.need("pe", "back", f"h{f}", e)
                    me.did(a.activation(hid[:, f % 4, :], HB[f % 4][:, :], ACT.Gelu,
                                        bias=b1[:, bass.ds(e, 1), f:f + 1].rearrange("p o f -> p (o f)")),
                           "back", f"h{f}")

            high1(0)
            front(0)
            with act.Fori(0, E - 1) as e:
                back(e)
                high1(e + 1)
                front(e + 1)
            back(E - 1)

        @block.vector
        def _(dve):
            me = EngineSteps(dve, "dve", counts)
            v = nc.vector
            me.credit("find", "front", "gate", "hidden", "split1", "back")
            slot = keep["slot"][:, :].rearrange("p (g o) -> p g o", o=1).broadcast_to([P, G, P])

            def index(e):
                if not (isinstance(e, int) and e == 0):
                    gathered(me, crow_in, e - 1)
                me.did(v.tensor_copy(idx[:, :], keep["cumrow"][:, bass.ds(e * G, G)]), "find", "idx")

            def find(e):
                gathered(me, crow_in, e)
                me.did(v.tensor_tensor(cmp[:, :, :], crow[:, :, :], slot, ALU.is_le), "find", "cmp")
                me.need("dve", "find", "cmp", e)
                me.did(v.tensor_reduce(pin[:, :], cmp[:, :, :], AX.X, ALU.add), "find", "pin")
                me.need("dve", "find", "pin", e)
                if not (isinstance(e, int) and e == 0):
                    gathered(me, rows_in, e - 1)
                me.did(v.scalar_tensor_tensor(tok[:, :], keep["tile"][:, bass.ds(e * G, G)], float(P), pin[:, :],
                                              ALU.mult, ALU.add), "find", "tok")
                me.need("dve", "find", "tok", e)
                me.did(v.tensor_copy(tokall[:, bass.ds(e * G, G)], tok[:, :]), "find", "all")

            def turned(e):
                for hp in range(HP):
                    me.need("act", "front", f"xh{hp}", e)
                    me.did(v.tensor_tensor(xl[:, hp, :], XB[hp][:, :], xh[:, hp, :].bitcast(F32), ALU.subtract),
                           "front", f"xl{hp}")

            def gates(e):
                gathered(me, rows_in, e)
                me.need("dve", "back", f"y{G-1}", e - 1)
                me.did(v.tensor_copy(gate[:, :], xg[:, :, bass.ds(e + C, 1)].rearrange("p g o -> p (g o)")),
                       "gate", "gate")

            def hidden(e):
                me.need("pe", "back", f"y{G-1}", e - 1)
                for f in range(FT + 1):
                    if f < FT:
                        me.need("act", "back", f"h{f}", e)
                        me.did(v.tensor_copy(hh[:, f, :], hid[:, f % 4, :]), "hidden", f"hh{f}")
                    if f:
                        me.need("dve", "hidden", f"hh{f-1}", e)
                        me.did(v.tensor_tensor(hl[:, f - 1, :], hid[:, (f - 1) % 4, :],
                                               hh[:, f - 1, :].bitcast(F32), ALU.subtract), "hidden", f"hl{f-1}")

            def back(e, groups):
                for j in groups:
                    if j == 0:
                        me.need("pool", "back", "add", e - 1)
                        me.did(v.tensor_copy(tokadd[:, :], tokall[:, bass.ds(e * G, G)]), "back", "add_idx")
                        me.arrived(b2_in, 16 * (e + 1))
                        me.need("dve", "gate", "gate", e)
                    if j >= 2:
                        me.need("dve", "back", f"y{j-2}", e)
                    me.need("pe", "back", f"y{j}", e)
                    me.did(v.tensor_tensor(yb[:, j % 2, :], YB[j % 2][:, 0:C], b2[:, :], ALU.add), "back", f"yb{j}")
                    me.did(v.tensor_copy(yg[:, j, C:C + 1], gate[:, j:j + 1]), "back", f"c{j}")
                    me.need("dve", "back", f"yb{j}", e)
                    me.did(v.tensor_scalar(yg[:, j, 0:C], yb[:, j % 2, :], gate[:, j:j + 1], None, ALU.mult),
                           "back", f"y{j}")

            def low1(e):
                me.need("act", "split1", "w1h", e)
                me.did(v.tensor_tensor(w1l[:, :, :], w1[:, :, :], w1h[:, :, :].bitcast(F32), ALU.subtract),
                       "split1", "w1l")

            def tiles(first, last):
                for ins in slot_tiles(nc, keep, first, last):
                    tiled[0] += 1
                    ins.then_inc(tiles_made, 1)
                    dve.wait_ge(tiles_made, tiled[0])

            tiled = [0]
            index(0)
            tiles(1, 6)
            find(0)
            index(1)
            v.memset(yg[:, :, :], 0.0).then_inc(yg_clear, 1)
            dve.wait_ge(yg_clear, 1)
            tiles(6, E)
            low1(0)
            find(1)
            turned(0)
            gates(0)
            index(2)
            with dve.Fori(0, E - 1) as e:
                hidden(e)
                back(e, (0,))
                low1(e + 1)
                back(e, (1,))
                turned(e + 1)
                find(e + 2)
                back(e, (2, 3))
                gates(e + 1)
                index(e + 3)
            hidden(E - 1)
            back(E - 1, (0, 1, 2, 3))

        @block.tensor
        def _(pe):
            me = EngineSteps(pe, "pe", counts)
            mm = nc.tensor.matmul
            me.credit("front", "back")
            pe.wait_ge(ready, 1)

            def front(e):
                gathered(me, rows_in, e)
                for hp in range(HP):
                    me.need("dve", "front", f"xl{hp}", e - 1)
                    for j in range(G):
                        ins = nc.tensor.transpose(XB[hp][:, j * P:j * P + P], xg[:, j, hp * P:hp * P + P], ident[:, :])
                    me.did(ins, "front", f"xt{hp}")

            def up(e):
                me.need("dve", "split1", "w1l", e)
                me.need("dve", "front", "xl1", e)
                for f in range(FT):
                    me.need("act", "back", f"h{(f-4) % FT}", e if f >= 4 else e - 1)
                    cols = slice(f * P, f * P + P)
                    passes = [(w, x, a_) for a_ in range(HP) for w, x in ((w1h, xh), (w1h, xl), (w1l, xh))]
                    for i, (w, x, a_) in enumerate(passes):
                        ins = mm(HB[f % 4][:, :], w[:, a_, cols], x[:, a_, :], start=(i == 0),
                                 stop=(i == len(passes) - 1))
                    me.did(ins, "back", f"h{f}")

            def down(e, groups):
                if groups[0] == 0:
                    me.need("pool", "split2", "w2l", e)
                for j in groups:
                    me.need("dve", "back", f"yb{(j-2) % G}", e if j >= 2 else e - 1)
                    slots = slice(j * P, j * P + P)
                    for f in range(FT):
                        if j == 0:
                            me.need("dve", "hidden", f"hl{f}", e)
                        for i, (h_, w) in enumerate(((hh, w2h), (hh, w2l), (hl, w2h))):
                            ins = mm(YB[j % 2][:, 0:C], h_[:, f, slots], w[:, f, :], start=(f == 0 and i == 0),
                                     stop=(f == FT - 1 and i == 2))
                    me.did(ins, "back", f"y{j}")

            front(0)
            with pe.Fori(0, E - 1) as e:
                up(e)
                down(e, (0, 1))
                front(e + 1)
                down(e, (2, 3))
            up(E - 1)
            down(E - 1, (0, 1, 2, 3))


D_SP, D_POOL = ["in"], ["rstd"]
D_DVE = ["den", "rec"] + [f"{s}{c}" for s in ("x", "st", "mv") for c in range(CH)] + ["ve"]
D_ACT = [f"o{c}" for c in range(CH)]


def stage_d(nc, io, keep):
    with ExitStack() as ctx:
        def sb(name, shape, dt=F32):
            return ctx.enter_context(nc.sbuf_tensor(name, shape, dt))

        def sem(name):
            return ctx.enter_context(nc.semaphore(name))

        BUF = 4
        acc = sb("accb", [P, BUF, CH, ARow])
        o = sb("ob", [P, BUF, CH, C])
        x3 = sb("x3", [P, BUF, CH, C])
        neghalf = sb("neghalf_d", [P, CH])
        small = {k: sb(k + "_d", [P, BUF, CH]) for k in ("den", "rec", "ve", "rstd", "nm")}
        st = sb("st_d", [P, BUF, CH, 6])
        mv = sb("mv_d", [P, BUF, CH, 2])
        half_ready = sem("half_ready")
        acc_in, out_done = [sem(f"acc_in{b}") for b in range(BUF)], [sem(f"out_done{b}") for b in range(BUF)]
        engines = ("act", "dve", "pool")
        parts = [f"b{b}" for b in range(BUF)]
        done = {(e, p): sem(f"{e}_{p}_d") for e in engines + ("sp",) for p in parts}
        order = {(e, p): s for e, s in (("act", D_ACT), ("dve", D_DVE), ("pool", D_POOL), ("sp", D_SP)) for p in parts}
        order.update({("dve", "nm_" + p): ["nm"] for p in parts})
        done.update({("dve", "nm_" + p): sem(f"dve_nm_{p}_d") for p in parts})
        counts = Counts(done, order, {e: sem(f"{e}_turns_d") for e in engines + ("sp",)})
        block = ctx.enter_context(nc.Block())

        def rows(b, n):
            return bass.ds((n * BUF + b) * T, T)

        @block.sync
        def _(sp):
            me = EngineSteps(sp, "sp", counts)
            with sp.Fori(0, NB // BUF) as n:
                for b in range(BUF):
                    me.need("dve", f"b{b}", f"x{CH-1}", n - 1)
                    sp.dma_start(acc[:, b, :, :], io["acc"][rows(b, n), :].rearrange("(c p) d -> p c d", p=P))\
                        .then_inc(acc_in[b], 16)

        @block.gpsimd
        def _(pool):
            me = EngineSteps(pool, "pool", counts)
            g = nc.gpsimd
            me.credit(*parts)
            g.memset(neghalf[:, :], -0.5).then_inc(half_ready, 1)
            pool.wait_ge(half_ready, 1)
            with pool.Fori(0, NB // BUF) as n:
                for b in range(BUF):
                    me.need("dve", f"b{b}", "ve", n)
                    me.did(g.tensor_tensor(small["rstd"][:, b, :], small["ve"][:, b, :], neghalf[:, :], ALU.pow),
                           f"b{b}", "rstd")

        @block.vector
        def _(dve):
            me = EngineSteps(dve, "dve", counts)
            v = nc.vector
            me.credit(*parts, *(f"nm_{p}" for p in parts))
            def shift(b, n):
                me.need("pool", f"b{b}", "rstd", n)
                me.did(v.scalar_tensor_tensor(small["nm"][:, b, :], mv[:, b, :, 0], -1.0, small["rstd"][:, b, :],
                                              ALU.mult, ALU.mult), f"nm_b{b}", "nm")

            with dve.Fori(0, NB // BUF) as n:
                for b in range(BUF):
                    p = f"b{b}"
                    me.arrived(acc_in[b], 16 * (n + 1))
                    gs = acc[:, b, :, C]
                    me.did(v.scalar_tensor_tensor(small["den"][:, b, :], gs, 0.0, gs, ALU.is_le, ALU.add), p, "den")
                    me.need("dve", p, "den", n)
                    me.did(v.reciprocal(small["rec"][:, b, :], small["den"][:, b, :]), p, "rec")
                    me.need("dve", p, "rec", n)
                    me.need("act", p, f"o{CH-1}", n - 1)
                    for c in range(CH):
                        x2c = keep["x2all"][:, bass.ds((n * BUF + b) * CH + c, 1), :].rearrange("p o d -> p (o d)")
                        me.did(v.scalar_tensor_tensor(x3[:, b, c, :], acc[:, b, c, 0:C], small["rec"][:, b, c:c + 1],
                                                      x2c, ALU.mult, ALU.add), p, f"x{c}")
                    for c in range(CH):
                        me.need("dve", p, f"x{c}", n)
                        me.did(v.bn_stats(st[:, b, c, :], x3[:, b, c, :]), p, f"st{c}")
                    for c in range(CH):
                        me.need("dve", p, f"st{c}", n)
                        me.did(v.bn_aggr(mv[:, b, c, :], st[:, b, c, :]), p, f"mv{c}")
                    me.need("dve", p, f"mv{CH-1}", n)
                    me.did(v.tensor_scalar(small["ve"][:, b, :], mv[:, b, :, 1], LN_EPS, None, ALU.add), p, "ve")
                    if b:
                        shift(b - 1, n)
                shift(BUF - 1, n)

        @block.scalar
        def _(act):
            me = EngineSteps(act, "act", counts)
            a = nc.scalar
            me.credit(*parts)
            for b in range(BUF):
                act.sem_inc(done[("sp", f"b{b}")], 1)

            def stored(b, n):
                act.wait_ge(out_done[b], 16 * (n + 1)).then_inc(done[("sp", f"b{b}")], 1)

            with act.Fori(0, NB // BUF) as n:
                for b in range(BUF):
                    p = f"b{b}"
                    me.need("dve", "nm_" + p, "nm", n)
                    me.need("sp", p, "in", n - 1)
                    for c in range(CH):
                        me.did(a.activation(o[:, b, c, :], x3[:, b, c, :], ACT.Identity, bias=small["nm"][:, b, c:c + 1],
                                            scale=small["rstd"][:, b, c:c + 1]), p, f"o{c}")
                    me.need("act", p, f"o{CH-1}", n)
                    act.dma_start(io["out"][rows(b, n), :].rearrange("(c p) d -> p c d", p=P), o[:, b, :, :])\
                        .then_inc(out_done[b], 16)
                    if b >= 2:
                        stored(b - 2, n)
                stored(BUF - 2, n)
                stored(BUF - 1, n)


def build(nc, io):
    with ExitStack() as ctx:
        keep = {"x2all": ctx.enter_context(nc.sbuf_tensor("x2all", [P, TILES, C], F32)),
                "slot": ctx.enter_context(nc.sbuf_tensor("slot", [P, G], F32)),
                "tile": ctx.enter_context(nc.sbuf_tensor("tile", [P, (E + 2) * G], F32)),
                "cumrow": ctx.enter_context(nc.sbuf_tensor("cumrow", [P, (E + 2) * G], F32))}
        stage_a(nc, io, keep)
        keep["fw1"] = ctx.enter_context(nc.sbuf_tensor("fw1", [P, HP, FF], F32))
        keep["fw2"] = ctx.enter_context(nc.sbuf_tensor("fw2", [P, FT, C], F32))
        keep["b1"] = ctx.enter_context(nc.sbuf_tensor("b1", [P, E, FT], F32))
        keep["allends"] = ctx.enter_context(nc.sbuf_tensor("allends", [P, E * TILES], F32))
        keep["eoff"] = ctx.enter_context(nc.sbuf_tensor("eoff", [P, E * G], F32))
        keep["tile_cmp"] = ctx.enter_context(nc.sbuf_tensor("tile_cmp", [P, E, G, TILES], F32))
        for name in ("w1_in", "w2_in", "b1_in"):
            keep[name] = ctx.enter_context(nc.semaphore(name))
        stage_b(nc, io, keep)
        stage_c(nc, io, keep)
        stage_d(nc, io, keep)


def kernel(**inputs):
    import numpy as np
    import concourse.bacc as bacc
    from concourse.bass_utils import run_bass_kernel_spmd as run

    g = {k: np.asarray(v) for k, v in inputs.items()}
    A = "L0_attn_"
    x = g[A + "x"].reshape(NT, C)
    cols = np.stack([g[A + k].reshape(HP, P) for k in
                     ("maa_x", "maa_w", "maa_k", "maa_v", "maa_r", "maa_g", "time_decay", "u")])
    F = "L0_ffn_"
    arrays = {
        "x": x, "xT": x.T,
        "cols": cols.reshape(16, P).T,
        "rows": np.concatenate([g[A + "ln_g"], g[A + "ln_b"], g[F + "norm_weight"], g[F + "router_bias"]])[None],
        "maa_w1": g[A + "maa_w1"], "maa_w2": g[A + "maa_w2"].reshape(160, C),
        "Wr": g[A + "Wr"], "Wk": g[A + "Wk"], "Wv": g[A + "Wv"], "Wo": g[A + "Wo"],
        "decay_w1": g[A + "decay_w1"], "decay_w2": g[A + "decay_w2"],
        "gate_w1": g[A + "gate_w1"], "gate_w2": g[A + "gate_w2"],
        "rwT": g[F + "router_weight"].T,
        "fc1T": g[F + "fc1_weight"].transpose(0, 2, 1), "fc2T": g[F + "fc2_weight"].transpose(0, 2, 1),
        "b1": g[F + "fc1_bias"].reshape(E, FT, P).transpose(2, 0, 1), "b2": g[F + "fc2_bias"],
    }
    arrays = {f"in_{k}": np.ascontiguousarray(v) for k, v in arrays.items()}
    nc = bacc.Bacc("TRN2", target_bir_lowering=False, num_devices=1)
    io = {k[3:]: nc.dram_tensor(k, v.shape, mybir.dt.from_np(v.dtype), kind="ExternalInput").ap()
          for k, v in arrays.items()}
    io["out"] = nc.dram_tensor("out_dram", (NT, C), F32, kind="ExternalOutput").ap()
    for name, shape in (("table", (NT, ROW)), ("logitsT", (E, NT)), ("ends", (1, E * TILES)),
                        ("cum", (E * TILES, P)), ("acc", (NT, ARow))):
        io[name] = nc.dram_tensor(f"tmp_{name}", shape, F32, kind="Internal").ap()
    build(nc, io)
    r = run(nc, [arrays], core_ids=[0])
    return r.results[0]["out_dram"].reshape(NB, T, C)
```
